# Optimizing a Trainium2 kernel written in Bass

```python
import numpy as np
import jax
import jax.numpy as jnp

def _softmax(x, axis=-1):
    return jax.nn.softmax(x, axis=axis)

def _gelu(x):
    return jax.nn.gelu(x, approximate=True)

def _silu(x):
    return jax.nn.silu(x)

def _sigmoid(x):
    return jax.nn.sigmoid(x)

def _layernorm(x, axis=-1, eps=1e-05):
    m = jnp.mean(x, axis=axis, keepdims=True)
    v = jnp.var(x, axis=axis, keepdims=True)
    return (x - m) / jnp.sqrt(v + eps)

def _scatter_add(tgt, idx, src, axis=0):
    return tgt.at[idx].add(src)

def _segment_sum(src, seg, n):
    return jax.ops.segment_sum(src, seg, n)
kernel_name = 'mk_adj_resnorm_d4_adj_r2_772e1b'

def setup_inputs(seed: int=0):
    np.random.seed(seed)
    _w = jnp.asarray

    def _rec_inputs():
        import jax
        import jax.numpy as jnp
        _gk = jax.random.key(seed)
        x = -0.0002928 + 1 * jax.random.normal(jax.random.fold_in(_gk, 1), (2048, 256), jnp.float32)
        _a = jax.random.bernoulli(jax.random.fold_in(_gk, 2), 0.0078125, (2048, 2048))
        adj = _a.astype(jnp.int32)
        return (x, adj)
    x, adj = _rec_inputs()

    def _L0_gnn_setup():
        import jax, jax.numpy as jnp
        import numpy as np
        N, D_IN, D_OUT = (4096, 256, 256)
        key = jax.random.key(seed)
        ks = jax.random.split(key, 8)
        scale_in = 1.0 / np.sqrt(D_IN)
        scale_cat = 1.0 / np.sqrt(2 * D_OUT)
        return {'x': jax.random.normal(ks[0], (N, D_IN), dtype=jnp.float32), 'adj': jax.random.randint(ks[1], (N, N), 0, 2, dtype=jnp.int32), 'W_self': jax.random.uniform(ks[2], (D_IN, D_OUT), jnp.float32, -scale_in, scale_in), 'b_self': jax.random.uniform(ks[3], (D_OUT,), jnp.float32, -scale_in, scale_in), 'W_nb': jax.random.uniform(ks[4], (D_IN, D_OUT), jnp.float32, -scale_in, scale_in), 'b_nb': jax.random.uniform(ks[5], (D_OUT,), jnp.float32, -scale_in, scale_in), 'W_comb': jax.random.uniform(ks[6], (2 * D_OUT, D_OUT), jnp.float32, -scale_cat, scale_cat), 'b_comb': jax.random.uniform(ks[7], (D_OUT,), jnp.float32, -scale_cat, scale_cat)}
    _L0_gnn_all = _L0_gnn_setup()
    _L0_gnn_in = {k: v for k, v in _L0_gnn_all.items() if k in ('W_self', 'b_self', 'W_nb', 'b_nb', 'W_comb', 'b_comb')}
    del _L0_gnn_all

    def _L1_gnn_setup():
        import jax, jax.numpy as jnp
        import numpy as np
        N = 2048
        STATE_DIM = 256
        OUTPUT_DIM = 256
        N_STEPS = 5
        W_STD = 0.02

        def _lin_params(key, out_dim, in_dim):
            W = jax.random.normal(key, (out_dim, in_dim), dtype=jnp.float32) * W_STD
            b = jnp.zeros((out_dim,), dtype=jnp.float32)
            return (W, b)
        key = jax.random.key(seed)
        ks = jax.random.split(key, 10)
        prop_state = jax.random.normal(ks[0], (N, STATE_DIM), dtype=jnp.float32)
        A = jax.random.randint(ks[1], (N, N), 0, 2, dtype=jnp.int64)
        in_W, in_b = _lin_params(ks[2], STATE_DIM, STATE_DIM)
        out_W, out_b = _lin_params(ks[3], STATE_DIM, STATE_DIM)
        r_W, r_b = _lin_params(ks[4], STATE_DIM, 3 * STATE_DIM)
        z_W, z_b = _lin_params(ks[5], STATE_DIM, 3 * STATE_DIM)
        h_W, h_b = _lin_params(ks[6], STATE_DIM, 3 * STATE_DIM)
        o1_W, o1_b = _lin_params(ks[7], STATE_DIM, STATE_DIM)
        o2_W, o2_b = _lin_params(ks[8], OUTPUT_DIM, STATE_DIM)
        return {'prop_state': prop_state, 'A': A, 'in_W': in_W, 'in_b': in_b, 'out_W': out_W, 'out_b': out_b, 'r_W': r_W, 'r_b': r_b, 'z_W': z_W, 'z_b': z_b, 'h_W': h_W, 'h_b': h_b, 'o1_W': o1_W, 'o1_b': o1_b, 'o2_W': o2_W, 'o2_b': o2_b}
    _L1_gnn_all = _L1_gnn_setup()
    _L1_gnn_in = {k: v for k, v in _L1_gnn_all.items() if k in ('in_W', 'in_b', 'out_W', 'out_b', 'r_W', 'r_b', 'z_W', 'z_b', 'h_W', 'h_b', 'o1_W', 'o1_b', 'o2_W', 'o2_b')}
    del _L1_gnn_all

    def _L2_gnn_setup():
        import jax, jax.numpy as jnp
        import numpy as np
        HEAD_SIZE = 8
        QK_DIM = 256
        V_DIM = 256
        N = 2048
        ATT_DIM = QK_DIM // HEAD_SIZE
        SCALE = ATT_DIM ** (-0.5)
        NEG_FILL = jnp.float32(-9000000000000000.0)
        key = jax.random.key(seed)
        k1, k2, k3, k4 = jax.random.split(key, 4)
        x1 = jax.random.normal(k1, (N, QK_DIM), dtype=jnp.float32)
        x2 = jax.random.normal(k2, (N, QK_DIM), dtype=jnp.float32)
        v = jax.random.normal(k3, (N, V_DIM), dtype=jnp.float32)
        adj = jax.random.randint(k4, (N, N), 0, 2, dtype=jnp.int32)
        return {'x1': x1, 'x2': x2, 'v': v, 'adj': adj}
    _L2_gnn_all = _L2_gnn_setup()
    _L2_gnn_in = {k: v for k, v in _L2_gnn_all.items() if k in ('x2', 'v')}
    del _L2_gnn_all

    def _L3_gnn_setup():
        import jax, jax.numpy as jnp
        import numpy as np
        N = 4096
        EMB2 = 256
        HID = 128
        NEG_SLOPE = 0.01
        key = jax.random.key(seed)
        ks = jax.random.split(key, 7)
        inlayer = jax.random.normal(ks[0], (N, EMB2), dtype=jnp.float32)
        adj_mat = jax.random.randint(ks[1], (N, N), 0, 2, dtype=jnp.int32)
        W1 = jax.random.normal(ks[2], (HID, EMB2), dtype=jnp.float32) * (1.0 / np.sqrt(EMB2))
        w2 = jax.random.normal(ks[3], (HID,), dtype=jnp.float32) * (1.0 / np.sqrt(HID))
        b2 = jax.random.normal(ks[4], (1,), dtype=jnp.float32) * 0.01
        w3 = jax.random.normal(ks[5], (HID,), dtype=jnp.float32) * (1.0 / np.sqrt(HID))
        b3 = jax.random.normal(ks[6], (1,), dtype=jnp.float32) * 0.01
        return {'inlayer': inlayer, 'adj_mat': adj_mat, 'W1': W1, 'w2': w2, 'b2': b2, 'w3': w3, 'b3': b3}
    _L3_gnn_all = _L3_gnn_setup()
    _L3_gnn_in = {k: v for k, v in _L3_gnn_all.items() if k in ('W1', 'w2', 'b2', 'w3', 'b3')}
    del _L3_gnn_all
    return {'x': x, 'adj': adj, 'L0_gnn_W_self': _L0_gnn_in['W_self'], 'L0_gnn_b_self': _L0_gnn_in['b_self'], 'L0_gnn_W_nb': _L0_gnn_in['W_nb'], 'L0_gnn_b_nb': _L0_gnn_in['b_nb'], 'L0_gnn_W_comb': _L0_gnn_in['W_comb'], 'L0_gnn_b_comb': _L0_gnn_in['b_comb'], 'L1_gnn_in_W': _L1_gnn_in['in_W'], 'L1_gnn_in_b': _L1_gnn_in['in_b'], 'L1_gnn_out_W': _L1_gnn_in['out_W'], 'L1_gnn_out_b': _L1_gnn_in['out_b'], 'L1_gnn_r_W': _L1_gnn_in['r_W'], 'L1_gnn_r_b': _L1_gnn_in['r_b'], 'L1_gnn_z_W': _L1_gnn_in['z_W'], 'L1_gnn_z_b': _L1_gnn_in['z_b'], 'L1_gnn_h_W': _L1_gnn_in['h_W'], 'L1_gnn_h_b': _L1_gnn_in['h_b'], 'L1_gnn_o1_W': _L1_gnn_in['o1_W'], 'L1_gnn_o1_b': _L1_gnn_in['o1_b'], 'L1_gnn_o2_W': _L1_gnn_in['o2_W'], 'L1_gnn_o2_b': _L1_gnn_in['o2_b'], 'L2_gnn_x2': _L2_gnn_in['x2'], 'L2_gnn_v': _L2_gnn_in['v'], 'L3_gnn_W1': _L3_gnn_in['W1'], 'L3_gnn_w2': _L3_gnn_in['w2'], 'L3_gnn_b2': _L3_gnn_in['b2'], 'L3_gnn_w3': _L3_gnn_in['w3'], 'L3_gnn_b3': _L3_gnn_in['b3']}

def reference(x, adj, L0_gnn_W_self, L0_gnn_b_self, L0_gnn_W_nb, L0_gnn_b_nb, L0_gnn_W_comb, L0_gnn_b_comb, L1_gnn_in_W, L1_gnn_in_b, L1_gnn_out_W, L1_gnn_out_b, L1_gnn_r_W, L1_gnn_r_b, L1_gnn_z_W, L1_gnn_z_b, L1_gnn_h_W, L1_gnn_h_b, L1_gnn_o1_W, L1_gnn_o1_b, L1_gnn_o2_W, L1_gnn_o2_b, L2_gnn_x2, L2_gnn_v, L3_gnn_W1, L3_gnn_w2, L3_gnn_b2, L3_gnn_w3, L3_gnn_b3):
    import jax
    import jax.numpy as jnp

    def _L0_gnn_ref(x, adj, W_self, b_self, W_nb, b_nb, W_comb, b_comb):
        import jax, jax.numpy as jnp
        import numpy as np
        N, D_IN, D_OUT = (4096, 256, 256)
        mask = (adj > 0).astype(x.dtype)
        deg = jnp.sum(mask, axis=1, keepdims=True)
        agg = mask @ x / jnp.maximum(deg, 1.0)
        self_f = x @ W_self + b_self
        nb_f = agg @ W_nb + b_nb
        combined = jnp.concatenate([self_f, nb_f], axis=-1)
        out = combined @ W_comb + b_comb
        return jax.nn.relu(out)

    def _L1_gnn_ref(prop_state, A, in_W, in_b, out_W, out_b, r_W, r_b, z_W, z_b, h_W, h_b, o1_W, o1_b, o2_W, o2_b):
        import jax, jax.numpy as jnp
        import numpy as np
        N = 2048
        STATE_DIM = 256
        OUTPUT_DIM = 256
        N_STEPS = 5
        W_STD = 0.02

        def _lin_params(key, out_dim, in_dim):
            W = jax.random.normal(key, (out_dim, in_dim), dtype=jnp.float32) * W_STD
            b = jnp.zeros((out_dim,), dtype=jnp.float32)
            return (W, b)
        Af = A.astype(prop_state.dtype)
        AfT = Af.T
        state = prop_state
        for _ in range(N_STEPS):
            s_in = state @ in_W.T + in_b
            s_out = state @ out_W.T + out_b
            a_in = Af @ s_in
            a_out = AfT @ s_out
            a = jnp.concatenate([a_in, a_out, state], axis=-1)
            r = jax.nn.sigmoid(a @ r_W.T + r_b)
            z = jax.nn.sigmoid(a @ z_W.T + z_b)
            joined = jnp.concatenate([a_in, a_out, r * state], axis=-1)
            h_hat = jnp.tanh(joined @ h_W.T + h_b)
            state = (1.0 - z) * state + z * h_hat
        out = jnp.tanh(state @ o1_W.T + o1_b) @ o2_W.T + o2_b
        return out

    def _L2_gnn_ref(x1, x2, v, adj):
        import jax, jax.numpy as jnp
        import numpy as np
        HEAD_SIZE = 8
        QK_DIM = 256
        V_DIM = 256
        N = 2048
        ATT_DIM = QK_DIM // HEAD_SIZE
        SCALE = ATT_DIM ** (-0.5)
        NEG_FILL = jnp.float32(-9000000000000000.0)
        n = x1.shape[0]
        q = x1.reshape(n, HEAD_SIZE, -1).transpose(1, 0, 2) * SCALE
        k = x2.reshape(n, HEAD_SIZE, -1).transpose(1, 0, 2)
        vv = v.reshape(n, HEAD_SIZE, -1).transpose(1, 0, 2)
        scores = jnp.einsum('hnd,hmd->hnm', q, k)
        scores = jnp.where(adj > 0, scores, NEG_FILL)
        attn = jax.nn.softmax(scores, axis=-1)
        out = jnp.einsum('hnm,hmd->hnd', attn, vv)
        return out.transpose(1, 0, 2).reshape(n, -1)

    def _L3_gnn_ref(inlayer, adj_mat, W1, w2, b2, w3, b3):
        import jax, jax.numpy as jnp
        import numpy as np
        N = 4096
        EMB2 = 256
        HID = 128
        NEG_SLOPE = 0.01
        in_fts = jnp.einsum('ne,he->nh', inlayer, W1)
        f_1 = in_fts @ w2 + b2[0]
        f_2 = in_fts @ w3 + b3[0]
        logits = f_1[:, None] + f_2[None, :]
        adj_f = adj_mat.astype(jnp.float32)
        logits = adj_f * logits
        bias_mat = -1000000000.0 * (1.0 - (adj_mat > 0).astype(jnp.float32))
        coefs = jax.nn.softmax(jax.nn.leaky_relu(logits, NEG_SLOPE) + bias_mat, axis=1)
        vals = coefs @ inlayer
        return jax.nn.relu(vals)
    x = _layernorm(x + _L0_gnn_ref(x, adj, L0_gnn_W_self, L0_gnn_b_self, L0_gnn_W_nb, L0_gnn_b_nb, L0_gnn_W_comb, L0_gnn_b_comb), axis=-1)
    x = _layernorm(x + _L1_gnn_ref(x, adj, L1_gnn_in_W, L1_gnn_in_b, L1_gnn_out_W, L1_gnn_out_b, L1_gnn_r_W, L1_gnn_r_b, L1_gnn_z_W, L1_gnn_z_b, L1_gnn_h_W, L1_gnn_h_b, L1_gnn_o1_W, L1_gnn_o1_b, L1_gnn_o2_W, L1_gnn_o2_b), axis=-1)
    x = _layernorm(x + _L2_gnn_ref(x, L2_gnn_x2, L2_gnn_v, adj), axis=-1)
    x = _layernorm(x + _L3_gnn_ref(x, adj, L3_gnn_W1, L3_gnn_w2, L3_gnn_b2, L3_gnn_w3, L3_gnn_b3), axis=-1)
    return x

_drawn_inputs = setup_inputs


def setup_inputs(seed=0):
    import zlib

    import numpy as np

    out = dict(_drawn_inputs(seed))
    spreads = {'L1_gnn_in_b': (0.0, 0.1),
     'L1_gnn_out_b': (0.0, 0.1),
     'L1_gnn_r_b': (0.0, 2.0),
     'L1_gnn_z_b': (0.0, 2.0),
     'L1_gnn_h_b': (0.0, 0.448),
     'L1_gnn_o1_b': (0.0, 0.1),
     'L1_gnn_o2_b': (0.0, 0.1)}
    factors = {'L0_gnn_b_self': 4.826, 'L0_gnn_b_nb': 4.102, 'L1_gnn_r_W': 62.909}
    for name, (base, spread) in spreads.items():
        noise = np.random.default_rng([zlib.crc32(name.encode()), seed]).standard_normal(out[name].shape)
        drawn = base * np.exp(spread * noise) if base else spread * noise
        out[name] = jnp.asarray(drawn.astype(out[name].dtype))
    for name, factor in factors.items():
        out[name] = (out[name] * factor).astype(out[name].dtype)
    return out
```

```python
from contextlib import ExitStack

import concourse.bass as bass
from concourse import mybir

P = 128
F32 = mybir.dt.float32
F32R = mybir.dt.float32r
BF16 = mybir.dt.bfloat16
F16 = mybir.dt.float16
I32 = mybir.dt.int32
ALU = mybir.AluOpType
ACT = mybir.ActivationFunctionType
AX = mybir.AxisListType

N = 2048
D = 256
T = N // P
FT = D // P
CH = 512
C = N // CH
TC = CH // P
STEPS = 5
HEADS = 8
HD = D // HEADS
EPS = 1e-5
NEG_INIT = -3.4e38
FINISH = 2
RING = 3


def program(nc, a, out):
    ctx = ExitStack()
    with ctx:
        def sem(name):
            return ctx.enter_context(nc.semaphore(name))

        def sb(name, shape, dt, scope=ctx):
            return scope.enter_context(nc.sbuf_tensor(name, shape, dt))

        x1_dram = nc.dram_tensor("x1_rows_scratch", [N, D], F32, kind="Internal").ap()
        ps = ctx.enter_context(nc.psum_tensor("ps", [P, 8, 512], F32))

        identf = sb("identf", [P, P], F32)
        identh = sb("identh", [P, P], F16)
        onesf = sb("onesf", [P, P], F32)
        onesh = sb("onesh", [P, P], F16)
        eps_col = sb("eps_col", [P, 1], F32)
        stats = sb("stats", [P, TC, 6], F32)
        TURN = [6, 7, 1, 2, 3, 6, 7, 4]
        mv = sb("mv", [P, T, 2], F32)
        rstd = sb("rstd", [P, T], F32)

        graph = ExitStack()
        A16 = sb("A16", [P, T, N], F16, graph)
        At16 = sb("At16", [P, T, N], F16, graph)
        xT = sb("xT", [P, FT, N], F32, graph)

        l0 = ExitStack()
        stage = sb("stage", [P, 2, N], I32, l0)
        xb = sb("xb", [P, T, 3, D], BF16, l0)
        mk = sb("mk", [P, RING, CH], F16, l0)
        aggT = sb("aggT", [P, FT, CH], F32, l0)
        rdeg = sb("rdeg", [P, CH], F32, l0)
        xres = sb("xres", [P, TC, D], F32, l0)
        y0 = sb("y0", [P, TC, D], F32, l0)
        W0 = sb("W0", [P, 2 * FT, D], F32, l0)
        bias0 = sb("bias0", [P, D], F32, l0)
        bcol0 = sb("bcol0", [P, 2 * FT], F32, l0)
        x32 = A16[:, 12:16, :].bitcast(F32).rearrange("p a (b n) -> p (a b) n", n=D)
        rest = A16[:, 4:8, :].bitcast(F32).rearrange("p a (b n) -> p (a b) n", n=D)
        w_raw = A16[:, 8:10, :].bitcast(F32).rearrange("p a (b n) -> p (a b) n", n=D)
        w_tr = A16[:, 10, :].bitcast(F32).rearrange("p (b n) -> p b n", n=D)
        bstat = A16[:, 11, 0:1024].bitcast(F32).rearrange("p (b n) -> p b n", n=P)
        bcomb = A16[0:1, 11, 1024:1024 + 2 * D].bitcast(F32)
        l0.close()

        l1 = ExitStack()
        gates = 3 * D
        drows = sb("drows", [8, N], F32R, l1)
        dw = sb("dw", [8, gates], F32R, l1)
        Wg = sb("Wg", [P, 3 * FT, gates], F32, l1)
        gb = sb("gb", [P, 3 * FT], F32, l1)
        gz = sb("gz", [P, 2 * FT, CH], F32, l1)
        bcol1 = sb("bcol1", [P, 2 * FT], F32, l1)
        sel = sb("sel", [P, 2, 8], F16, l1)
        bst1 = sb("bst1", [P, 2 * FT, 8], F32, l1)
        dmask = sb("dmask", [8, 4], F32, l1)
        prep = ExitStack()
        RT = sb("RT", [P, 2 * FT, gates], F32, prep)
        graw = sb("graw", [P, FT, gates], F32, prep)
        ioW = sb("ioW", [P, 2 * FT, D], F32, prep)
        prep.close()
        run = ExitStack()
        rows16 = sb("rows16", [P, T, 2, D], F16, run)
        U = sb("U", [P, 2 * FT, CH], F32, run)
        run.close()
        dsum = gz[0:8, :, :].rearrange("p a b -> p (a b)")
        fin = ExitStack()
        oraw = sb("oraw", [P, 2 * FT, D], F32, fin)
        oT = sb("oT", [P, 2 * FT, D], F32, fin)
        o2b = sb("o2b", [1, D], F32, fin)
        bias1 = sb("bias1", [P, D], F32, fin)
        o1col = sb("o1col", [P, FT], F32, fin)
        TT = sb("TT", [P, FT, CH], F32, fin)
        x1r = sb("x1r", [P, 2, TC, D], F32, fin)
        fin.close()
        l1.close()
        graph.close()

        l2 = ExitStack()
        kst = sb("kst", [P, HEADS, N], F32R, l2)
        xr = sb("xr", [P, T, D], F32, l2)
        v_sb = sb("v_sb", [P, T, D], F32, l2)
        adj2 = sb("adj2", [P, N], I32, l2)
        bias2 = sb("bias2", [P, 2, N], BF16, l2)
        kprep = ExitStack()
        kin = sb("kin", [P, 2, D], F32, kprep)
        kstk = sb("kstk", [P, 2, HEADS, 4, HD], F32R, kprep)
        kprep.close()
        PT = sb("PT", [P, 2, 4, CH], F32, l2)
        prob = sb("prob", [P, HEADS, N], F32, l2)
        qst = sb("qst", [P, 2, HEADS, P], F32R, l2)
        qstk = sb("qstk", [P, HEADS, 4, HD], F32R, l2)
        oT2 = sb("oT2", [P, P], F32, l2)
        mv1 = sb("mv1", [P, 2], F32, l2)
        row2 = sb("row2", [P, D], F32, l2)
        mx2 = sb("mx2", [P, 16, 2], F32, l2)
        neg2 = sb("neg2", [P, 16], F32, l2)
        rsum2 = sb("rsum2", [P, 16], F32, l2)
        rinv2 = sb("rinv2", [P, 4], F32, l2)
        l2.close()

        l3 = ExitStack()
        adj3 = sb("adj3", [P, 2, N], I32, l3)
        bias3 = sb("bias3", [P, 2, N], F32, l3)
        coef = sb("coef", [P, 2, N], F32, l3)
        coefT = sb("coefT", [P, 2, N], F32, l3)
        same_place = sb("xr_again", [P, T, D], F32, l3)
        y3 = sb("y3", [P, T, D], F32, l3)
        x3T = sb("x3T", [P, FT, N], F32, l3)
        f2 = sb("f2", [P, N], F32, l3)
        f1 = sb("f1", [P, T], F32, l3)
        W1 = sb("W1", [P, D], F32, l3)
        w23 = sb("w23", [P, 2], F32, l3)
        b23 = sb("b23", [1, 2], F32, l3)
        bc23 = sb("bc23", [P, 2], F32, l3)
        u23 = sb("u23", [P, FT, 2], F32, l3)
        u3b = sb("u3b", [P, FT, P], F32, l3)
        mv3 = sb("mv3", [P, 2], F32, l3)
        row3 = sb("row3", [P, 2, D], F32, l3)
        mx3 = sb("mx3", [P, 2], F32, l3)
        neg3 = sb("neg3", [P, 2], F32, l3)
        rsum3 = sb("rsum3", [P, 2], F32, l3)
        rinv3 = sb("rinv3", [P, 2], F32, l3)
        l3.close()

        s_const = sem("s_const")
        s_x = sem("s_x")
        s_w0 = sem("s_w0")
        s_adj = [sem(f"s_adj{b}") for b in range(2)]
        s_xres = sem("s_xres")
        s_xb = sem("s_xb")
        s_bstat = sem("s_bstat")
        s_cast = sem("s_cast")
        s_tadj = sem("s_tadj")
        s_tadj_out = sem("s_tadj_out")
        s_w0t = sem("s_w0t")
        s_w0t_out = sem("s_w0t_out")
        s_w0c = sem("s_w0c")
        s_w0c_out = sem("s_w0c_out")
        s_xt = sem("s_xt")
        s_xt_out = sem("s_xt_out")
        s_mask = sem("s_mask")
        s_agg_m = sem("s_agg_m")
        s_agg_out = sem("s_agg_out")
        s_lin = sem("s_lin")
        s_lin_out = sem("s_lin_out")
        s_var0 = sem("s_var0")
        s_std0 = sem("s_std0")
        s_x1 = sem("s_x1")
        s_x1_saved = sem("s_x1_saved")
        s_x1t = sem("s_x1t")
        s_x1t_out = sem("s_x1t_out")
        s_w1 = sem("s_w1")
        s_graw = sem("s_graw")
        s_deg = sem("s_deg")
        s_deg_out = sem("s_deg_out")
        s_drows = sem("s_drows")
        s_sel = sem("s_sel")
        s_gt = sem("s_gt")
        s_gt_out = sem("s_gt_out")
        s_wg = sem("s_wg")
        s_wg_out = sem("s_wg_out")
        s_dwp = sem("s_dwp")
        s_dwp_out = sem("s_dwp_out")
        s_state = sem("s_state")
        s_turn = sem("s_turn")
        s_hi = sem("s_hi")
        s_rows = sem("s_rows")
        s_prod = sem("s_prod")
        s_U = sem("s_U")
        s_gate = sem("s_gate")
        s_r = sem("s_r")
        s_z = sem("s_z")
        s_rs = sem("s_rs")
        s_h = sem("s_h")
        s_upd = sem("s_upd")
        s_ow = sem("s_ow")
        s_ot = sem("s_ot")
        s_ot_out = sem("s_ot_out")
        s_x1r = [sem(f"s_x1r{b}") for b in range(2)]
        s_o1 = sem("s_o1")
        s_o1_out = sem("s_o1_out")
        s_o2 = sem("s_o2")
        s_y1 = sem("s_y1")
        s_var1 = sem("s_var1")
        s_std1 = sem("s_std1")
        s_x2 = sem("s_x2")
        s_kin = [sem(f"s_kin{b}") for b in range(2)]
        s_v = sem("s_v")
        s_passed = {"dve": sem("s_passed_dve"), "pool": sem("s_passed_pool")}
        s_fin2 = sem("s_fin2")
        s_stat2 = sem("s_stat2")
        s_f3 = sem("s_f3")
        s_khi = sem("s_khi")
        s_klo = sem("s_klo")
        s_kt = sem("s_kt")
        s_kout = [sem(f"s_kout{b}") for b in range(2)]
        s_adj2 = sem("s_adj2")
        s_bias2 = sem("s_bias2")
        s_qhi = sem("s_qhi")
        s_qlo = sem("s_qlo")
        s_qT = sem("s_qT")
        s_qout = [sem(f"s_qout{b}") for b in range(2)]
        s_score = sem("s_score")
        s_masked = sem("s_masked")
        s_neg = sem("s_neg")
        s_exp = sem("s_exp")
        s_T = sem("s_T")
        s_PT = {"act": sem("s_PT_act"), "dve": sem("s_PT_dve")}
        s_pv = sem("s_pv")
        s_o = sem("s_o")
        s_oT = sem("s_oT")
        s_att = sem("s_att")
        s_var2 = sem("s_var2")
        s_std2 = sem("s_std2")
        s_x3 = sem("s_x3")
        s_w3 = sem("s_w3")
        s_u = sem("s_u")
        s_u_out = sem("s_u_out")
        s_x3t = sem("s_x3t")
        s_x3t_out = sem("s_x3t_out")
        s_f = sem("s_f")
        s_f_out = sem("s_f_out")
        s_adj3 = [sem(f"s_adj3{b}") for b in range(2)]
        s_bias3 = sem("s_bias3")
        s_logit = sem("s_logit")
        s_l3 = sem("s_l3")
        s_neg3 = sem("s_neg3")
        s_exp3 = sem("s_exp3")
        s_T3 = sem("s_T3")
        s_T3_out = sem("s_T3_out")
        s_val = sem("s_val")
        s_val_out = sem("s_val_out")
        s_var3 = sem("s_var3")
        s_std3 = sem("s_std3")
        s_y3 = sem("s_y3")
        s_out = sem("s_out")
        s_dve = sem("s_dve")
        s_act = sem("s_act")

        x_rows = a["x"].rearrange("(t p) d -> p t d", p=P)
        adj_rows = a["adj"].rearrange("(t p) n -> t p n", p=P)
        x1_rows = x1_dram.rearrange("(t p) d -> p t d", p=P)
        W0_BITS = 6
        GROUPS = 2 * T

        TAKER = ["dve" if b % 4 == 3 or (b % 4 == 2 and (b // 4) % 2) else "act" for b in range(T)]
        TAKEN = {who: TAKER.count(who) for who in ("act", "dve")}

        def wait_block_taken(eng, g, b):
            who = TAKER[b]
            eng.wait_ge(s_PT[who], TAKEN[who] * g + TAKER[:b + 1].count(who))

        def take_block(eng, copy, g, b, has_before):
            eng.wait_ge(s_T, T * g + b + 1)
            q = b // 4
            if has_before or q >= 2:
                eng.wait_ge(s_pv, 4 * g + q - 1)
            copy(PT[:, q % 2, b % 4, :], ps[:, 4 + b % 2, :]).then_inc(s_PT[TAKER[b]], 1)

        def layer2(eng, slot):
            for gamma in range(4):
                for j in range(4):
                    slot(gamma // 2, gamma, gamma, j, gamma >= 1, gamma >= 2, True, True)
            with eng.Fori(1, T // 2 - 1) as i:
                for gamma in range(4):
                    for j in range(4):
                        slot(2 * i + gamma // 2, 4 * i + gamma, gamma, j, True, True, True, True)
            for gamma in range(4):
                for j in range(4):
                    slot(T - 2 + gamma // 2, GROUPS - 4 + gamma, gamma, j, True, True, True, gamma < 2)
            for j in range(4):
                slot(T, GROUPS, 0, j, True, True, False, False)
            for j in range(3):
                slot(T, GROUPS + 1, 1, j, False, True, False, False)

        block = ctx.enter_context(nc.Block())

        @block.gpsimd
        def _(pool):
            pool.memset(identf[:, :], 0.0).then_inc(s_const, 1)
            pool.memset(identh[:, :], 0.0).then_inc(s_const, 1)
            pool.memset(onesf[:, :], 1.0).then_inc(s_const, 1)
            pool.memset(onesh[:, :], 1.0).then_inc(s_const, 1)
            pool.memset(eps_col[:, :], EPS).then_inc(s_const, 1)
            pool.wait_ge(s_const, 5)
            for m in (identf, identh):
                pool.affine_select(out=m[:, :], in_=m[:, :], compare_op=ALU.not_equal, fill=1.0, base=0,
                                   pattern=[[-1, P]], channel_multiplier=1).then_inc(s_const, 1)
            for c in range(C):
                if c >= 1:
                    pool.wait_ge(s_lin_out, TC * c)
                pool.dma_start(xres[:, :, :], x_rows[:, c * TC:(c + 1) * TC, :]).then_inc(s_xres, 16)
                pool.wait_ge(s_x1, TC * (c + 1))
                pool.dma_start(x1_rows[:, c * TC:(c + 1) * TC, :], y0[:, :, :]).then_inc(s_x1_saved, 16)
            pool.wait_ge(s_x1_saved, 16 * C)
            pool.wait_ge(s_state, 4 + C * STEPS)
            for c in range(C):
                if c >= 2:
                    pool.wait_ge(s_y1, TC * (c - 1) + 1)
                pool.dma_start(x1r[:, c % 2, :, :], x1_rows[:, c * TC:(c + 1) * TC, :]).then_inc(s_x1r[c % 2], 16)

            pool.wait_ge(s_prod, 16 * STEPS)

            def bias_2(t, b, used):
                pool.wait_ge(s_adj2, 16 * t + 16)
                if used:
                    pool.wait_ge(s_neg, 8 * t - 8)
                pool.sem_inc(s_passed["pool"], 1)
                pool.tensor_scalar(bias2[:, b, :], adj2[:, :], 0.0, -9e15, ALU.is_le, ALU.mult).then_inc(s_bias2, 1)

            bias_2(0, 0, False)
            bias_2(1, 1, False)
            with pool.Fori(1, T // 2) as i:
                for b in range(2):
                    bias_2(2 * i + b, b, True)

            def bias_3(t, k, b, used):
                pool.wait_ge(s_adj3[b], 16 * k + 16)
                if used:
                    pool.wait_ge(s_neg3, t - 1)
                pool.sem_inc(s_passed["pool"], 1)
                pool.tensor_scalar(bias3[:, b, :], adj3[:, b, :], 0.0, -1e9, ALU.is_le, ALU.mult).then_inc(s_bias3, 1)

            bias_3(0, 0, 0, False)
            bias_3(1, 0, 1, False)
            with pool.Fori(1, T // 2) as i:
                for b in range(2):
                    bias_3(2 * i + b, i, b, True)

        @block.sync
        def _(sp):
            sp.dma_start(x32, x_rows).then_inc(s_x, 16)
            sp.dma_start(w_raw[:, 0:2, :], a["L0_gnn_W_self"].rearrange("(k p) d -> p k d", p=P)).then_inc(s_w0, 16)
            sp.dma_start(w_raw[:, 2:4, :], a["L0_gnn_W_nb"].rearrange("(k p) d -> p k d", p=P)).then_inc(s_w0, 16)
            sp.dma_start(w_raw[:, 4:8, :], a["L0_gnn_W_comb"].rearrange("(k p) d -> p k d", p=P)).then_inc(s_w0, 16)
            sp.dma_start(bcol0[:, 0:2], a["L0_gnn_b_self"].rearrange("(k p) -> p k", p=P), allow_slow_non_contiguous=True).then_inc(s_w0, 16)
            sp.dma_start(bcol0[:, 2:4], a["L0_gnn_b_nb"].rearrange("(k p) -> p k", p=P), allow_slow_non_contiguous=True).then_inc(s_w0, 16)
            sp.dma_start(bcomb, a["L0_gnn_b_comb"].rearrange("(a d) -> a d", a=1)).then_inc(s_w0, 16)
            for t in range(T):
                if t >= 2:
                    sp.wait_ge(s_cast, t - 1)
                sp.dma_start(stage[:, t % 2, :], adj_rows[t]).then_inc(s_adj[t % 2], 16)

            sp.wait_ge(s_x1_saved, 16 * C)
            sp.wait_ge(s_x1t_out, FT * C)
            for k, name in enumerate(("in", "out")):
                sp.dma_start(bcol1[:, 2 * k:2 * k + 2], a[f"L1_gnn_{name}_b"].rearrange("(k p) -> p k", p=P),
                             allow_slow_non_contiguous=True).then_inc(s_w1, 16)
                sp.dma_start(ioW[:, 2 * k:2 * k + 2, :],
                             a[f"L1_gnn_{name}_W"].rearrange("(k p) d -> p k d", p=P)).then_inc(s_w1, 16)
            for k, name in enumerate(("r", "z", "h")):
                sp.dma_start(gb[:, 2 * k:2 * k + 2], a[f"L1_gnn_{name}_b"].rearrange("(k p) -> p k", p=P),
                             allow_slow_non_contiguous=True).then_inc(s_w1, 16)
            for k, name in enumerate(("r", "z", "h")):
                if k:
                    sp.wait_ge(s_gt, 3 * k)
                sp.dma_start(graw[:, :, :], a[f"L1_gnn_{name}_W"].rearrange("(k p) d -> p k d", p=P)).then_inc(s_graw, 16)
            sp.wait_ge(s_state, 4 + C * STEPS)
            for k in range(2):
                sp.dma_start(oraw[:, 2 * k:2 * k + 2, :],
                             a[f"L1_gnn_o{k + 1}_W"].rearrange("(k p) d -> p k d", p=P)).then_inc(s_ow, 16)
            sp.dma_start(o1col[:, :], a["L1_gnn_o1_b"].rearrange("(k p) -> p k", p=P),
                         allow_slow_non_contiguous=True).then_inc(s_ow, 16)
            sp.dma_start(o2b[:, :], a["L1_gnn_o2_b"].rearrange("(a d) -> a d", a=1)).then_inc(s_ow, 16)

            def load_adj2(t, used):
                if used:
                    sp.wait_ge(s_bias2, t)
                sp.dma_start(adj2[:, :], adj_rows[t]).then_inc(s_adj2, 16)

            load_adj2(0, False)
            for t in range(T):
                if t >= 2:
                    sp.wait_ge(s_klo, 2 * (t - 1))
                sp.dma_start(kin[:, t % 2, :], a["L2_gnn_x2"][t * P:(t + 1) * P, :]).then_inc(s_kin[t % 2], 16)
            sp.dma_start(v_sb[:, :, :], a["L2_gnn_v"].rearrange("(t p) d -> p t d", p=P)).then_inc(s_v, 16)
            for t in range(1, T):
                load_adj2(t, True)

            sp.wait_ge(s_var2, 1)
            sp.wait_ge(s_bias2, T)
            for b in range(2):
                sp.dma_start(adj3[:, b, :], adj_rows[b]).then_inc(s_adj3[b], 16)
            sp.dma_start(W1[:, :], a["L3_gnn_W1"]).then_inc(s_w3, 16)
            for k in range(2):
                sp.dma_start(w23[:, k:k + 1], a[f"L3_gnn_w{k + 2}"].rearrange("(p a) -> p a", a=1)).then_inc(s_w3, 16)
                sp.dma_start(b23[:, k:k + 1], a[f"L3_gnn_b{k + 2}"].rearrange("(p a) -> p a", a=1)).then_inc(s_w3, 16)
            for t in range(2, T):
                sp.wait_ge(s_bias3, t - 1)
                sp.wait_ge(s_logit, t - 1)
                sp.dma_start(adj3[:, t % 2, :], adj_rows[t]).then_inc(s_adj3[t % 2], 16)
            for c in range(C):
                sp.wait_ge(s_y3, TC * (c + 1))
                sp.dma_start(out.rearrange("(t p) d -> p t d", p=P)[:, c * TC:(c + 1) * TC, :],
                             y3[:, c * TC:(c + 1) * TC, :]).then_inc(s_out, 16)
            sp.wait_ge(s_out, 16 * C)

        @block.scalar
        def _(act):
            def copy(dst, src):
                return act.activation(dst, src, ACT.Copy)

            act.wait_ge(s_w0t, 1)
            copy(w_tr[:, 0:2, :], ps[:, 4, :]).then_inc(s_w0t_out, 1)
            act.wait_ge(s_w0t, 2)
            copy(w_tr[:, 2:4, :], ps[:, 5, :]).then_inc(s_w0t_out, 1)
            for k in range(2):
                act.wait_ge(s_w0c, k + 1)
                copy(W0[:, 2 * k:2 * k + 2, :], ps[:, k, :]).then_inc(s_w0c_out, 1)
            act.wait_ge(s_w0c, 3)
            copy(bias0[:, :], ps[:, 2, 0:D]).then_inc(s_w0c_out, 1)
            for n in range(2 * C):
                f, c = n // C, n % C
                act.wait_ge(s_xt, n + 1)
                copy(xT[:, f, c * CH:(c + 1) * CH], ps[:, 4 + n % 2, :]).then_inc(s_xt_out, 1)

            def tadj_out(t):
                for h in range(2):
                    act.wait_ge(s_tadj, 2 * t + h + 1)
                    copy(At16[:, 8 * h:8 * h + 8, t * P:(t + 1) * P],
                         ps[:, 6 + h, :].bitcast(F16).rearrange("p (b n) -> p b n", n=P)).then_inc(s_tadj_out, 1)

            def x1t_out(c):
                for f in range(FT):
                    act.wait_ge(s_x1t, FT * c + f + 1)
                    copy(xT[:, f, c * CH:(c + 1) * CH], ps[:, 4 + f, :]).then_inc(s_x1t_out, 1)

            for t in range(TC):
                tadj_out(t)
            for c in range(C):
                if c + 1 < C:
                    for t in range(TC * (c + 1), TC * (c + 2)):
                        tadj_out(t)
                act.wait_ge(s_var0, c + 1)
                act.activation(rstd[:, c * TC:(c + 1) * TC], mv[:, c * TC:(c + 1) * TC, 1], ACT.Sqrt,
                               bias=eps_col[:, 0:1]).then_inc(s_std0, 1)
                x1t_out(c)

            for c in range(C):
                act.wait_ge(s_deg, c + 1)
                copy(dsum[:, c * CH:(c + 1) * CH], ps[0:8, c, :]).then_inc(s_deg_out, 1)
            for n in range(9):
                g, kk = n // 3, n % 3
                act.wait_ge(s_gt, n + 1)
                dst = (RT[:, 2 * kk:2 * kk + 2, g * D:(g + 1) * D] if kk < 2 else Wg[:, 4:6, g * D:(g + 1) * D])
                copy(dst, ps[:, 4 + n % 2, :].rearrange("p (k n) -> p k n", k=2)).then_inc(s_gt_out, 1)
            for n in range(4):
                act.wait_ge(s_wg, n + 1)
                copy(Wg[:, n, :], ps[:, 2 * (n % 2):2 * (n % 2) + 2, :].rearrange("p a b -> p (a b)")[:, 0:gates])\
                    .then_inc(s_wg_out, 1)

            with act.Fori(0, STEPS) as i:
                for p in range(T // 2):
                    act.wait_ge(s_turn, 8 * i + p + 1)
                    act.activation(rows16[:, 2 * p:2 * p + 2, 0, :],
                                   ps[:, TURN[p], :].rearrange("p (t n) -> p t n", t=2), ACT.Copy,
                                   scale=2048.0).then_inc(s_hi, 1)
                for c in range(C):
                    for g in range(2 * FT):
                        act.wait_ge(s_prod, 16 * i + 4 * c + g + 1)
                        act.activation(U[:, g, :], ps[:, g, :], ACT.Copy, scale=1.0 / 2048).then_inc(s_U, 1)
                    act.wait_ge(s_state, 4 * i + 4 + c)
                    for j in range(2 * FT):
                        act.wait_ge(s_gate, 24 * i + 6 * c + j + 1)
                        act.activation(gz[:, j, :], ps[:, 4 + j, :], ACT.Sigmoid, bias=gb[:, j:j + 1])\
                            .then_inc(s_r if j < 2 else s_z, 1)
                    act.wait_ge(s_gate, 24 * i + 6 * c + 6)
                    for f in range(FT):
                        act.activation(gz[:, f, :], ps[:, 4 + f, :], ACT.Tanh, bias=gb[:, 4 + f:5 + f]).then_inc(s_h, 1)

            for k in range(2):
                act.wait_ge(s_ot, k + 1)
                copy(oT[:, 2 * k:2 * k + 2, :], ps[:, k, :].rearrange("p (k n) -> p k n", k=2)).then_inc(s_ot_out, 1)
            act.wait_ge(s_ot, 3)
            copy(bias1[:, :], ps[:, 2, 0:D]).then_inc(s_ot_out, 1)
            for c in range(C):
                if c >= 1:
                    act.wait_ge(s_o2, TC * c)
                for g in range(FT):
                    act.wait_ge(s_o1, FT * c + g + 1)
                    act.activation(TT[:, g, :], ps[:, 4 + g, :], ACT.Tanh, bias=o1col[:, g:g + 1]).then_inc(s_o1_out, 1)
            act.wait_ge(s_var1, 1)
            act.activation(rstd[:, :], mv[:, :, 1], ACT.Sqrt, bias=eps_col[:, 0:1]).then_inc(s_std1, 1)

            for t in range(T):
                b = t % 2
                act.wait_ge(s_kin[b], 16 * (t // 2 + 1))
                if t >= 2:
                    act.wait_ge(s_kt, 2 * (t - 1))
                for r in (0, 2):
                    copy(kstk[:, b, :, r, :], kin[:, b, :].rearrange("p (h d) -> p h d", h=HEADS)).then_inc(s_khi, 1)
                act.wait_ge(s_kt, 2 * t + 1)
                copy(kst[:, 0:4, t * P:(t + 1) * P], ps[:, 4, :].rearrange("p (h n) -> p h n", h=4))\
                    .then_inc(s_kout[0], 1)

            SCALE = float(HD) ** -0.5

            def q_hi(t):
                for r in (0, 1):
                    act.activation(qstk[:, :, r, :], xr[:, t, :].rearrange("p (h d) -> p h d", h=HEADS), ACT.Copy,
                                   scale=SCALE).then_inc(s_qhi, 1)

            def q_out(t, b):
                act.wait_ge(s_qT, 2 * t + 1)
                copy(qst[:, b, 0:4, :], ps[:, 7, :].rearrange("p (h n) -> p h n", h=4)).then_inc(s_qout[0], 1)

            act.wait_ge(s_x2, T)
            q_hi(0)
            q_out(0, 0)

            def slot(t, g, gamma, j, has1, has2, front, more):
                hh, n = gamma % 2, 4 * g + j
                ring = 4 * gamma + j
                if has2 and j == 1:
                    act.wait_ge(s_pv, 4 * g - 4)
                    copy(oT2[:, :], ps[:, 6, 0:P]).then_inc(s_o, 1)
                if more and hh == 1 and j == 0:
                    q_hi(t + 1)
                if more and hh == 1 and j == 3:
                    q_out(t + 1, (gamma // 2 + 1) % 2)
                if has1:
                    for b in range(4 * j, 4 * j + 4):
                        if TAKER[b] == "act":
                            take_block(act, copy, g - 1, b, has2)
                if front:
                    act.wait_ge(s_neg, n + 1)
                    act.activation(prob[:, 4 * hh + j, :], prob[:, 4 * hh + j, :], ACT.Exp, bias=neg2[:, ring:ring + 1],
                                   accum_out=rsum2[:, ring:ring + 1]).then_inc(s_exp, 1)

            layer2(act, slot)
            act.wait_ge(s_var2, 1)
            act.activation(rstd[:, :], mv[:, :, 1], ACT.Sqrt, bias=eps_col[:, 0:1]).then_inc(s_std2, 1)

            act.wait_ge(s_u, 1)
            copy(u23[:, :, :], ps[:, 0, 0:4].rearrange("p (f k) -> p f k", f=FT)).then_inc(s_u_out, 1)
            copy(bc23[:, :], ps[:, 0, 4:6]).then_inc(s_u_out, 1)
            act.wait_ge(s_u_out, 2)
            for n in range(FT * C):
                f, c = n % FT, n // FT
                act.wait_ge(s_x3t, n + 1)
                copy(x3T[:, f, c * CH:(c + 1) * CH], ps[:, 4 + n % 2, :]).then_inc(s_x3t_out, 1)
            for c in range(C):
                act.wait_ge(s_f, c + 2)
                act.activation(f2[:, c * CH:(c + 1) * CH], ps[:, 2 + c % 2, :], ACT.Identity, bias=bc23[:, 1:2])\
                    .then_inc(s_f_out, 1)

            def tile3(t, b, first):
                act.wait_ge(s_neg3, t + 1)
                act.activation(coef[:, b, :], coef[:, b, :], ACT.Exp, bias=neg3[:, b:b + 1],
                               accum_out=rsum3[:, b:b + 1]).then_inc(s_exp3, 1)
                for c in range(C):
                    act.wait_ge(s_T3, C * t + c + 1)
                    copy(coefT[:, b, c * CH:(c + 1) * CH], ps[:, 2 + c, :]).then_inc(s_T3_out, 1)

            with act.Fori(0, T // 2) as i:
                for b in range(2):
                    tile3(2 * i + b, b, False)
            act.wait_ge(s_var3, 1)
            act.activation(rstd[:, :], mv[:, :, 1], ACT.Sqrt, bias=eps_col[:, 0:1]).then_inc(s_std3, 1)

        @block.tensor
        def _(pe):
            pe.wait_ge(s_const, 7)
            pe.wait_ge(s_w0, 16 * W0_BITS)
            for k in range(2):
                for i in range(2):
                    for j in range(2):
                        mm = pe.transpose(ps[:, 4 + k, j * D + i * P:j * D + (i + 1) * P],
                                          w_raw[:, 2 * k + i, j * P:(j + 1) * P], identf[:, :])
                mm.then_inc(s_w0t, 1)
            for k in range(2):
                pe.wait_ge(s_w0t_out, k + 1)
                for i in range(2):
                    for j in range(2):
                        mm = pe.matmul(ps[:, k, i * D:(i + 1) * D], w_tr[:, 2 * k + j, i * P:(i + 1) * P],
                                       w_raw[:, 4 + 2 * k + j, :], start=(j == 0), stop=(j == 1))
                mm.then_inc(s_w0c, 1)
            pe.wait_ge(s_bstat, 1)
            for j in range(4):
                pe.matmul(ps[:, 2, 0:D], bstat[:, j, :], w_raw[:, 4 + j, :], start=(j == 0), stop=False)
            pe.matmul(ps[:, 2, 0:D], onesf[0:1, :], bcomb, start=False, stop=True).then_inc(s_w0c, 1)
            pe.wait_ge(s_x, 16)
            for n in range(2 * C):
                f, c = n // C, n % C
                if n < 2:
                    pe.wait_ge(s_w0t_out, n + 1)
                else:
                    pe.wait_ge(s_xt_out, n - 1)
                for q in range(TC):
                    mm = pe.transpose(ps[:, 4 + n % 2, q * P:(q + 1) * P],
                                      x32[:, c * TC + q, f * P:(f + 1) * P], identf[:, :])
                mm.then_inc(s_xt, 1)

            def transpose_adj(t):
                pe.wait_ge(s_cast, t + 1)
                for h in range(2):
                    if t >= 1:
                        pe.wait_ge(s_tadj_out, 2 * t - 1 + h)
                    bank = ps[:, 6 + h, :].bitcast(F16)
                    for b in range(8):
                        m = 8 * h + b
                        mm = pe.transpose(bank[:, b * P:(b + 1) * P], A16[:, t, m * P:(m + 1) * P], identh[:, :])
                    mm.then_inc(s_tadj, 1)

            def aggregate(c):
                if c == 0:
                    pe.wait_ge(s_xb, 1)
                    pe.wait_ge(s_w0c_out, 3)
                else:
                    pe.wait_ge(s_agg_out, c)
                for m in range(T):
                    pe.wait_ge(s_mask, c * T + m + 1)
                    mask = mk[:, m % RING, :]
                    for f in range(FT):
                        for s in range(3):
                            pe.matmul(ps[:, f, :], xb[:, m, s, f * P:(f + 1) * P], mask,
                                      start=(m == 0 and s == 0), stop=(m == T - 1 and s == 2))
                    if m == 0 and c >= 1:
                        pe.wait_ge(s_lin_out, TC * c - 1)
                    pe.matmul(ps[:, 2, :], onesh[:, :], mask, start=(m == 0), stop=(m == T - 1)).then_inc(s_agg_m, 1)

            def linear(c):
                pe.wait_ge(s_agg_out, c + 1)
                if c == 0:
                    pe.wait_ge(s_xt_out, 2 * C)
                for q in range(TC):
                    n = c * TC + q
                    if n >= 2:
                        pe.wait_ge(s_lin_out, n - 1)
                    o = ps[:, 2 + q % 2, 0:D]
                    for f in range(FT):
                        pe.matmul(o, xT[:, f, n * P:(n + 1) * P], W0[:, f, :], start=(f == 0), stop=False)
                    for f in range(FT):
                        mm = pe.matmul(o, aggT[:, f, q * P:(q + 1) * P], W0[:, FT + f, :], start=False,
                                       stop=(f == FT - 1))
                    mm.then_inc(s_lin, 1)

            def transpose_x1(c):
                pe.wait_ge(s_x1, TC * (c + 1))
                for f in range(FT):
                    if c >= 1:
                        pe.wait_ge(s_x1t_out, FT * (c - 1) + f + 1)
                    for q in range(TC):
                        mm = pe.transpose(ps[:, 4 + f, q * P:(q + 1) * P], y0[:, q, f * P:(f + 1) * P], identf[:, :])
                    mm.then_inc(s_x1t, 1)

            for t in range(TC):
                transpose_adj(t)
            for c in range(C):
                aggregate(c)
                if c >= 1:
                    transpose_x1(c - 1)
                if c + 1 < C:
                    for t in range(TC * (c + 1), TC * (c + 2)):
                        transpose_adj(t)
                linear(c)
            transpose_x1(C - 1)

            pe.wait_ge(s_sel, 1)
            pe.wait_ge(s_lin_out, N // P)
            for c in range(C):
                for m in range(T):
                    pe.matmul(ps[0:8, c, :], sel[:, 0, :], At16[:, m, c * CH:(c + 1) * CH], start=(m == 0), stop=False)
                for m in range(T):
                    mm = pe.matmul(ps[0:8, c, :], sel[:, 1, :], A16[:, m, c * CH:(c + 1) * CH], start=False,
                                   stop=(m == T - 1))
                mm.then_inc(s_deg, 1)
            pe.wait_ge(s_x1t_out, FT * C)
            for n in range(9):
                g, kk = n // 3, n % 3
                pe.wait_ge(s_graw, 16 * (g + 1))
                if n >= 2:
                    pe.wait_ge(s_gt_out, n - 1)
                for k in range(2):
                    for j in range(2):
                        mm = pe.transpose(ps[:, 4 + n % 2, k * D + j * P:k * D + (j + 1) * P],
                                          graw[:, j, (2 * kk + k) * P:(2 * kk + k + 1) * P], identf[:, :])
                mm.then_inc(s_gt, 1)
            pe.wait_ge(s_gt_out, 9)
            pe.wait_ge(s_w1, 16 * 7)
            pe.wait_ge(s_deg_out, C)
            for n in range(4):
                io, i = n // 2, n % 2
                if n >= 2:
                    pe.wait_ge(s_wg_out, n - 1)
                for lo, hi, bank in ((0, 512, 0), (512, gates, 1)):
                    for j in range(2):
                        mm = pe.matmul(ps[:, 2 * (n % 2) + bank, 0:hi - lo], ioW[:, 2 * io + j, i * P:(i + 1) * P],
                                       RT[:, 2 * io + j, lo:hi], start=(j == 0), stop=(j == 1))
                mm.then_inc(s_wg, 1)
            pe.wait_ge(s_sel, 2)
            for lo, hi, bank in ((0, 512, 6), (512, gates, 7)):
                for j in range(4):
                    mm = pe.matmul(ps[0:8, bank, 0:hi - lo], bst1[:, j, :], RT[:, j, lo:hi], start=(j == 0), stop=(j == 3))
            mm.then_inc(s_dwp, 1)
            pe.wait_ge(s_wg_out, 4)
            pe.wait_ge(s_dwp_out, 1)
            pe.wait_ge(s_drows, 1)

            def turn(i, p):
                pe.wait_ge(s_state, 4 * i + p // 2 + 1)
                if p in (5, 6):
                    pe.wait_ge(s_rows, 8 * i + p - 4)
                for t in range(2):
                    for f in range(FT):
                        n = 2 * p + t
                        mm = pe.transpose(ps[:, TURN[p], t * D + f * P:t * D + (f + 1) * P],
                                          xT[:, f, n * P:(n + 1) * P], identf[:, :])
                mm.then_inc(s_turn, 1)

            with pe.Fori(0, STEPS) as i:
                pe.wait_ge(s_z, 8 * i + 8)
                for p in range(4):
                    turn(i, p)
                for c in range(C):
                    moving = [At16, At16, A16, A16]
                    for g in range(2 * FT):
                        f = g % 2
                        if c == 0 and g == 1:
                            pe.wait_ge(s_rows, 8 * i + 8)
                        if c >= 1:
                            pe.wait_ge(s_U, 16 * i + 4 * (c - 1) + g + 1)
                        for m in range(T):
                            if c == 0 and g == 0 and m % 2 == 0:
                                if m >= 2 and m // 2 + 3 < 8:
                                    turn(i, m // 2 + 3)
                                pe.wait_ge(s_rows, 8 * i + m // 2 + 1)
                            for s in range(2):
                                mm = pe.matmul(ps[:, g, :], rows16[:, m, s, f * P:(f + 1) * P],
                                               moving[g][:, m, c * CH:(c + 1) * CH], start=(m == 0 and s == 0),
                                               stop=(m == T - 1 and s == 1))
                        mm.then_inc(s_prod, 1)
                    cols = slice(c * CH, (c + 1) * CH)

                    def gate(j, last):
                        o, w = ps[:, 4 + j % 4, :], slice(j * P, (j + 1) * P)
                        pe.matmul(o, dw[:, w], drows[:, cols], start=True, stop=False)
                        if j < 4:
                            for f in range(FT):
                                pe.matmul(o, Wg[:, 4 + f, w], xT[:, f, cols], start=False, stop=False)
                        for g in range(2 * FT):
                            if j == 0:
                                pe.wait_ge(s_U, 16 * i + 4 * c + g + 1)
                            mm = pe.matmul(o, Wg[:, g, w], U[:, g, :], start=False, stop=(j < 4 and g == 3))
                        if j >= 4:
                            pe.wait_ge(s_rs, 4 * i + c + 1)
                            for f in range(FT):
                                mm = pe.matmul(o, Wg[:, 4 + f, w], gz[:, f, :], start=False, stop=(f == 1))
                        mm.then_inc(s_gate, 1)

                    if c >= 1:
                        pe.wait_ge(s_h, 8 * i + 2 * c)
                        pe.wait_ge(s_z, 8 * i + 8 + 2 * c)
                    for j in range(4):
                        gate(j, False)
                    pe.wait_ge(s_r, 8 * i + 2 * c + 2)
                    for j in range(4, 6):
                        gate(j, True)

            pe.wait_ge(s_state, 4 + C * STEPS)
            pe.wait_ge(s_ow, 16 * 4)
            for k in range(2):
                for j in range(2):
                    for i in range(2):
                        mm = pe.transpose(ps[:, k, j * D + i * P:j * D + (i + 1) * P],
                                          oraw[:, 2 * k + i, j * P:(j + 1) * P], identf[:, :])
                mm.then_inc(s_ot, 1)
            pe.matmul(ps[:, 2, 0:D], onesf[0:1, :], o2b[:, :], start=True, stop=True).then_inc(s_ot, 1)
            pe.wait_ge(s_ot_out, 2)
            for c in range(C):
                for g in range(FT):
                    if c >= 1:
                        pe.wait_ge(s_o1_out, FT * (c - 1) + g + 1)
                    for k in range(FT):
                        mm = pe.matmul(ps[:, 4 + g, :], oT[:, k, g * P:(g + 1) * P], xT[:, k, c * CH:(c + 1) * CH],
                                       start=(k == 0), stop=(k == 1))
                    mm.then_inc(s_o1, 1)
                pe.wait_ge(s_o1_out, FT * (c + 1))
                for q in range(TC):
                    n = c * TC + q
                    if n >= 2:
                        pe.wait_ge(s_y1, n - 1)
                    for k in range(FT):
                        mm = pe.matmul(ps[:, 6 + q % 2, 0:D], TT[:, k, q * P:(q + 1) * P], oT[:, 2 + k, :],
                                       start=(k == 0), stop=(k == 1))
                    mm.then_inc(s_o2, 1)

            for t in range(T):
                pe.wait_ge(s_klo, 2 * t + 2)
                for hh in range(2):
                    if t >= 1:
                        pe.wait_ge(s_kout[hh], t)
                    for h in range(4):
                        mm = pe.transpose(ps[:, 4 + hh, h * P:(h + 1) * P],
                                          kstk[:, t % 2, 4 * hh + h, :, :].bitcast(F32).rearrange("p a b -> p (a b)"),
                                          identf[:, :])
                    mm.then_inc(s_kt, 1)

            def turn_q(t, hh):
                if hh == 0:
                    pe.wait_ge(s_qlo, 2 * t + 2)
                else:
                    pe.wait_ge(s_qout[0], t + 1)
                for h in range(4):
                    mm = pe.transpose(ps[:, 7, h * P:(h + 1) * P],
                                      qstk[:, 4 * hh + h, :, :].bitcast(F32).rearrange("p a b -> p (a b)"),
                                      identf[:, :])
                mm.then_inc(s_qT, 1)

            turn_q(0, 0)
            turn_q(0, 1)
            for hh in range(2):
                pe.wait_ge(s_kout[hh], T)
            pe.wait_ge(s_v, 16)

            def products(g, q):
                hh = q[1]
                for who in ("act", "dve"):
                    wait_block_taken(pe, g, max(b for b in range(4 * q[0] + 4) if TAKER[b] == who))
                for b in range(4 * q[0], 4 * q[0] + 4):
                    for h in range(4):
                        col = (4 * hh + h) * HD
                        mm = pe.matmul(ps[h * HD:(h + 1) * HD, 6, 0:P], v_sb[:, b, col:col + HD],
                                       PT[:, q[0] % 2, b % 4, h * P:(h + 1) * P], start=(b == 0), stop=(b == T - 1),
                                       tile_position=(0, h * HD))
                mm.then_inc(s_pv, 1)

            def slot(t, g, gamma, j, has1, has2, front, more):
                hh, n = gamma % 2, 4 * g + j
                if front:
                    if j == 0:
                        pe.wait_ge(s_qout[hh], t + 1)
                    h = 4 * hh + j
                    for u in range(2):
                        if has1 or j >= 1:
                            pe.wait_ge(s_masked, 2 * n + u - 1)
                        for w in range(2):
                            mm = pe.matmul(ps[:, 2 * u + w, :], qst[:, gamma // 2, h, :],
                                           kst[:, h, (2 * u + w) * CH:(2 * u + w + 1) * CH], start=True, stop=True)
                        mm.then_inc(s_score, 1)
                if has1:
                    if j == 0:
                        pe.wait_ge(s_exp, 4 * g)
                    for b in range(4 * j, 4 * j + 4):
                        if b >= 2:
                            wait_block_taken(pe, g - 1, b - 2)
                        elif has2:
                            wait_block_taken(pe, g - 2, b + 14)
                        for h in range(4):
                            mm = pe.transpose(ps[:, 4 + b % 2, h * P:(h + 1) * P],
                                              prob[:, 4 * (1 - hh) + h, b * P:(b + 1) * P], identf[:, :])
                        mm.then_inc(s_T, 1)
                if has2 and j == 1:
                    pe.wait_ge(s_o, g - 1)
                    pe.transpose(ps[:, 7, 0:P], oT2[:, :], identf[:, :]).then_inc(s_oT, 1)
                if j == 0:
                    if has2:
                        products(g - 2, (3, hh))
                elif has1:
                    products(g - 1, (j - 1, 1 - hh))
                if more and hh == 1 and j >= 2:
                    if j == 2:
                        pe.wait_ge(s_att, g - 1) if has2 else None
                    turn_q(t + 1, j - 2)

            layer2(pe, slot)

            pe.wait_ge(s_w3, 16 * 5)
            for f in range(FT):
                pe.matmul(ps[:, 0, 2 * f:2 * f + 2], W1[:, f * P:(f + 1) * P], w23[:, :], start=True, stop=True)
            pe.matmul(ps[:, 0, 4:6], onesf[0:1, :], b23[:, :], start=True, stop=True).then_inc(s_u, 1)
            for n in range(FT * C):
                f, c = n % FT, n // FT
                pe.wait_ge(s_x3, TC * (c + 1))
                if n >= 2:
                    pe.wait_ge(s_x3t_out, n - 1)
                for q in range(TC):
                    mm = pe.transpose(ps[:, 4 + n % 2, q * P:(q + 1) * P], xr[:, c * TC + q, f * P:(f + 1) * P],
                                      identf[:, :])
                mm.then_inc(s_x3t, 1)
            pe.wait_ge(s_x3t_out, FT * C)
            pe.wait_ge(s_u_out, 3)
            for t in range(T):
                for f in range(FT):
                    mm = pe.matmul(ps[:, 1, t:t + 1], x3T[:, f, t * P:(t + 1) * P], u23[:, f, 0:1], start=(f == 0),
                                   stop=(f == 1))
            mm.then_inc(s_f, 1)
            for c in range(C):
                if c >= 2:
                    pe.wait_ge(s_f_out, c - 1)
                for f in range(FT):
                    mm = pe.matmul(ps[:, 2 + c % 2, :], u3b[:, f, :], x3T[:, f, c * CH:(c + 1) * CH], start=(f == 0),
                                   stop=(f == 1))
                mm.then_inc(s_f, 1)
            pe.wait_ge(s_f_out, C)

            def tile3(t, b, first, bank):
                pe.wait_ge(s_exp3, t + 1)
                for c in range(C):
                    if not first:
                        pe.wait_ge(s_T3_out, C * t + c - 3)
                    for q in range(TC):
                        m = c * TC + q
                        mm = pe.transpose(ps[:, 2 + c, q * P:(q + 1) * P], coef[:, b, m * P:(m + 1) * P], identf[:, :])
                    mm.then_inc(s_T3, 1)

            def values3(t, b, used):
                if used:
                    pe.wait_ge(s_val_out, t - 1)
                for m in range(T):
                    if m % TC == 0:
                        pe.wait_ge(s_T3_out, C * t + m // TC + 1)
                    mm = pe.matmul(ps[:, 6 + b, 0:D], coefT[:, b, m * P:(m + 1) * P], xr[:, m, :], start=(m == 0),
                                   stop=(m == T - 1))
                mm.then_inc(s_val, 1)

            tile3(0, 0, True, 0)
            tile3(1, 1, False, 0)
            values3(0, 0, False)
            with pe.Fori(1, T // 2) as i:
                tile3(2 * i, 0, False, 0)
                values3(2 * i - 1, 1, False)
                tile3(2 * i + 1, 1, False, 0)
                values3(2 * i, 0, True)
            values3(T - 1, 1, True)

        @block.vector
        def _(dve):
            steps = [0]

            def link(ins):
                steps[0] += 1
                ins.then_inc(s_dve, 1)
                dve.wait_ge(s_dve, steps[0])

            dve.wait_ge(s_x, 16)
            link(dve.tensor_copy(xb[:, :, 0, :], x32))
            link(dve.tensor_tensor(rest, x32, xb[:, :, 0, :], ALU.subtract))
            link(dve.tensor_copy(xb[:, :, 1, :], rest))
            link(dve.tensor_tensor(rest, rest, xb[:, :, 1, :], ALU.subtract))
            dve.tensor_copy(xb[:, :, 2, :], rest).then_inc(s_xb, 1)
            dve.wait_ge(s_const, 7)
            dve.wait_ge(s_w0, 16 * W0_BITS)
            for j in range(4):
                last = dve.tensor_scalar(bstat[:, j, :], onesf[:, :], bcol0[:, j:j + 1], None, ALU.mult)
            last.then_inc(s_bstat, 1)

            def cast(t):
                dve.wait_ge(s_adj[t % 2], 16 * (t // 2 + 1))
                if t == 4:
                    dve.wait_ge(s_xb, 1)
                if t == 8:
                    dve.wait_ge(s_w0c, 3)
                    dve.wait_ge(s_w0t_out, 2)
                if t == 12:
                    dve.wait_ge(s_xt, 2 * C)
                dve.tensor_copy(A16[:, t, :], stage[:, t % 2, :]).then_inc(s_cast, 1)

            def mask(c, m):
                n = c * T + m
                if m == 0:
                    dve.wait_ge(s_tadj_out, 2 * TC * (c + 1))
                if n >= RING:
                    dve.wait_ge(s_agg_m, n - RING + 1)
                dve.tensor_scalar(mk[:, m % RING, :], At16[:, m, c * CH:(c + 1) * CH], 0.0, None, ALU.is_gt).then_inc(s_mask, 1)

            def mean_of_neighbours(c):
                dve.wait_ge(s_agg_m, T * (c + 1))
                if c >= 1:
                    dve.wait_ge(s_lin, TC * c)
                link(dve.tensor_scalar(rdeg[:, :], ps[:, 2, :], 1.0, None, ALU.max))
                link(dve.reciprocal(rdeg[:, :], rdeg[:, :]))
                for f in range(FT):
                    last = dve.tensor_tensor(aggT[:, f, :], ps[:, f, :], rdeg[:, :], ALU.mult)
                last.then_inc(s_agg_out, 1)

            def residual(c):
                dve.wait_ge(s_xres, 16 * (c + 1))
                if c == 0:
                    dve.wait_ge(s_w0c_out, 3)
                else:
                    dve.wait_ge(s_x1_saved, 16 * c)
                    dve.wait_ge(s_x1t, FT * c)
                for q in range(TC):
                    n = c * TC + q
                    dve.wait_ge(s_lin, n + 1)
                    link(dve.tensor_tensor(y0[:, q, :], ps[:, 2 + q % 2, 0:D], bias0[:, :], ALU.add))
                    steps[0] += 1
                    dve.scalar_tensor_tensor(y0[:, q, :], y0[:, q, :], 0.0, xres[:, q, :], ALU.max,
                                             ALU.add).then_inc(s_lin_out, 1)
                    steps[0] -= 1
                    dve.wait_ge(s_lin_out, n + 1)
                    link(dve.bn_stats(stats[:, q, :], y0[:, q, :]))
                    ins = dve.bn_aggr(mv[:, n, :], stats[:, q, :])
                    if q == TC - 1:
                        ins.then_inc(s_var0, 1)
                    else:
                        link(ins)

            def normalise(c):
                dve.wait_ge(s_std0, c + 1)
                r = rstd[:, c * TC:(c + 1) * TC]
                link(dve.reciprocal(r, r))
                for q in range(TC):
                    n = c * TC + q
                    dve.tensor_scalar(y0[:, q, :], y0[:, q, :], mv[:, n, 0:1], rstd[:, n:n + 1], ALU.subtract,
                                      ALU.mult).then_inc(s_x1, 1)

            for t in range(TC):
                cast(t)
            for m in range(RING):
                mask(0, m)
            for c in range(C):
                for m in range(RING, T):
                    mask(c, m)
                    if m % 3 == 0 and m >= 6 and c + 1 < C:
                        cast(TC * (c + 1) + m // 3 - 2)
                mean_of_neighbours(c)
                if c + 1 < C:
                    for m in range(RING):
                        mask(c + 1, m)
                residual(c)
                normalise(c)

            dve.wait_ge(s_x1t_out, FT * C)
            dve.wait_ge(s_x1_saved, 16 * C)
            link(dve.memset(sel[:, :, :], 0.0))
            for k in range(2):
                last = dve.memset(sel[:, k, 4 * k:4 * k + 4], 1.0)
            last.then_inc(s_sel, 1)
            link(dve.memset(bst1[:, :, :], 0.0))
            dve.wait_ge(s_w1, 16 * 7)
            for j in range(4):
                k = j // 2
                last = dve.tensor_scalar(bst1[:, j, 4 * k:4 * k + 4], onesf[:, 0:4], bcol1[:, j:j + 1], None, ALU.mult)
            last.then_inc(s_sel, 1)
            eye = identf[0:8, 0:8]
            halves = eye.rearrange("p (a b) -> p a b", b=4)
            evens = eye.rearrange("p (a b) -> p b a", b=2)
            dve.tensor_reduce(dmask[:, 0:1], halves[:, :, 0:2], AX.XY, ALU.add)
            dve.tensor_reduce(dmask[:, 1:2], halves[:, :, 2:4], AX.XY, ALU.add)
            dve.tensor_reduce(dmask[:, 2:3], evens[:, 0, :], AX.X, ALU.add)
            link(dve.tensor_reduce(dmask[:, 3:4], evens[:, 1, :], AX.X, ALU.add))

            def split_rows(dst, src, masks):
                link(dve.tensor_copy(dst, src))
                link(dve.tensor_tensor(src, src, dst.bitcast(F32), ALU.subtract))
                link(dve.tensor_scalar(src, src, dmask[:, masks + 1:masks + 2], None, ALU.mult))
                return dve.scalar_tensor_tensor(dst, dst.bitcast(F32), dmask[:, masks:masks + 1], src, ALU.mult, ALU.add)

            dve.wait_ge(s_deg_out, C)
            link(split_rows(drows[:, :], dsum, 0))
            dve.wait_ge(s_dwp, 1)
            link(dve.tensor_copy(dsum[:, 0:gates], ps[0:8, 6:8, :].rearrange("p a b -> p (a b)")[:, 0:gates]))
            split_rows(dw[:, :], dsum[:, 0:gates], 2).then_inc(s_dwp_out, 1)
            dve.wait_ge(s_dwp_out, 1)
            dve.memset(rstd[:, :], 0.0).then_inc(s_drows, 1)
            dve.sem_inc(s_z, 8)
            dve.sem_inc(s_state, 4)

            with dve.Fori(0, STEPS) as i:
                for p in range(T // 2):
                    dve.wait_ge(s_hi, 8 * i + p + 1)
                    dve.scalar_tensor_tensor(rows16[:, 2 * p:2 * p + 2, 1, :],
                                             ps[:, TURN[p], :].rearrange("p (t n) -> p t n", t=2), 2048.0,
                                             rows16[:, 2 * p:2 * p + 2, 0, :], ALU.mult, ALU.subtract).then_inc(s_rows, 1)
                for c in range(C):
                    state = xT[:, :, c * CH:(c + 1) * CH]
                    dve.wait_ge(s_r, 8 * i + 2 * c + 2)
                    dve.tensor_tensor(gz[:, 0:2, :], gz[:, 0:2, :], state, ALU.mult).then_inc(s_rs, 1)
                    dve.wait_ge(s_h, 8 * i + 2 * c + 2)
                    dve.tensor_tensor(gz[:, 0:2, :], gz[:, 0:2, :], state, ALU.subtract).then_inc(s_upd, 1)
                    dve.wait_ge(s_upd, 8 * i + 2 * c + 1)
                    dve.wait_ge(s_z, 8 * i + 8 + 2 * c + 2)
                    dve.tensor_tensor(gz[:, 0:2, :], gz[:, 0:2, :], gz[:, 2:4, :], ALU.mult).then_inc(s_upd, 1)
                    dve.wait_ge(s_upd, 8 * i + 2 * c + 2)
                    dve.tensor_tensor(state, state, gz[:, 0:2, :], ALU.add).then_inc(s_state, 1)

            dve.wait_ge(s_ot_out, 3)
            for c in range(C):
                dve.wait_ge(s_x1r[c % 2], 16 * (c // 2 + 1))
                for q in range(TC):
                    n = c * TC + q
                    dve.wait_ge(s_o2, n + 1)
                    dve.tensor_tensor(xr[:, n, :], ps[:, 6 + q % 2, 0:D], bias1[:, :], ALU.add).then_inc(s_y1, 1)
                    dve.wait_ge(s_y1, n + 1)
                    link(dve.tensor_tensor(xr[:, n, :], xr[:, n, :], x1r[:, c % 2, q, :], ALU.add))
                    link(dve.bn_stats(stats[:, q, :], xr[:, n, :]))
                    ins = dve.bn_aggr(mv[:, n, :], stats[:, q, :])
                    if n == T - 1:
                        ins.then_inc(s_var1, 1)
                    else:
                        link(ins)
            dve.wait_ge(s_std1, 1)
            link(dve.reciprocal(rstd[:, :], rstd[:, :]))
            for n in range(T):
                dve.tensor_scalar(xr[:, n, :], xr[:, n, :], mv[:, n, 0:1], rstd[:, n:n + 1], ALU.subtract,
                                  ALU.mult).then_inc(s_x2, 1)

            for t in range(T):
                b = t % 2
                for r in (0, 1):
                    dve.wait_ge(s_khi, 2 * t + r + 1)
                    dve.tensor_tensor(kstk[:, b, :, 2 * r + 1, :], kin[:, b, :].rearrange("p (h d) -> p h d", h=HEADS),
                                      kstk[:, b, :, 2 * r, :].bitcast(F32), ALU.subtract).then_inc(s_klo, 1)
                dve.wait_ge(s_kt, 2 * t + 2)
                dve.tensor_copy(kst[:, 4:8, t * P:(t + 1) * P], ps[:, 5, :].rearrange("p (h n) -> p h n", h=4))\
                    .then_inc(s_kout[1], 1)

            SCALE = float(HD) ** -0.5

            def q_lo(t):
                for r in (0, 1):
                    dve.wait_ge(s_qhi, 2 * t + r + 1)
                    dve.scalar_tensor_tensor(qstk[:, :, 2 + r, :], xr[:, t, :].rearrange("p (h d) -> p h d", h=HEADS),
                                             SCALE, qstk[:, :, r, :].bitcast(F32), ALU.mult, ALU.subtract)\
                        .then_inc(s_qlo, 1)

            def q_out(t, b):
                dve.wait_ge(s_qT, 2 * t + 2)
                dve.tensor_copy(qst[:, b, 4:8, :], ps[:, 7, :].rearrange("p (h n) -> p h n", h=4)).then_inc(s_qout[1], 1)

            q_lo(0)
            q_out(0, 0)

            def slot(t, g, gamma, j, has1, has2, front, more):
                hh, n = gamma % 2, 4 * g + j
                ring = 4 * gamma + j
                if has2 and j == 2:
                    old = (gamma + 2) % 4
                    rows = xr[:, t - 1, hh * P:(hh + 1) * P]
                    base = FINISH * (g - 2)
                    dve.wait_ge(s_exp, 4 * g - 4)
                    dve.reciprocal(rinv2[:, :], rsum2[:, 4 * old:4 * old + 4]).then_inc(s_fin2, 1)
                    dve.wait_ge(s_oT, g - 1)
                    dve.wait_ge(s_fin2, base + 1)
                    dve.tensor_tensor(row2[:, hh * P:(hh + 1) * P].rearrange("p (h d) -> p h d", h=4),
                                      ps[:, 7, 0:P].rearrange("p (h d) -> p h d", h=4),
                                      rinv2[:, :].unsqueeze(2).broadcast_to([P, 4, HD]), ALU.mult).then_inc(s_att, 1)
                    dve.wait_ge(s_att, g - 1)
                    dve.tensor_tensor(row2[:, hh * P:(hh + 1) * P], rows, row2[:, hh * P:(hh + 1) * P], ALU.add).then_inc(s_fin2, 1)
                    if hh == 1:
                        dve.wait_ge(s_fin2, base + 2)
                        dve.sem_inc(s_passed["dve"], 1)
                        dve.bn_stats(stats[:, 0, :], row2[:, :]).then_inc(s_stat2, 1)
                        dve.tensor_copy(xr[:, t - 1, :], row2[:, :]).then_inc(s_stat2, 1)
                        dve.wait_ge(s_stat2, 4 * t - 2)
                        dve.sem_inc(s_passed["dve"], 1)
                        dve.bn_aggr(mv1[:, :], stats[:, 0, :]).then_inc(s_stat2, 1)
                        dve.wait_ge(s_stat2, 4 * t - 1)
                        dve.tensor_copy(mv[:, t - 1, :], mv1[:, :]).then_inc(s_stat2, 1)
                if front:
                    if hh == 0 and j == 0:
                        dve.wait_ge(s_bias2, t + 1)
                    if has2:
                        dve.wait_ge(s_T, T * (g - 1))
                    for u in range(2):
                        half = slice(u * 1024, (u + 1) * 1024)
                        dve.wait_ge(s_score, 2 * n + u + 1)
                        dve.sem_inc(s_passed["dve"], 1)
                        dve.tensor_tensor_reduce(prob[:, 4 * hh + j, half],
                                                 ps[:, 2 * u:2 * u + 2, :].rearrange("p a b -> p (a b)"),
                                                 bias2[:, gamma // 2, half], 1.0, NEG_INIT, ALU.add, ALU.max,
                                                 mx2[:, ring, u:u + 1]).then_inc(s_masked, 1)
                    dve.wait_ge(s_masked, 2 * n + 2)
                    dve.tensor_scalar(neg2[:, ring:ring + 1], mx2[:, ring, 0:1], mx2[:, ring, 1:2], -1.0, ALU.max,
                                      ALU.mult).then_inc(s_neg, 1)
                if more and hh == 1 and j == 1:
                    q_lo(t + 1)
                if has1:
                    for b in range(4 * j, 4 * j + 4):
                        if TAKER[b] == "dve":
                            take_block(dve, dve.tensor_copy, g - 1, b, has2)
                if more and hh == 1 and j == 3:
                    q_out(t + 1, (gamma // 2 + 1) % 2)

            layer2(dve, slot)
            dve.wait_ge(s_stat2, 4 * T)
            dve.sem_inc(s_var2, 1)
            dve.wait_ge(s_std2, 1)
            link(dve.reciprocal(rstd[:, :], rstd[:, :]))
            for n in range(T):
                dve.tensor_scalar(xr[:, n, :], xr[:, n, :], mv[:, n, 0:1], rstd[:, n:n + 1], ALU.subtract,
                                  ALU.mult).then_inc(s_x3, 1)

            dve.wait_ge(s_u_out, 2)
            for f in range(FT):
                last = dve.tensor_scalar(u3b[:, f, :], onesf[:, :], u23[:, f, 1:2], None, ALU.mult)
            last.then_inc(s_u_out, 1)
            dve.wait_ge(s_f, 1)
            link(dve.tensor_scalar(f1[:, :], ps[:, 1, 0:T], bc23[:, 0:1], None, ALU.add))
            dve.wait_ge(s_f_out, C)

            def logits3(t, b, k, used):
                w = coef[:, b, :]
                dve.wait_ge(s_adj3[b], 16 * k + 16)
                if used:
                    dve.wait_ge(s_T3, C * (t - 1))
                dve.scalar_tensor_tensor(w, f2[:, :], f1[:, t:t + 1] if isinstance(t, int) else f1[:, bass.ds(t, 1)],
                                         adj3[:, b, :], ALU.add, ALU.mult).then_inc(s_logit, 1)
                dve.wait_ge(s_logit, t + 1)
                dve.scalar_tensor_tensor(w, w, 0.01, w, ALU.mult, ALU.max).then_inc(s_l3, 1)
                dve.wait_ge(s_l3, 2 * t + 1)
                dve.wait_ge(s_bias3, t + 1)
                dve.sem_inc(s_passed["dve"], 1)
                dve.tensor_tensor_reduce(w, w, bias3[:, b, :], 1.0, NEG_INIT, ALU.add, ALU.max, mx3[:, b:b + 1])\
                    .then_inc(s_l3, 1)
                dve.wait_ge(s_l3, 2 * t + 2)
                dve.tensor_scalar(neg3[:, b:b + 1], mx3[:, b:b + 1], -1.0, None, ALU.mult).then_inc(s_neg3, 1)

            def finish3(t, b):
                row = row3[:, b, :]
                base = 6 * t
                dve.wait_ge(s_val, t + 1)
                dve.reciprocal(rinv3[:, b:b + 1], rsum3[:, b:b + 1]).then_inc(s_f3, 1)
                dve.wait_ge(s_f3, base + 1)
                dve.tensor_scalar(row, ps[:, 6 + b, 0:D], rinv3[:, b:b + 1], 0.0, ALU.mult, ALU.max)\
                    .then_inc(s_val_out, 1)
                dve.wait_ge(s_val_out, t + 1)
                dve.tensor_tensor(row, row, xr[:, t, :], ALU.add).then_inc(s_f3, 1)
                dve.wait_ge(s_f3, base + 2)
                dve.sem_inc(s_passed["dve"], 1)
                dve.bn_stats(stats[:, 0, :], row).then_inc(s_f3, 1)
                dve.tensor_copy(y3[:, t, :], row).then_inc(s_f3, 1)
                dve.wait_ge(s_f3, base + 4)
                dve.sem_inc(s_passed["dve"], 1)
                dve.bn_aggr(mv3[:, :], stats[:, 0, :]).then_inc(s_f3, 1)
                dve.wait_ge(s_f3, base + 5)
                dve.tensor_copy(mv[:, t, :], mv3[:, :]).then_inc(s_f3, 1)

            logits3(0, 0, 0, False)
            logits3(1, 1, 0, False)
            finish3(0, 0)
            with dve.Fori(1, T // 2) as i:
                for b in range(2):
                    logits3(2 * i + b, b, i, True)
                    finish3(2 * i + b - 1, 1 - b)
            finish3(T - 1, 1)
            dve.wait_ge(s_f3, 6 * T)
            dve.sem_inc(s_var3, 1)
            dve.wait_ge(s_std3, 1)
            link(dve.reciprocal(rstd[:, :], rstd[:, :]))
            for n in range(T):
                dve.tensor_scalar(y3[:, n, :], y3[:, n, :], mv[:, n, 0:1], rstd[:, n:n + 1], ALU.subtract,
                                  ALU.mult).then_inc(s_y3, 1)


NAMES = ["x", "adj", "L0_gnn_W_self", "L0_gnn_b_self", "L0_gnn_W_nb", "L0_gnn_b_nb", "L0_gnn_W_comb", "L0_gnn_b_comb",
         "L1_gnn_in_W", "L1_gnn_in_b", "L1_gnn_out_W", "L1_gnn_out_b", "L1_gnn_r_W", "L1_gnn_r_b", "L1_gnn_z_W",
         "L1_gnn_z_b", "L1_gnn_h_W", "L1_gnn_h_b", "L1_gnn_o1_W", "L1_gnn_o1_b", "L1_gnn_o2_W", "L1_gnn_o2_b",
         "L2_gnn_x2", "L2_gnn_v", "L3_gnn_W1", "L3_gnn_w2", "L3_gnn_b2", "L3_gnn_w3", "L3_gnn_b3"]


def kernel(**inputs):
    import numpy as _np
    import concourse.bacc as _bacc
    from concourse import mybir as _mybir
    from concourse.bass_utils import run_bass_kernel_spmd as _run

    nc = _bacc.Bacc("TRN2", target_bir_lowering=False, num_devices=1)
    arrays, args = {}, {}
    for name in NAMES:
        v = _np.ascontiguousarray(inputs[name])
        arrays[f"in_{name}_dram"] = v
        args[name] = nc.dram_tensor(f"in_{name}_dram", v.shape, _mybir.dt.from_np(v.dtype), kind="ExternalInput").ap()
    out = nc.dram_tensor("out_0_dram", (N, D), F32, kind="ExternalOutput").ap()
    program(nc, args, out)
    r = _run(nc, [arrays], core_ids=[0])
    return r.results[0]["out_0_dram"]
```

```python
from contextlib import ExitStack

import concourse.bass as bass
from concourse import mybir

P = 128
F32 = mybir.dt.float32
F32R = mybir.dt.float32r
BF16 = mybir.dt.bfloat16
F16 = mybir.dt.float16
I32 = mybir.dt.int32
F8 = mybir.dt.float8e4
ALU = mybir.AluOpType
ACT = mybir.ActivationFunctionType
AX = mybir.AxisListType

N = 2048
D = 256
T = N // P
FT = D // P
CH = 512
C = N // CH
TC = CH // P
STEPS = 5
HEADS = 8
HD = D // HEADS
EPS = 1e-5
NEG_INIT = -3.4e38
FINISH = 2
RING = 4


def program(nc, a, out):
    ctx = ExitStack()
    with ctx:
        def sem(name):
            return ctx.enter_context(nc.semaphore(name))

        def sb(name, shape, dt, scope=ctx):
            return scope.enter_context(nc.sbuf_tensor(name, shape, dt))

        x1_dram = nc.dram_tensor("x1_rows_scratch", [N, D], F32, kind="Internal").ap()
        ps = ctx.enter_context(nc.psum_tensor("ps", [P, 8, 512], F32))

        identf = sb("identf", [P, P], F32)
        identh = sb("identh", [P, P], F16)
        onesf = sb("onesf", [P, P], F32)
        onesh = sb("onesh", [P, P], F16)
        eps_col = sb("eps_col", [P, 1], F32)
        stats = sb("stats", [P, TC, 6], F32)
        TURN = [6, 7, 1, 2, 3, 6, 7, 4]
        mv = sb("mv", [P, T, 2], F32)
        rstd = sb("rstd", [P, T], F32)

        graph = ExitStack()
        A8 = sb("A8", [P, T, N], F8, graph)
        At8 = sb("At8", [P, T, N], F8, graph)
        xT = sb("xT", [P, FT, N], F32, graph)
        gates = 3 * D

        first = ExitStack()
        x32 = sb("x32", [P, T, D], F32, first)
        rest = sb("rest", [P, T, D], F32, first)
        first.close()
        raw = ExitStack()
        graw = sb("graw", [P, 3, FT, gates], F32, raw)
        ioW = sb("ioW", [P, 2 * FT, D], F32, raw)
        raw.close()
        fin = ExitStack()
        oraw = sb("oraw", [P, 2 * FT, D], F32, fin)
        oT = sb("oT", [P, 2 * FT, D], F32, fin)
        o2b = sb("o2b", [1, D], F32, fin)
        bias1 = sb("bias1", [P, D], F32, fin)
        o1col = sb("o1col", [P, FT], F32, fin)
        TT = sb("TT", [P, FT, CH], F32, fin)
        x1r = sb("x1r", [P, 2, TC, D], F32, fin)
        fin.close()
        rows16 = sb("rows16", [P, T, 2, D], F16, graph)
        SX = sb("SX", [P, 2, FT, CH], F32R, graph)
        RX = sb("RX", [P, 2, FT, CH], F32R, graph)

        l0 = ExitStack()
        stage = sb("stage", [P, 2, N], I32, l0)
        a16 = sb("a16", [P, TC, N], F16, l0)
        xb = sb("xb", [P, T, 3, D], BF16, l0)
        mk = sb("mk", [P, RING, CH], F16, l0)
        aggT = sb("aggT", [P, FT, CH], F32, l0)
        rdeg = sb("rdeg", [P, CH], F32, l0)
        xres = sb("xres", [P, TC, D], F32, l0)
        y0 = sb("y0", [P, TC, D], F32, l0)
        W0 = sb("W0", [P, 2 * FT, D], F32, l0)
        bias0 = sb("bias0", [P, D], F32, l0)
        bcol0 = sb("bcol0", [P, 2 * FT], F32, l0)
        w_raw = sb("w_raw", [P, 4 * FT, D], F32, l0)
        w_tr = sb("w_tr", [P, 2 * FT, D], F32, l0)
        bstat = sb("bstat", [P, 2 * FT, P], F32, l0)
        bcomb = sb("bcomb", [1, D], F32, l0)
        l0.close()

        l1 = ExitStack()
        drows = sb("drows", [8, N], F32R, l1)
        dw = sb("dw", [8, gates], F32R, l1)
        Wg = sb("Wg", [P, 2, 3 * FT, gates], F32R, l1)
        gb = sb("gb", [P, 3 * FT], F32, l1)
        gz = sb("gz", [P, 2 * FT, CH], F32, l1)
        bcol1 = sb("bcol1", [P, 2 * FT], F32, l1)
        sel = sb("sel", [P, 2, 8], F16, l1)
        bst1 = sb("bst1", [P, 2 * FT, 8], F32, l1)
        dmask = sb("dmask", [8, 4], F32, l1)
        dsum = gz[0:8, :, :].rearrange("p a b -> p (a b)")
        prep = ExitStack()
        RT = sb("RT", [P, 2 * FT, gates], F32, prep)
        prep.close()
        U = sb("U", [P, 2, 2 * FT, CH], F32R, l1)
        l1.close()
        graph.close()

        l2 = ExitStack()
        kst = sb("kst", [P, HEADS, N], F32R, l2)
        PT = sb("PT", [P, 2, 4, CH], F32, l2)
        before = ExitStack()
        place_of_fin = sb("place_of_fin", [P, 4, N], F32, before)
        kin = sb("kin", [P, 2, D], F32, before)
        kstk = sb("kstk", [P, 2, HEADS, 4, HD], F32R, before)
        before.close()
        prob = sb("prob", [P, HEADS, N], F32, l2)
        xr = sb("xr", [P, T, D], F32, l2)
        v_sb = sb("v_sb", [P, T, D], F32, l2)
        adj2 = sb("adj2", [P, N], I32, l2)
        bias2 = sb("bias2", [P, 2, N], BF16, l2)
        qst = sb("qst", [P, 2, HEADS, P], F32R, l2)
        qstk = sb("qstk", [P, HEADS, 4, HD], F32R, l2)
        oT2 = sb("oT2", [P, P], F32, l2)
        mv1 = sb("mv1", [P, 2], F32, l2)
        row2 = sb("row2", [P, D], F32, l2)
        mx2 = sb("mx2", [P, 16, 2], F32, l2)
        neg2 = sb("neg2", [P, 16], F32, l2)
        rsum2 = sb("rsum2", [P, 16], F32, l2)
        rinv2 = sb("rinv2", [P, 4], F32, l2)
        l2.close()

        l3 = ExitStack()
        adj3 = sb("adj3", [P, 2, N], I32, l3)
        bias3 = sb("bias3", [P, 2, N], F32, l3)
        coef = sb("coef", [P, 2, N], F32, l3)
        coefT = sb("coefT", [P, 2, N], F32, l3)
        y3 = sb("y3", [P, T, D], F32, l3)
        x3T = sb("x3T", [P, FT, N], F32, l3)
        f2 = sb("f2", [P, N], F32, l3)
        f1 = sb("f1", [P, T], F32, l3)
        W1 = sb("W1", [P, D], F32, l3)
        w23 = sb("w23", [P, 2], F32, l3)
        b23 = sb("b23", [1, 2], F32, l3)
        bc23 = sb("bc23", [P, 2], F32, l3)
        u23 = sb("u23", [P, FT, 2], F32, l3)
        u3b = sb("u3b", [P, FT, P], F32, l3)
        mv3 = sb("mv3", [P, 2], F32, l3)
        row3 = sb("row3", [P, 2, D], F32, l3)
        mx3 = sb("mx3", [P, 2], F32, l3)
        neg3 = sb("neg3", [P, 2], F32, l3)
        rsum3 = sb("rsum3", [P, 2], F32, l3)
        rinv3 = sb("rinv3", [P, 2], F32, l3)
        l3.close()

        s_const = sem("s_const")
        s_x = sem("s_x")
        s_w0 = sem("s_w0")
        s_adj = [sem(f"s_adj{b}") for b in range(2)]
        s_xres = sem("s_xres")
        s_xb = sem("s_xb")
        s_bstat = sem("s_bstat")
        s_cast = sem("s_cast")
        s_cast8 = sem("s_cast8")
        s_tadj = sem("s_tadj")
        s_tadj_out = sem("s_tadj_out")
        s_w0t = sem("s_w0t")
        s_w0t_out = sem("s_w0t_out")
        s_w0c = sem("s_w0c")
        s_w0c_out = sem("s_w0c_out")
        s_xt = sem("s_xt")
        s_xt_out = sem("s_xt_out")
        s_mask = sem("s_mask")
        s_agg_m = sem("s_agg_m")
        s_agg_out = sem("s_agg_out")
        s_lin = sem("s_lin")
        s_lin_out = sem("s_lin_out")
        s_var0 = sem("s_var0")
        s_std0 = sem("s_std0")
        s_x1 = sem("s_x1")
        s_x1_saved = sem("s_x1_saved")
        s_x1t = sem("s_x1t")
        s_x1t_out = sem("s_x1t_out")
        s_w1 = sem("s_w1")
        s_b1 = sem("s_b1")
        s_wlo = sem("s_wlo")
        s_gt_lo = sem("s_gt_lo")
        s_Ulo = sem("s_Ulo")
        s_shi = sem("s_shi")
        s_slo = sem("s_slo")
        s_rhi = sem("s_rhi")
        s_deg = sem("s_deg")
        s_deg_out = sem("s_deg_out")
        s_drows = sem("s_drows")
        s_sel = sem("s_sel")
        s_gt = sem("s_gt")
        s_gt_out = sem("s_gt_out")
        s_wg = sem("s_wg")
        s_wg_out = sem("s_wg_out")
        s_dwp = sem("s_dwp")
        s_dwp_out = sem("s_dwp_out")
        s_state = sem("s_state")
        s_turn = sem("s_turn")
        s_hi = sem("s_hi")
        s_rows = sem("s_rows")
        s_prod = sem("s_prod")
        s_U = sem("s_U")
        s_gate = sem("s_gate")
        s_r = sem("s_r")
        s_z = sem("s_z")
        s_rs = sem("s_rs")
        s_h = sem("s_h")
        s_upd = sem("s_upd")
        s_ow = sem("s_ow")
        s_ot = sem("s_ot")
        s_ot_out = sem("s_ot_out")
        s_x1r = [sem(f"s_x1r{b}") for b in range(2)]
        s_o1 = sem("s_o1")
        s_o1_out = sem("s_o1_out")
        s_o2 = sem("s_o2")
        s_y1 = sem("s_y1")
        s_var1 = sem("s_var1")
        s_std1 = sem("s_std1")
        s_x2 = sem("s_x2")
        s_kin = [sem(f"s_kin{b}") for b in range(2)]
        s_v = sem("s_v")
        s_passed = {"dve": sem("s_passed_dve"), "pool": sem("s_passed_pool"), "pe": sem("s_passed_pe")}
        s_fin2 = sem("s_fin2")
        s_stat2 = sem("s_stat2")
        s_f3 = sem("s_f3")
        s_khi = sem("s_khi")
        s_klo = sem("s_klo")
        s_kt = sem("s_kt")
        s_kout = [sem(f"s_kout{b}") for b in range(2)]
        s_adj2 = sem("s_adj2")
        s_bias2 = sem("s_bias2")
        s_qhi = sem("s_qhi")
        s_qlo = sem("s_qlo")
        s_qT = sem("s_qT")
        s_qout = [sem(f"s_qout{b}") for b in range(2)]
        s_score = sem("s_score")
        s_masked = sem("s_masked")
        s_neg = sem("s_neg")
        s_exp = sem("s_exp")
        s_T = sem("s_T")
        s_PT = {"act": sem("s_PT_act"), "dve": sem("s_PT_dve")}
        s_pv = sem("s_pv")
        s_o = sem("s_o")
        s_oT = sem("s_oT")
        s_att = sem("s_att")
        s_var2 = sem("s_var2")
        s_std2 = sem("s_std2")
        s_x3 = sem("s_x3")
        s_w3 = sem("s_w3")
        s_u = sem("s_u")
        s_u_out = sem("s_u_out")
        s_x3t = sem("s_x3t")
        s_x3t_out = sem("s_x3t_out")
        s_f = sem("s_f")
        s_f_out = sem("s_f_out")
        s_adj3 = [sem(f"s_adj3{b}") for b in range(2)]
        s_bias3 = sem("s_bias3")
        s_logit = sem("s_logit")
        s_l3 = sem("s_l3")
        s_neg3 = sem("s_neg3")
        s_exp3 = sem("s_exp3")
        s_T3 = sem("s_T3")
        s_T3_out = sem("s_T3_out")
        s_val = sem("s_val")
        s_val_out = sem("s_val_out")
        s_var3 = sem("s_var3")
        s_std3 = sem("s_std3")
        s_y3 = sem("s_y3")
        s_out = sem("s_out")
        s_dve = sem("s_dve")
        s_act = sem("s_act")

        x_rows = a["x"].rearrange("(t p) d -> p t d", p=P)
        adj_rows = a["adj"].rearrange("(t p) n -> t p n", p=P)
        x1_rows = x1_dram.rearrange("(t p) d -> p t d", p=P)
        W0_BITS = 6
        GROUPS = 2 * T

        TAKER = ["dve" if b % 4 == 3 else "act" for b in range(T)]
        TAKEN = {who: TAKER.count(who) for who in ("act", "dve")}

        def wait_block_taken(eng, g, b):
            who = TAKER[b]
            eng.wait_ge(s_PT[who], TAKEN[who] * g + TAKER[:b + 1].count(who))

        def take_block(eng, copy, g, b, has_before):
            eng.wait_ge(s_T, T * g + b + 1)
            q = b // 4
            if has_before or q >= 2:
                eng.wait_ge(s_pv, 4 * g + q - 1)
            copy(PT[:, q % 2, b % 4, :], ps[:, 4 + b % 2, :]).then_inc(s_PT[TAKER[b]], 1)

        def layer2(eng, slot):
            for gamma in range(4):
                for j in range(4):
                    slot(gamma // 2, gamma, gamma, j, gamma >= 1, gamma >= 2, True, True)
            with eng.Fori(1, T // 2 - 1) as i:
                for gamma in range(4):
                    for j in range(4):
                        slot(2 * i + gamma // 2, 4 * i + gamma, gamma, j, True, True, True, True)
            for gamma in range(4):
                for j in range(4):
                    slot(T - 2 + gamma // 2, GROUPS - 4 + gamma, gamma, j, True, True, True, gamma < 2)
            for j in range(4):
                slot(T, GROUPS, 0, j, True, True, False, False)
            for j in range(3):
                slot(T, GROUPS + 1, 1, j, False, True, False, False)

        block = ctx.enter_context(nc.Block())

        @block.gpsimd
        def _(pool):
            pool.memset(identf[:, :], 0.0).then_inc(s_const, 1)
            pool.memset(identh[:, :], 0.0).then_inc(s_const, 1)
            pool.memset(onesf[:, :], 1.0).then_inc(s_const, 1)
            pool.memset(onesh[:, :], 1.0).then_inc(s_const, 1)
            pool.memset(eps_col[:, :], EPS).then_inc(s_const, 1)
            pool.wait_ge(s_const, 5)
            for m in (identf, identh):
                pool.affine_select(out=m[:, :], in_=m[:, :], compare_op=ALU.not_equal, fill=1.0, base=0,
                                   pattern=[[-1, P]], channel_multiplier=1).then_inc(s_const, 1)
            for c in range(C):
                if c >= 1:
                    pool.wait_ge(s_lin_out, TC * c)
                pool.dma_start(xres[:, :, :], x_rows[:, c * TC:(c + 1) * TC, :]).then_inc(s_xres, 16)
                pool.wait_ge(s_x1, TC * (c + 1))
                pool.dma_start(x1_rows[:, c * TC:(c + 1) * TC, :], y0[:, :, :]).then_inc(s_x1_saved, 16)
            pool.wait_ge(s_x1_saved, 16 * C)
            pool.wait_ge(s_state, 4 + C * STEPS)
            for c in range(C):
                if c >= 2:
                    pool.wait_ge(s_y1, TC * (c - 1) + 1)
                pool.dma_start(x1r[:, c % 2, :, :], x1_rows[:, c * TC:(c + 1) * TC, :]).then_inc(s_x1r[c % 2], 16)

            pool.wait_ge(s_prod, 16 * STEPS)

            def bias_2(t, b, used):
                pool.wait_ge(s_adj2, 16 * t + 16)
                if used:
                    pool.wait_ge(s_neg, 8 * t - 8)
                pool.sem_inc(s_passed["pool"], 1)
                pool.tensor_scalar(bias2[:, b, :], adj2[:, :], 0.0, -9e15, ALU.is_le, ALU.mult).then_inc(s_bias2, 1)

            bias_2(0, 0, False)
            bias_2(1, 1, False)
            with pool.Fori(1, T // 2) as i:
                for b in range(2):
                    bias_2(2 * i + b, b, True)

            def bias_3(t, k, b, used):
                pool.wait_ge(s_adj3[b], 16 * k + 16)
                if used:
                    pool.wait_ge(s_neg3, t - 1)
                pool.sem_inc(s_passed["pool"], 1)
                pool.tensor_scalar(bias3[:, b, :], adj3[:, b, :], 0.0, -1e9, ALU.is_le, ALU.mult).then_inc(s_bias3, 1)

            bias_3(0, 0, 0, False)
            bias_3(1, 0, 1, False)
            with pool.Fori(1, T // 2) as i:
                for b in range(2):
                    bias_3(2 * i + b, i, b, True)

        @block.sync
        def _(sp):
            sp.dma_start(x32[:, :, :], x_rows).then_inc(s_x, 16)
            sp.dma_start(w_raw[:, 0:2, :], a["L0_gnn_W_self"].rearrange("(k p) d -> p k d", p=P)).then_inc(s_w0, 16)
            sp.dma_start(w_raw[:, 2:4, :], a["L0_gnn_W_nb"].rearrange("(k p) d -> p k d", p=P)).then_inc(s_w0, 16)
            sp.dma_start(w_raw[:, 4:8, :], a["L0_gnn_W_comb"].rearrange("(k p) d -> p k d", p=P)).then_inc(s_w0, 16)
            sp.dma_start(bcol0[:, 0:2], a["L0_gnn_b_self"].rearrange("(k p) -> p k", p=P), allow_slow_non_contiguous=True).then_inc(s_w0, 16)
            sp.dma_start(bcol0[:, 2:4], a["L0_gnn_b_nb"].rearrange("(k p) -> p k", p=P), allow_slow_non_contiguous=True).then_inc(s_w0, 16)
            sp.dma_start(bcomb[:, :], a["L0_gnn_b_comb"].rearrange("(a d) -> a d", a=1)).then_inc(s_w0, 16)
            for t in range(T):
                if t >= 2:
                    sp.wait_ge(s_cast, t - 1)
                sp.dma_start(stage[:, t % 2, :], adj_rows[t]).then_inc(s_adj[t % 2], 16)

            sp.wait_ge(s_xb, 1)
            sp.wait_ge(s_xt, 2 * C)
            for k, name in enumerate(("in", "out")):
                sp.dma_start(ioW[:, 2 * k:2 * k + 2, :],
                             a[f"L1_gnn_{name}_W"].rearrange("(k p) d -> p k d", p=P)).then_inc(s_w1, 16)
            for k, name in enumerate(("r", "z", "h")):
                sp.dma_start(graw[:, k, :, :], a[f"L1_gnn_{name}_W"].rearrange("(k p) d -> p k d", p=P))\
                    .then_inc(s_w1, 16)
            sp.wait_ge(s_x1_saved, 16 * C)
            sp.wait_ge(s_x1t_out, FT * C)
            for k, name in enumerate(("in", "out")):
                sp.dma_start(bcol1[:, 2 * k:2 * k + 2], a[f"L1_gnn_{name}_b"].rearrange("(k p) -> p k", p=P),
                             allow_slow_non_contiguous=True).then_inc(s_b1, 16)
            for k, name in enumerate(("r", "z", "h")):
                sp.dma_start(gb[:, 2 * k:2 * k + 2], a[f"L1_gnn_{name}_b"].rearrange("(k p) -> p k", p=P),
                             allow_slow_non_contiguous=True).then_inc(s_b1, 16)
            sp.wait_ge(s_state, 4 + C * STEPS)
            for k in range(2):
                sp.dma_start(oraw[:, 2 * k:2 * k + 2, :],
                             a[f"L1_gnn_o{k + 1}_W"].rearrange("(k p) d -> p k d", p=P)).then_inc(s_ow, 16)
            sp.dma_start(o1col[:, :], a["L1_gnn_o1_b"].rearrange("(k p) -> p k", p=P),
                         allow_slow_non_contiguous=True).then_inc(s_ow, 16)
            sp.dma_start(o2b[:, :], a["L1_gnn_o2_b"].rearrange("(a d) -> a d", a=1)).then_inc(s_ow, 16)

            def load_adj2(t, used):
                if used:
                    sp.wait_ge(s_bias2, t)
                sp.dma_start(adj2[:, :], adj_rows[t]).then_inc(s_adj2, 16)

            load_adj2(0, False)
            for t in range(T):
                if t >= 2:
                    sp.wait_ge(s_klo, 2 * (t - 1))
                sp.dma_start(kin[:, t % 2, :], a["L2_gnn_x2"][t * P:(t + 1) * P, :]).then_inc(s_kin[t % 2], 16)
            sp.dma_start(v_sb[:, :, :], a["L2_gnn_v"].rearrange("(t p) d -> p t d", p=P)).then_inc(s_v, 16)
            for t in range(1, T):
                load_adj2(t, True)

            sp.wait_ge(s_var2, 1)
            sp.wait_ge(s_bias2, T)
            for b in range(2):
                sp.dma_start(adj3[:, b, :], adj_rows[b]).then_inc(s_adj3[b], 16)
            sp.dma_start(W1[:, :], a["L3_gnn_W1"]).then_inc(s_w3, 16)
            for k in range(2):
                sp.dma_start(w23[:, k:k + 1], a[f"L3_gnn_w{k + 2}"].rearrange("(p a) -> p a", a=1)).then_inc(s_w3, 16)
                sp.dma_start(b23[:, k:k + 1], a[f"L3_gnn_b{k + 2}"].rearrange("(p a) -> p a", a=1)).then_inc(s_w3, 16)
            for t in range(2, T):
                sp.wait_ge(s_bias3, t - 1)
                sp.wait_ge(s_logit, t - 1)
                sp.dma_start(adj3[:, t % 2, :], adj_rows[t]).then_inc(s_adj3[t % 2], 16)
            for c in range(C):
                sp.wait_ge(s_y3, TC * (c + 1))
                sp.dma_start(out.rearrange("(t p) d -> p t d", p=P)[:, c * TC:(c + 1) * TC, :],
                             y3[:, c * TC:(c + 1) * TC, :]).then_inc(s_out, 16)
            sp.wait_ge(s_out, 16 * C)

        @block.scalar
        def _(act):
            def copy(dst, src, **kw):
                return act.activation(dst, src, ACT.Copy, **kw)

            act.wait_ge(s_w0t, 1)
            copy(w_tr[:, 0:2, :], ps[:, 4, :]).then_inc(s_w0t_out, 1)
            act.wait_ge(s_w0t, 2)
            copy(w_tr[:, 2:4, :], ps[:, 5, :]).then_inc(s_w0t_out, 1)
            for k in range(2):
                act.wait_ge(s_w0c, k + 1)
                copy(W0[:, 2 * k:2 * k + 2, :], ps[:, k, :]).then_inc(s_w0c_out, 1)
            act.wait_ge(s_w0c, 3)
            copy(bias0[:, :], ps[:, 2, 0:D]).then_inc(s_w0c_out, 1)
            for n in range(2 * C):
                f, c = n // C, n % C
                act.wait_ge(s_xt, n + 1)
                copy(xT[:, f, c * CH:(c + 1) * CH], ps[:, 4 + n % 2, :]).then_inc(s_xt_out, 1)

            def tadj_out(t):
                for h in range(2):
                    act.wait_ge(s_tadj, 2 * t + h + 1)
                    copy(At8[:, 8 * h:8 * h + 8, t * P:(t + 1) * P],
                         ps[:, 6 + h, :].bitcast(F16).rearrange("p (b n) -> p b n", n=P),
                         saturate=False).then_inc(s_tadj_out, 1)

            def x1t_out(c):
                for f in range(FT):
                    act.wait_ge(s_x1t, FT * c + f + 1)
                    copy(xT[:, f, c * CH:(c + 1) * CH], ps[:, 4 + f, :]).then_inc(s_x1t_out, 1)

            for t in range(TC):
                tadj_out(t)
            for c in range(C):
                if c + 1 < C:
                    for t in range(TC * (c + 1), TC * (c + 2)):
                        tadj_out(t)
                act.wait_ge(s_var0, c + 1)
                act.activation(rstd[:, c * TC:(c + 1) * TC], mv[:, c * TC:(c + 1) * TC, 1], ACT.Sqrt,
                               bias=eps_col[:, 0:1]).then_inc(s_std0, 1)
                x1t_out(c)

            act.wait_ge(s_deg, 1)
            for c in range(C):
                copy(dsum[:, c * CH:(c + 1) * CH], ps[32 * c:32 * c + 8, 0, :]).then_inc(s_deg_out, 1)
            for n in range(9):
                g, kk = n // 3, n % 3
                act.wait_ge(s_gt, n + 1)
                dst = (RT[:, 2 * kk:2 * kk + 2, g * D:(g + 1) * D] if kk < 2 else Wg[:, 0, 4:6, g * D:(g + 1) * D])
                copy(dst, ps[:, 4 + n % 2, :].rearrange("p (k n) -> p k n", k=2)).then_inc(s_gt_out, 1)
            for n in range(4):
                act.wait_ge(s_wg, n + 1)
                copy(Wg[:, 0, n, :], ps[:, 2 * (n % 2):2 * (n % 2) + 2, :].rearrange("p a b -> p (a b)")[:, 0:gates])\
                    .then_inc(s_wg_out, 1)

            with act.Fori(0, STEPS) as i:
                for p in range(T // 2):
                    act.wait_ge(s_turn, 8 * i + p + 1)
                    act.activation(rows16[:, 2 * p:2 * p + 2, 0, :],
                                   ps[:, TURN[p], :].rearrange("p (t n) -> p t n", t=2), ACT.Copy,
                                   scale=2048.0).then_inc(s_hi, 1)
                for c in range(C):
                    act.wait_ge(s_state, 4 * i + 4 + c)
                    copy(SX[:, 0, :, :], xT[:, :, c * CH:(c + 1) * CH]).then_inc(s_shi, 1)
                    for g in range(2 * FT):
                        act.wait_ge(s_prod, 16 * i + 4 * c + g + 1)
                        act.activation(U[:, 0, g, :], ps[:, g, :], ACT.Copy, scale=1.0 / 2048).then_inc(s_U, 1)
                    for j in range(2 * FT):
                        act.wait_ge(s_gate, 24 * i + 6 * c + j + 1)
                        act.activation(gz[:, j, :], ps[:, 4 + j, :], ACT.Sigmoid, bias=gb[:, j:j + 1])\
                            .then_inc(s_r if j < 2 else s_z, 1)
                        if j == 1:
                            act.wait_ge(s_rs, 8 * i + 2 * c + 1)
                            copy(RX[:, 0, :, :], gz[:, 0:2, :]).then_inc(s_rhi, 1)
                    act.wait_ge(s_gate, 24 * i + 6 * c + 6)
                    for f in range(FT):
                        act.activation(gz[:, f, :], ps[:, 4 + f, :], ACT.Tanh, bias=gb[:, 4 + f:5 + f]).then_inc(s_h, 1)

            for k in range(2):
                act.wait_ge(s_ot, k + 1)
                copy(oT[:, 2 * k:2 * k + 2, :], ps[:, k, :].rearrange("p (k n) -> p k n", k=2)).then_inc(s_ot_out, 1)
            act.wait_ge(s_ot, 3)
            copy(bias1[:, :], ps[:, 2, 0:D]).then_inc(s_ot_out, 1)
            for c in range(C):
                if c >= 1:
                    act.wait_ge(s_o2, TC * c)
                for g in range(FT):
                    act.wait_ge(s_o1, FT * c + g + 1)
                    act.activation(TT[:, g, :], ps[:, 4 + g, :], ACT.Tanh, bias=o1col[:, g:g + 1]).then_inc(s_o1_out, 1)
            act.wait_ge(s_var1, 1)
            act.activation(rstd[:, :], mv[:, :, 1], ACT.Sqrt, bias=eps_col[:, 0:1]).then_inc(s_std1, 1)

            for t in range(T):
                b = t % 2
                act.wait_ge(s_kin[b], 16 * (t // 2 + 1))
                if t >= 2:
                    act.wait_ge(s_kt, 2 * (t - 1))
                for r in (0, 2):
                    copy(kstk[:, b, :, r, :], kin[:, b, :].rearrange("p (h d) -> p h d", h=HEADS)).then_inc(s_khi, 1)
                act.wait_ge(s_kt, 2 * t + 1)
                copy(kst[:, 0:4, t * P:(t + 1) * P], ps[:, 4, :].rearrange("p (h n) -> p h n", h=4))\
                    .then_inc(s_kout[0], 1)

            SCALE = float(HD) ** -0.5

            def q_hi(t):
                for r in (0, 1):
                    act.activation(qstk[:, :, r, :], xr[:, t, :].rearrange("p (h d) -> p h d", h=HEADS), ACT.Copy,
                                   scale=SCALE).then_inc(s_qhi, 1)

            def q_out(t, b):
                act.wait_ge(s_qT, 2 * t + 1)
                copy(qst[:, b, 0:4, :], ps[:, 7, :].rearrange("p (h n) -> p h n", h=4)).then_inc(s_qout[0], 1)

            act.wait_ge(s_x2, T)
            q_hi(0)
            q_out(0, 0)

            def slot(t, g, gamma, j, has1, has2, front, more):
                hh, n = gamma % 2, 4 * g + j
                ring = 4 * gamma + j
                if has2 and j == 1:
                    act.wait_ge(s_pv, 4 * g - 4)
                    copy(oT2[:, :], ps[:, 6, 0:P]).then_inc(s_o, 1)
                if more and hh == 1 and j == 0:
                    q_hi(t + 1)
                if more and hh == 1 and j == 3:
                    q_out(t + 1, (gamma // 2 + 1) % 2)
                if has1:
                    for b in range(4 * j, 4 * j + 4):
                        if TAKER[b] == "act":
                            take_block(act, copy, g - 1, b, has2)
                if front:
                    act.wait_ge(s_neg, n + 1)
                    act.activation(prob[:, 4 * hh + j, :], prob[:, 4 * hh + j, :], ACT.Exp, bias=neg2[:, ring:ring + 1],
                                   accum_out=rsum2[:, ring:ring + 1]).then_inc(s_exp, 1)

            layer2(act, slot)
            act.wait_ge(s_var2, 1)
            act.activation(rstd[:, :], mv[:, :, 1], ACT.Sqrt, bias=eps_col[:, 0:1]).then_inc(s_std2, 1)

            act.wait_ge(s_u, 1)
            copy(u23[:, :, :], ps[:, 0, 0:4].rearrange("p (f k) -> p f k", f=FT)).then_inc(s_u_out, 1)
            copy(bc23[:, :], ps[:, 0, 4:6]).then_inc(s_u_out, 1)
            act.wait_ge(s_u_out, 2)
            for n in range(FT * C):
                f, c = n % FT, n // FT
                act.wait_ge(s_x3t, n + 1)
                copy(x3T[:, f, c * CH:(c + 1) * CH], ps[:, 4 + n % 2, :]).then_inc(s_x3t_out, 1)
            for c in range(C):
                act.wait_ge(s_f, c + 2)
                act.activation(f2[:, c * CH:(c + 1) * CH], ps[:, 2 + c % 2, :], ACT.Identity, bias=bc23[:, 1:2])\
                    .then_inc(s_f_out, 1)

            def tile3(t, b, first):
                act.wait_ge(s_neg3, t + 1)
                act.activation(coef[:, b, :], coef[:, b, :], ACT.Exp, bias=neg3[:, b:b + 1],
                               accum_out=rsum3[:, b:b + 1]).then_inc(s_exp3, 1)
                for c in range(C):
                    act.wait_ge(s_T3, C * t + c + 1)
                    copy(coefT[:, b, c * CH:(c + 1) * CH], ps[:, 2 + c, :]).then_inc(s_T3_out, 1)

            with act.Fori(0, T // 2) as i:
                for b in range(2):
                    tile3(2 * i + b, b, False)
            act.wait_ge(s_var3, 1)
            act.activation(rstd[:, :], mv[:, :, 1], ACT.Sqrt, bias=eps_col[:, 0:1]).then_inc(s_std3, 1)

        @block.tensor
        def _(pe):
            pe.wait_ge(s_const, 7)
            pe.wait_ge(s_w0, 16 * W0_BITS)
            for k in range(2):
                for i in range(2):
                    for j in range(2):
                        mm = pe.transpose(ps[:, 4 + k, j * D + i * P:j * D + (i + 1) * P],
                                          w_raw[:, 2 * k + i, j * P:(j + 1) * P], identf[:, :])
                mm.then_inc(s_w0t, 1)
            for k in range(2):
                pe.wait_ge(s_w0t_out, k + 1)
                for i in range(2):
                    for j in range(2):
                        mm = pe.matmul(ps[:, k, i * D:(i + 1) * D], w_tr[:, 2 * k + j, i * P:(i + 1) * P],
                                       w_raw[:, 4 + 2 * k + j, :], start=(j == 0), stop=(j == 1))
                mm.then_inc(s_w0c, 1)
            pe.wait_ge(s_bstat, 1)
            for j in range(4):
                pe.matmul(ps[:, 2, 0:D], bstat[:, j, :], w_raw[:, 4 + j, :], start=(j == 0), stop=False)
            pe.matmul(ps[:, 2, 0:D], onesf[0:1, :], bcomb[:, :], start=False, stop=True).then_inc(s_w0c, 1)
            pe.wait_ge(s_x, 16)
            for n in range(2 * C):
                f, c = n // C, n % C
                if n < 2:
                    pe.wait_ge(s_w0t_out, n + 1)
                else:
                    pe.wait_ge(s_xt_out, n - 1)
                for q in range(TC):
                    mm = pe.transpose(ps[:, 4 + n % 2, q * P:(q + 1) * P],
                                      x32[:, c * TC + q, f * P:(f + 1) * P], identf[:, :])
                mm.then_inc(s_xt, 1)

            def transpose_adj(t):
                pe.wait_ge(s_cast, t + 1)
                for h in range(2):
                    if t >= 1:
                        pe.wait_ge(s_tadj_out, 2 * t - 1 + h)
                    bank = ps[:, 6 + h, :].bitcast(F16)
                    for b in range(8):
                        m = 8 * h + b
                        mm = pe.transpose(bank[:, b * P:(b + 1) * P], a16[:, t % TC, m * P:(m + 1) * P], identh[:, :])
                    mm.then_inc(s_tadj, 1)

            def aggregate(c):
                if c == 0:
                    pe.wait_ge(s_xb, 1)
                    pe.wait_ge(s_w0c_out, 3)
                else:
                    pe.wait_ge(s_agg_out, c)
                for m in range(T):
                    pe.wait_ge(s_mask, c * T + m + 1)
                    mask = mk[:, m % RING, :]
                    for f in range(FT):
                        for s in range(3):
                            pe.matmul(ps[:, f, :], xb[:, m, s, f * P:(f + 1) * P], mask,
                                      start=(m == 0 and s == 0), stop=(m == T - 1 and s == 2))
                    if m == 0 and c >= 1:
                        pe.wait_ge(s_lin_out, TC * c - 1)
                    pe.matmul(ps[:, 2, :], onesh[:, :], mask, start=(m == 0), stop=(m == T - 1)).then_inc(s_agg_m, 1)

            def linear(c):
                pe.wait_ge(s_agg_out, c + 1)
                if c == 0:
                    pe.wait_ge(s_xt_out, 2 * C)
                for q in range(TC):
                    n = c * TC + q
                    if n >= 2:
                        pe.wait_ge(s_lin_out, n - 1)
                    o = ps[:, 2 + q % 2, 0:D]
                    for f in range(FT):
                        pe.matmul(o, xT[:, f, n * P:(n + 1) * P], W0[:, f, :], start=(f == 0), stop=False)
                    for f in range(FT):
                        mm = pe.matmul(o, aggT[:, f, q * P:(q + 1) * P], W0[:, FT + f, :], start=False,
                                       stop=(f == FT - 1))
                    mm.then_inc(s_lin, 1)

            def transpose_x1(c):
                pe.wait_ge(s_x1, TC * (c + 1))
                for f in range(FT):
                    if c >= 1:
                        pe.wait_ge(s_x1t_out, FT * (c - 1) + f + 1)
                    for q in range(TC):
                        mm = pe.transpose(ps[:, 4 + f, q * P:(q + 1) * P], y0[:, q, f * P:(f + 1) * P], identf[:, :])
                    mm.then_inc(s_x1t, 1)

            for t in range(TC):
                transpose_adj(t)
            for c in range(C):
                aggregate(c)
                if c >= 1:
                    transpose_x1(c - 1)
                if c + 1 < C:
                    for t in range(TC * (c + 1), TC * (c + 2)):
                        transpose_adj(t)
                linear(c)
            transpose_x1(C - 1)

            pe.wait_ge(s_sel, 1)
            pe.wait_ge(s_lin_out, N // P)
            for m in range(T):
                for c in range(C):
                    pe.matmul(ps[32 * c:32 * c + 8, 0, :], sel[:, 0, :], At8[:, m, c * CH:(c + 1) * CH],
                              start=(m == 0), stop=False, tile_position=(0, 32 * c))
            for m in range(T):
                for c in range(C):
                    mm = pe.matmul(ps[32 * c:32 * c + 8, 0, :], sel[:, 1, :], A8[:, m, c * CH:(c + 1) * CH],
                                   start=False, stop=(m == T - 1), tile_position=(0, 32 * c))
            mm.then_inc(s_deg, 1)
            pe.wait_ge(s_x1t_out, FT * C)
            for n in range(9):
                g, kk = n // 3, n % 3
                if n == 0:
                    pe.wait_ge(s_w1, 16 * 5)
                if n >= 2:
                    pe.wait_ge(s_gt_out, n - 1)
                    if (n - 2) % 3 == 2:
                        pe.wait_ge(s_gt_lo, (n - 2) // 3 + 1)
                for k in range(2):
                    for j in range(2):
                        mm = pe.transpose(ps[:, 4 + n % 2, k * D + j * P:k * D + (j + 1) * P],
                                          graw[:, g, j, (2 * kk + k) * P:(2 * kk + k + 1) * P], identf[:, :])
                mm.then_inc(s_gt, 1)
            pe.wait_ge(s_gt_out, 9)
            pe.wait_ge(s_gt_lo, 3)
            pe.wait_ge(s_deg_out, C)
            for n in range(4):
                io, i = n // 2, n % 2
                if n >= 2:
                    pe.wait_ge(s_wlo, n - 1)
                for lo, hi, bank in ((0, 512, 0), (512, gates, 1)):
                    for j in range(2):
                        mm = pe.matmul(ps[:, 2 * (n % 2) + bank, 0:hi - lo], ioW[:, 2 * io + j, i * P:(i + 1) * P],
                                       RT[:, 2 * io + j, lo:hi], start=(j == 0), stop=(j == 1))
                mm.then_inc(s_wg, 1)
            pe.wait_ge(s_sel, 2)
            for lo, hi, bank in ((0, 512, 6), (512, gates, 7)):
                for j in range(4):
                    mm = pe.matmul(ps[0:8, bank, 0:hi - lo], bst1[:, j, :], RT[:, j, lo:hi], start=(j == 0), stop=(j == 3))
            mm.then_inc(s_dwp, 1)
            pe.wait_ge(s_wlo, 4)
            pe.wait_ge(s_dwp_out, 1)
            pe.wait_ge(s_drows, 1)

            def turn(i, p):
                pe.wait_ge(s_state, 4 * i + p // 2 + 1)
                if p in (5, 6):
                    pe.wait_ge(s_rows, 8 * i + p - 4)
                for t in range(2):
                    for f in range(FT):
                        n = 2 * p + t
                        mm = pe.transpose(ps[:, TURN[p], t * D + f * P:t * D + (f + 1) * P],
                                          xT[:, f, n * P:(n + 1) * P], identf[:, :])
                mm.then_inc(s_turn, 1)

            with pe.Fori(0, STEPS) as i:
                pe.wait_ge(s_z, 8 * i + 8)
                for p in range(4):
                    turn(i, p)
                for c in range(C):
                    moving = [At8, At8, A8, A8]
                    for g in range(2 * FT):
                        f = g % 2
                        if c == 0 and g == 1:
                            pe.wait_ge(s_rows, 8 * i + 8)
                            pe.sem_inc(s_passed["pe"], 1)
                        if c >= 1:
                            pe.wait_ge(s_Ulo, 16 * i + 4 * (c - 1) + g + 1)
                            pe.sem_inc(s_passed["pe"], 1)
                        for m in range(T):
                            if c == 0 and g == 0 and m % 2 == 0:
                                if m >= 2 and m // 2 + 3 < 8:
                                    turn(i, m // 2 + 3)
                                pe.wait_ge(s_rows, 8 * i + m // 2 + 1)
                                pe.sem_inc(s_passed["pe"], 1)
                            for s in range(2):
                                mm = pe.matmul(ps[:, g, :], rows16[:, m, s, f * P:(f + 1) * P],
                                               moving[g][:, m, c * CH:(c + 1) * CH], start=(m == 0 and s == 0),
                                               stop=(m == T - 1 and s == 1))
                        mm.then_inc(s_prod, 1)
                    cols = slice(c * CH, (c + 1) * CH)

                    def gate(j):
                        o, w = ps[:, 4 + j % 4, :], slice(j * P, (j + 1) * P)
                        pe.matmul(o, dw[:, w], drows[:, cols], start=True, stop=False)

                        def three(k, src, f, last=False):
                            for wp, xp in ((0, 0), (0, 1), (1, 0)):
                                mm = pe.matmul(o, Wg[:, wp, k, w], src[:, xp, f, :], start=False,
                                               stop=(last and wp == 1))
                            return mm

                        if j == 0:
                            pe.wait_ge(s_slo, 4 * i + c + 1)
                        if j < 4:
                            for f in range(FT):
                                three(4 + f, SX, f)
                        for g in range(2 * FT):
                            if j == 0:
                                pe.wait_ge(s_Ulo, 16 * i + 4 * c + g + 1)
                            mm = three(g, U, g, j < 4 and g == 3)
                        if j >= 4:
                            pe.wait_ge(s_rs, 8 * i + 2 * c + 2)
                            for f in range(FT):
                                mm = three(4 + f, RX, f, f == 1)
                        mm.then_inc(s_gate, 1)

                    if c >= 1:
                        pe.wait_ge(s_h, 8 * i + 2 * c)
                        pe.wait_ge(s_z, 8 * i + 8 + 2 * c)
                    for j in range(4):
                        gate(j)
                    pe.wait_ge(s_r, 8 * i + 2 * c + 2)
                    for j in range(4, 6):
                        gate(j)

            pe.wait_ge(s_state, 4 + C * STEPS)
            pe.wait_ge(s_ow, 16 * 4)
            for k in range(2):
                for j in range(2):
                    for i in range(2):
                        mm = pe.transpose(ps[:, k, j * D + i * P:j * D + (i + 1) * P],
                                          oraw[:, 2 * k + i, j * P:(j + 1) * P], identf[:, :])
                mm.then_inc(s_ot, 1)
            pe.matmul(ps[:, 2, 0:D], onesf[0:1, :], o2b[:, :], start=True, stop=True).then_inc(s_ot, 1)
            pe.wait_ge(s_ot_out, 2)
            for c in range(C):
                for g in range(FT):
                    if c >= 1:
                        pe.wait_ge(s_o1_out, FT * (c - 1) + g + 1)
                    for k in range(FT):
                        mm = pe.matmul(ps[:, 4 + g, :], oT[:, k, g * P:(g + 1) * P], xT[:, k, c * CH:(c + 1) * CH],
                                       start=(k == 0), stop=(k == 1))
                    mm.then_inc(s_o1, 1)
                pe.wait_ge(s_o1_out, FT * (c + 1))
                for q in range(TC):
                    n = c * TC + q
                    if n >= 2:
                        pe.wait_ge(s_y1, n - 1)
                    for k in range(FT):
                        mm = pe.matmul(ps[:, 6 + q % 2, 0:D], TT[:, k, q * P:(q + 1) * P], oT[:, 2 + k, :],
                                       start=(k == 0), stop=(k == 1))
                    mm.then_inc(s_o2, 1)

            for t in range(T):
                pe.wait_ge(s_klo, 2 * t + 2)
                for hh in range(2):
                    if t >= 1:
                        pe.wait_ge(s_kout[hh], t)
                    for h in range(4):
                        mm = pe.transpose(ps[:, 4 + hh, h * P:(h + 1) * P],
                                          kstk[:, t % 2, 4 * hh + h, :, :].bitcast(F32).rearrange("p a b -> p (a b)"),
                                          identf[:, :])
                    mm.then_inc(s_kt, 1)

            def turn_q(t, hh):
                if hh == 0:
                    pe.wait_ge(s_qlo, 2 * t + 2)
                else:
                    pe.wait_ge(s_qout[0], t + 1)
                for h in range(4):
                    mm = pe.transpose(ps[:, 7, h * P:(h + 1) * P],
                                      qstk[:, 4 * hh + h, :, :].bitcast(F32).rearrange("p a b -> p (a b)"),
                                      identf[:, :])
                mm.then_inc(s_qT, 1)

            turn_q(0, 0)
            turn_q(0, 1)
            for hh in range(2):
                pe.wait_ge(s_kout[hh], T)
            pe.wait_ge(s_v, 16)

            def products(g, q):
                hh = q[1]
                for who in ("act", "dve"):
                    wait_block_taken(pe, g, max(b for b in range(4 * q[0] + 4) if TAKER[b] == who))
                for b in range(4 * q[0], 4 * q[0] + 4):
                    for h in range(4):
                        col = (4 * hh + h) * HD
                        mm = pe.matmul(ps[h * HD:(h + 1) * HD, 6, 0:P], v_sb[:, b, col:col + HD],
                                       PT[:, q[0] % 2, b % 4, h * P:(h + 1) * P], start=(b == 0), stop=(b == T - 1),
                                       tile_position=(0, h * HD))
                mm.then_inc(s_pv, 1)

            def scores(t, g, gamma, j, u, first):
                h = 4 * (gamma % 2) + j
                if j == 0 and u == 0:
                    pe.wait_ge(s_qout[gamma % 2], t + 1)
                if not first:
                    pe.wait_ge(s_masked, 2 * (4 * g + j) + u - 1)
                for w in range(2):
                    mm = pe.matmul(ps[:, 2 * u + w, :], qst[:, gamma // 2, h, :],
                                   kst[:, h, (2 * u + w) * CH:(2 * u + w + 1) * CH], start=True, stop=True)
                mm.then_inc(s_score, 1)

            def slot(t, g, gamma, j, has1, has2, front, more):
                hh = gamma % 2
                if j < 3:
                    ahead = (t, g, gamma, j + 1)
                else:
                    ahead = (t + hh, g + 1, (gamma + 1) % 4, 0)
                is_ahead = front and (more or gamma < 3 or j < 3)
                if has1 and j == 0:
                    pe.wait_ge(s_exp, 4 * g)
                for b in range(4 * j, 4 * j + 4):
                    if b % 4 == 2 and is_ahead:
                        scores(*ahead, 0, False)
                    if has1:
                        if b >= 2:
                            wait_block_taken(pe, g - 1, b - 2)
                        elif has2:
                            wait_block_taken(pe, g - 2, b + 14)
                        for h in range(4):
                            mm = pe.transpose(ps[:, 4 + b % 2, h * P:(h + 1) * P],
                                              prob[:, 4 * (1 - hh) + h, b * P:(b + 1) * P], identf[:, :])
                        mm.then_inc(s_T, 1)
                if has2 and j == 1:
                    pe.wait_ge(s_o, g - 1)
                    pe.transpose(ps[:, 7, 0:P], oT2[:, :], identf[:, :]).then_inc(s_oT, 1)
                if j == 0:
                    if has2:
                        products(g - 2, (3, hh))
                elif has1:
                    products(g - 1, (j - 1, 1 - hh))
                if is_ahead:
                    scores(*ahead, 1, False)
                if more and hh == 1 and j >= 2:
                    if j == 2:
                        if has2:
                            pe.wait_ge(s_att, g - 1)
                    turn_q(t + 1, j - 2)

            for u in range(2):
                scores(0, 0, 0, 0, u, True)
            layer2(pe, slot)

            pe.wait_ge(s_w3, 16 * 5)
            for f in range(FT):
                pe.matmul(ps[:, 0, 2 * f:2 * f + 2], W1[:, f * P:(f + 1) * P], w23[:, :], start=True, stop=True)
            pe.matmul(ps[:, 0, 4:6], onesf[0:1, :], b23[:, :], start=True, stop=True).then_inc(s_u, 1)
            for n in range(FT * C):
                f, c = n % FT, n // FT
                pe.wait_ge(s_x3, TC * (c + 1))
                if n >= 2:
                    pe.wait_ge(s_x3t_out, n - 1)
                for q in range(TC):
                    mm = pe.transpose(ps[:, 4 + n % 2, q * P:(q + 1) * P], xr[:, c * TC + q, f * P:(f + 1) * P],
                                      identf[:, :])
                mm.then_inc(s_x3t, 1)
            pe.wait_ge(s_x3t_out, FT * C)
            pe.wait_ge(s_u_out, 3)
            for t in range(T):
                for f in range(FT):
                    mm = pe.matmul(ps[:, 1, t:t + 1], x3T[:, f, t * P:(t + 1) * P], u23[:, f, 0:1], start=(f == 0),
                                   stop=(f == 1))
            mm.then_inc(s_f, 1)
            for c in range(C):
                if c >= 2:
                    pe.wait_ge(s_f_out, c - 1)
                for f in range(FT):
                    mm = pe.matmul(ps[:, 2 + c % 2, :], u3b[:, f, :], x3T[:, f, c * CH:(c + 1) * CH], start=(f == 0),
                                   stop=(f == 1))
                mm.then_inc(s_f, 1)
            pe.wait_ge(s_f_out, C)

            def tile3(t, b, first, used):
                pe.wait_ge(s_exp3, t + 1)
                if used:
                    pe.wait_ge(s_val_out, t - 1)
                for c in range(C + 1):
                    if c < C:
                        if not first:
                            pe.wait_ge(s_T3_out, C * t + c - 3)
                        for q in range(TC):
                            m = c * TC + q
                            mm = pe.transpose(ps[:, 2 + c, q * P:(q + 1) * P], coef[:, b, m * P:(m + 1) * P],
                                              identf[:, :])
                        mm.then_inc(s_T3, 1)
                    if c >= 1:
                        pe.wait_ge(s_T3_out, C * t + c)
                        for m in range((c - 1) * TC, c * TC):
                            mm = pe.matmul(ps[:, 6 + b, 0:D], coefT[:, b, m * P:(m + 1) * P], xr[:, m, :],
                                           start=(m == 0), stop=(m == T - 1))
                mm.then_inc(s_val, 1)

            tile3(0, 0, True, False)
            tile3(1, 1, False, False)
            with pe.Fori(1, T // 2) as i:
                for b in range(2):
                    tile3(2 * i + b, b, False, True)

        @block.vector
        def _(dve):
            steps = [0]

            def link(ins):
                steps[0] += 1
                ins.then_inc(s_dve, 1)
                dve.wait_ge(s_dve, steps[0])

            dve.wait_ge(s_x, 16)
            r = rest[:, :, :]
            link(dve.tensor_copy(xb[:, :, 0, :], x32[:, :, :]))
            link(dve.tensor_tensor(r, x32[:, :, :], xb[:, :, 0, :], ALU.subtract))
            link(dve.tensor_copy(xb[:, :, 1, :], r))
            link(dve.tensor_tensor(r, r, xb[:, :, 1, :], ALU.subtract))
            dve.tensor_copy(xb[:, :, 2, :], r).then_inc(s_xb, 1)
            dve.wait_ge(s_const, 7)
            dve.wait_ge(s_w0, 16 * W0_BITS)
            for j in range(4):
                last = dve.tensor_scalar(bstat[:, j, :], onesf[:, :], bcol0[:, j:j + 1], None, ALU.mult)
            last.then_inc(s_bstat, 1)

            def cast(t):
                dve.wait_ge(s_adj[t % 2], 16 * (t // 2 + 1))
                if t >= TC:
                    dve.wait_ge(s_tadj, 2 * (t - TC + 1))
                    dve.wait_ge(s_cast8, t - TC + 1)
                dve.tensor_copy(a16[:, t % TC, :], stage[:, t % 2, :]).then_inc(s_cast, 1)
                dve.wait_ge(s_cast, t + 1)
                dve.tensor_copy(A8[:, t, :], a16[:, t % TC, :], saturate=False).then_inc(s_cast8, 1)

            def mask(c, m):
                n = c * T + m
                if m == 0:
                    dve.wait_ge(s_tadj_out, 2 * TC * (c + 1))
                if n >= RING:
                    dve.wait_ge(s_agg_m, n - RING + 1)
                dve.tensor_scalar(mk[:, m % RING, :], At8[:, m, c * CH:(c + 1) * CH], 0.0, None, ALU.is_gt).then_inc(s_mask, 1)

            def mean_of_neighbours(c):
                dve.wait_ge(s_agg_m, T * (c + 1))
                if c >= 1:
                    dve.wait_ge(s_lin, TC * c)
                link(dve.tensor_scalar(rdeg[:, :], ps[:, 2, :], 1.0, None, ALU.max))
                link(dve.reciprocal(rdeg[:, :], rdeg[:, :]))
                for f in range(FT):
                    last = dve.tensor_tensor(aggT[:, f, :], ps[:, f, :], rdeg[:, :], ALU.mult)
                last.then_inc(s_agg_out, 1)

            def residual(c):
                dve.wait_ge(s_xres, 16 * (c + 1))
                if c == 0:
                    dve.wait_ge(s_w0c_out, 3)
                else:
                    dve.wait_ge(s_x1_saved, 16 * c)
                    dve.wait_ge(s_x1t, FT * c)
                for q in range(TC):
                    n = c * TC + q
                    dve.wait_ge(s_lin, n + 1)
                    link(dve.tensor_tensor(y0[:, q, :], ps[:, 2 + q % 2, 0:D], bias0[:, :], ALU.add))
                    steps[0] += 1
                    dve.scalar_tensor_tensor(y0[:, q, :], y0[:, q, :], 0.0, xres[:, q, :], ALU.max,
                                             ALU.add).then_inc(s_lin_out, 1)
                    steps[0] -= 1
                    dve.wait_ge(s_lin_out, n + 1)
                    link(dve.bn_stats(stats[:, q, :], y0[:, q, :]))
                    ins = dve.bn_aggr(mv[:, n, :], stats[:, q, :])
                    if q == TC - 1:
                        ins.then_inc(s_var0, 1)
                    else:
                        link(ins)

            def normalise(c):
                dve.wait_ge(s_std0, c + 1)
                r = rstd[:, c * TC:(c + 1) * TC]
                link(dve.reciprocal(r, r))
                for q in range(TC):
                    n = c * TC + q
                    dve.tensor_scalar(y0[:, q, :], y0[:, q, :], mv[:, n, 0:1], rstd[:, n:n + 1], ALU.subtract,
                                      ALU.mult).then_inc(s_x1, 1)

            for t in range(TC):
                cast(t)
            for m in range(RING):
                mask(0, m)
            for c in range(C):
                for m in range(RING, T):
                    mask(c, m)
                    if m % 3 == 0 and m >= 6 and c + 1 < C:
                        cast(TC * (c + 1) + m // 3 - 2)
                mean_of_neighbours(c)
                if c + 1 < C:
                    for m in range(RING):
                        mask(c + 1, m)
                residual(c)
                normalise(c)

            dve.wait_ge(s_x1t_out, FT * C)
            dve.wait_ge(s_x1_saved, 16 * C)
            link(dve.memset(sel[:, :, :], 0.0))
            for k in range(2):
                last = dve.memset(sel[:, k, 4 * k:4 * k + 4], 1.0)
            last.then_inc(s_sel, 1)
            link(dve.memset(bst1[:, :, :], 0.0))
            dve.wait_ge(s_b1, 16 * 5)
            for j in range(4):
                k = j // 2
                last = dve.tensor_scalar(bst1[:, j, 4 * k:4 * k + 4], onesf[:, 0:4], bcol1[:, j:j + 1], None, ALU.mult)
            last.then_inc(s_sel, 1)
            eye = identf[0:8, 0:8]
            halves = eye.rearrange("p (a b) -> p a b", b=4)
            evens = eye.rearrange("p (a b) -> p b a", b=2)
            dve.tensor_reduce(dmask[:, 0:1], halves[:, :, 0:2], AX.XY, ALU.add)
            dve.tensor_reduce(dmask[:, 1:2], halves[:, :, 2:4], AX.XY, ALU.add)
            dve.tensor_reduce(dmask[:, 2:3], evens[:, 0, :], AX.X, ALU.add)
            link(dve.tensor_reduce(dmask[:, 3:4], evens[:, 1, :], AX.X, ALU.add))

            def split_rows(dst, src, masks):
                link(dve.tensor_copy(dst, src))
                link(dve.tensor_tensor(src, src, dst.bitcast(F32), ALU.subtract))
                link(dve.tensor_scalar(src, src, dmask[:, masks + 1:masks + 2], None, ALU.mult))
                return dve.scalar_tensor_tensor(dst, dst.bitcast(F32), dmask[:, masks:masks + 1], src, ALU.mult, ALU.add)

            for n in range(9):
                g, kk = n // 3, n % 3
                if kk == 2:
                    dve.wait_ge(s_gt_out, n + 1)
                    w = slice(g * D, (g + 1) * D)
                    link(dve.tensor_tensor(Wg[:, 1, 4:6, w], ps[:, 4 + n % 2, :].rearrange("p (k n) -> p k n", k=2),
                                           Wg[:, 0, 4:6, w].bitcast(F32), ALU.subtract))
                    dve.sem_inc(s_gt_lo, 1)
            for n in range(4):
                dve.wait_ge(s_wg_out, n + 1)
                dve.tensor_tensor(Wg[:, 1, n, :],
                                  ps[:, 2 * (n % 2):2 * (n % 2) + 2, :].rearrange("p a b -> p (a b)")[:, 0:gates],
                                  Wg[:, 0, n, :].bitcast(F32), ALU.subtract).then_inc(s_wlo, 1)
            dve.wait_ge(s_deg_out, C)
            link(split_rows(drows[:, :], dsum, 0))
            dve.wait_ge(s_dwp, 1)
            link(dve.tensor_copy(dsum[:, 0:gates], ps[0:8, 6:8, :].rearrange("p a b -> p (a b)")[:, 0:gates]))
            split_rows(dw[:, :], dsum[:, 0:gates], 2).then_inc(s_dwp_out, 1)
            dve.wait_ge(s_dwp_out, 1)
            dve.memset(rstd[:, :], 0.0).then_inc(s_drows, 1)
            dve.sem_inc(s_z, 8)
            dve.sem_inc(s_state, 4)

            with dve.Fori(0, STEPS) as i:
                for p in range(T // 2):
                    dve.wait_ge(s_hi, 8 * i + p + 1)
                    dve.scalar_tensor_tensor(rows16[:, 2 * p:2 * p + 2, 1, :],
                                             ps[:, TURN[p], :].rearrange("p (t n) -> p t n", t=2), 2048.0,
                                             rows16[:, 2 * p:2 * p + 2, 0, :], ALU.mult, ALU.subtract).then_inc(s_rows, 1)
                for c in range(C):
                    state = xT[:, :, c * CH:(c + 1) * CH]
                    r, z = gz[:, 0:2, :], gz[:, 2:4, :]
                    dve.wait_ge(s_shi, 4 * i + c + 1)
                    dve.tensor_tensor(SX[:, 1, :, :], state, SX[:, 0, :, :].bitcast(F32), ALU.subtract).then_inc(s_slo, 1)
                    for g in range(2 * FT):
                        dve.wait_ge(s_U, 16 * i + 4 * c + g + 1)
                        dve.scalar_tensor_tensor(U[:, 1, g, :], ps[:, g, :], 1.0 / 2048, U[:, 0, g, :].bitcast(F32),
                                                 ALU.mult, ALU.subtract).then_inc(s_Ulo, 1)
                    dve.wait_ge(s_r, 8 * i + 2 * c + 2)
                    dve.tensor_tensor(r, r, state, ALU.mult).then_inc(s_rs, 1)
                    dve.wait_ge(s_rhi, 4 * i + c + 1)
                    dve.tensor_tensor(RX[:, 1, :, :], r, RX[:, 0, :, :].bitcast(F32), ALU.subtract).then_inc(s_rs, 1)
                    dve.wait_ge(s_h, 8 * i + 2 * c + 2)
                    dve.tensor_tensor(r, r, state, ALU.subtract).then_inc(s_upd, 1)
                    dve.wait_ge(s_upd, 8 * i + 2 * c + 1)
                    dve.wait_ge(s_z, 8 * i + 8 + 2 * c + 2)
                    dve.tensor_tensor(r, r, z, ALU.mult).then_inc(s_upd, 1)
                    dve.wait_ge(s_upd, 8 * i + 2 * c + 2)
                    dve.tensor_tensor(state, state, r, ALU.add).then_inc(s_state, 1)

            dve.wait_ge(s_ot_out, 3)
            for c in range(C):
                dve.wait_ge(s_x1r[c % 2], 16 * (c // 2 + 1))
                for q in range(TC):
                    n = c * TC + q
                    dve.wait_ge(s_o2, n + 1)
                    dve.tensor_tensor(xr[:, n, :], ps[:, 6 + q % 2, 0:D], bias1[:, :], ALU.add).then_inc(s_y1, 1)
                    dve.wait_ge(s_y1, n + 1)
                    link(dve.tensor_tensor(xr[:, n, :], xr[:, n, :], x1r[:, c % 2, q, :], ALU.add))
                    link(dve.bn_stats(stats[:, q, :], xr[:, n, :]))
                    ins = dve.bn_aggr(mv[:, n, :], stats[:, q, :])
                    if n == T - 1:
                        ins.then_inc(s_var1, 1)
                    else:
                        link(ins)
            dve.wait_ge(s_std1, 1)
            link(dve.reciprocal(rstd[:, :], rstd[:, :]))
            for n in range(T):
                dve.tensor_scalar(xr[:, n, :], xr[:, n, :], mv[:, n, 0:1], rstd[:, n:n + 1], ALU.subtract,
                                  ALU.mult).then_inc(s_x2, 1)

            for t in range(T):
                b = t % 2
                for r in (0, 1):
                    dve.wait_ge(s_khi, 2 * t + r + 1)
                    dve.tensor_tensor(kstk[:, b, :, 2 * r + 1, :], kin[:, b, :].rearrange("p (h d) -> p h d", h=HEADS),
                                      kstk[:, b, :, 2 * r, :].bitcast(F32), ALU.subtract).then_inc(s_klo, 1)
                dve.wait_ge(s_kt, 2 * t + 2)
                dve.tensor_copy(kst[:, 4:8, t * P:(t + 1) * P], ps[:, 5, :].rearrange("p (h n) -> p h n", h=4))\
                    .then_inc(s_kout[1], 1)

            SCALE = float(HD) ** -0.5

            def q_lo(t):
                for r in (0, 1):
                    dve.wait_ge(s_qhi, 2 * t + r + 1)
                    dve.scalar_tensor_tensor(qstk[:, :, 2 + r, :], xr[:, t, :].rearrange("p (h d) -> p h d", h=HEADS),
                                             SCALE, qstk[:, :, r, :].bitcast(F32), ALU.mult, ALU.subtract)\
                        .then_inc(s_qlo, 1)

            def q_out(t, b):
                dve.wait_ge(s_qT, 2 * t + 2)
                dve.tensor_copy(qst[:, b, 4:8, :], ps[:, 7, :].rearrange("p (h n) -> p h n", h=4)).then_inc(s_qout[1], 1)

            q_lo(0)
            q_out(0, 0)

            def slot(t, g, gamma, j, has1, has2, front, more):
                hh, n = gamma % 2, 4 * g + j
                ring = 4 * gamma + j
                if has2 and j == 2:
                    old = (gamma + 2) % 4
                    rows = xr[:, t - 1, hh * P:(hh + 1) * P]
                    base = FINISH * (g - 2)
                    dve.wait_ge(s_exp, 4 * g - 4)
                    dve.reciprocal(rinv2[:, :], rsum2[:, 4 * old:4 * old + 4]).then_inc(s_fin2, 1)
                    dve.wait_ge(s_oT, g - 1)
                    dve.wait_ge(s_fin2, base + 1)
                    dve.tensor_tensor(row2[:, hh * P:(hh + 1) * P].rearrange("p (h d) -> p h d", h=4),
                                      ps[:, 7, 0:P].rearrange("p (h d) -> p h d", h=4),
                                      rinv2[:, :].unsqueeze(2).broadcast_to([P, 4, HD]), ALU.mult).then_inc(s_att, 1)
                    dve.wait_ge(s_att, g - 1)
                    dve.tensor_tensor(row2[:, hh * P:(hh + 1) * P], rows, row2[:, hh * P:(hh + 1) * P], ALU.add).then_inc(s_fin2, 1)
                    if hh == 1:
                        dve.wait_ge(s_fin2, base + 2)
                        dve.sem_inc(s_passed["dve"], 1)
                        dve.bn_stats(stats[:, 0, :], row2[:, :]).then_inc(s_stat2, 1)
                        dve.tensor_copy(xr[:, t - 1, :], row2[:, :]).then_inc(s_stat2, 1)
                        dve.wait_ge(s_stat2, 4 * t - 2)
                        dve.sem_inc(s_passed["dve"], 1)
                        dve.bn_aggr(mv1[:, :], stats[:, 0, :]).then_inc(s_stat2, 1)
                        dve.wait_ge(s_stat2, 4 * t - 1)
                        dve.tensor_copy(mv[:, t - 1, :], mv1[:, :]).then_inc(s_stat2, 1)
                if front:
                    if hh == 0 and j == 0:
                        dve.wait_ge(s_bias2, t + 1)
                    if has2:
                        dve.wait_ge(s_T, T * (g - 1))
                    for u in range(2):
                        half = slice(u * 1024, (u + 1) * 1024)
                        dve.wait_ge(s_score, 2 * n + u + 1)
                        dve.sem_inc(s_passed["dve"], 1)
                        dve.tensor_tensor_reduce(prob[:, 4 * hh + j, half],
                                                 ps[:, 2 * u:2 * u + 2, :].rearrange("p a b -> p (a b)"),
                                                 bias2[:, gamma // 2, half], 1.0, NEG_INIT, ALU.add, ALU.max,
                                                 mx2[:, ring, u:u + 1]).then_inc(s_masked, 1)
                    dve.wait_ge(s_masked, 2 * n + 2)
                    dve.tensor_scalar(neg2[:, ring:ring + 1], mx2[:, ring, 0:1], mx2[:, ring, 1:2], -1.0, ALU.max,
                                      ALU.mult).then_inc(s_neg, 1)
                if more and hh == 1 and j == 1:
                    q_lo(t + 1)
                if has1:
                    for b in range(4 * j, 4 * j + 4):
                        if TAKER[b] == "dve":
                            take_block(dve, dve.tensor_copy, g - 1, b, has2)
                if more and hh == 1 and j == 3:
                    q_out(t + 1, (gamma // 2 + 1) % 2)

            layer2(dve, slot)
            dve.wait_ge(s_stat2, 4 * T)
            dve.sem_inc(s_var2, 1)
            dve.wait_ge(s_std2, 1)
            link(dve.reciprocal(rstd[:, :], rstd[:, :]))
            for n in range(T):
                dve.tensor_scalar(xr[:, n, :], xr[:, n, :], mv[:, n, 0:1], rstd[:, n:n + 1], ALU.subtract,
                                  ALU.mult).then_inc(s_x3, 1)

            dve.wait_ge(s_u_out, 2)
            for f in range(FT):
                last = dve.tensor_scalar(u3b[:, f, :], onesf[:, :], u23[:, f, 1:2], None, ALU.mult)
            last.then_inc(s_u_out, 1)
            dve.wait_ge(s_f, 1)
            link(dve.tensor_scalar(f1[:, :], ps[:, 1, 0:T], bc23[:, 0:1], None, ALU.add))
            dve.wait_ge(s_f_out, C)

            def logits3(t, b, k, used):
                w = coef[:, b, :]
                dve.wait_ge(s_adj3[b], 16 * k + 16)
                if used:
                    dve.wait_ge(s_T3, C * (t - 1))
                dve.scalar_tensor_tensor(w, f2[:, :], f1[:, t:t + 1] if isinstance(t, int) else f1[:, bass.ds(t, 1)],
                                         adj3[:, b, :], ALU.add, ALU.mult).then_inc(s_logit, 1)
                dve.wait_ge(s_logit, t + 1)
                dve.scalar_tensor_tensor(w, w, 0.01, w, ALU.mult, ALU.max).then_inc(s_l3, 1)
                dve.wait_ge(s_l3, 2 * t + 1)
                dve.wait_ge(s_bias3, t + 1)
                dve.sem_inc(s_passed["dve"], 1)
                dve.tensor_tensor_reduce(w, w, bias3[:, b, :], 1.0, NEG_INIT, ALU.add, ALU.max, mx3[:, b:b + 1])\
                    .then_inc(s_l3, 1)
                dve.wait_ge(s_l3, 2 * t + 2)
                dve.tensor_scalar(neg3[:, b:b + 1], mx3[:, b:b + 1], -1.0, None, ALU.mult).then_inc(s_neg3, 1)

            def finish3(t, b):
                row = row3[:, b, :]
                base = 6 * t
                dve.wait_ge(s_val, t + 1)
                dve.reciprocal(rinv3[:, b:b + 1], rsum3[:, b:b + 1]).then_inc(s_f3, 1)
                dve.wait_ge(s_f3, base + 1)
                dve.tensor_scalar(row, ps[:, 6 + b, 0:D], rinv3[:, b:b + 1], 0.0, ALU.mult, ALU.max)\
                    .then_inc(s_val_out, 1)
                dve.wait_ge(s_val_out, t + 1)
                dve.tensor_tensor(row, row, xr[:, t, :], ALU.add).then_inc(s_f3, 1)
                dve.wait_ge(s_f3, base + 2)
                dve.sem_inc(s_passed["dve"], 1)
                dve.bn_stats(stats[:, 0, :], row).then_inc(s_f3, 1)
                dve.tensor_copy(y3[:, t, :], row).then_inc(s_f3, 1)
                dve.wait_ge(s_f3, base + 4)
                dve.sem_inc(s_passed["dve"], 1)
                dve.bn_aggr(mv3[:, :], stats[:, 0, :]).then_inc(s_f3, 1)
                dve.wait_ge(s_f3, base + 5)
                dve.tensor_copy(mv[:, t, :], mv3[:, :]).then_inc(s_f3, 1)

            logits3(0, 0, 0, False)
            logits3(1, 1, 0, False)
            finish3(0, 0)
            with dve.Fori(1, T // 2) as i:
                for b in range(2):
                    logits3(2 * i + b, b, i, True)
                    finish3(2 * i + b - 1, 1 - b)
            finish3(T - 1, 1)
            dve.wait_ge(s_f3, 6 * T)
            dve.sem_inc(s_var3, 1)
            dve.wait_ge(s_std3, 1)
            link(dve.reciprocal(rstd[:, :], rstd[:, :]))
            for n in range(T):
                dve.tensor_scalar(y3[:, n, :], y3[:, n, :], mv[:, n, 0:1], rstd[:, n:n + 1], ALU.subtract,
                                  ALU.mult).then_inc(s_y3, 1)


NAMES = ["x", "adj", "L0_gnn_W_self", "L0_gnn_b_self", "L0_gnn_W_nb", "L0_gnn_b_nb", "L0_gnn_W_comb", "L0_gnn_b_comb",
         "L1_gnn_in_W", "L1_gnn_in_b", "L1_gnn_out_W", "L1_gnn_out_b", "L1_gnn_r_W", "L1_gnn_r_b", "L1_gnn_z_W",
         "L1_gnn_z_b", "L1_gnn_h_W", "L1_gnn_h_b", "L1_gnn_o1_W", "L1_gnn_o1_b", "L1_gnn_o2_W", "L1_gnn_o2_b",
         "L2_gnn_x2", "L2_gnn_v", "L3_gnn_W1", "L3_gnn_w2", "L3_gnn_b2", "L3_gnn_w3", "L3_gnn_b3"]


def kernel(**inputs):
    import numpy as _np
    import concourse.bacc as _bacc
    from concourse import mybir as _mybir
    from concourse.bass_utils import run_bass_kernel_spmd as _run

    nc = _bacc.Bacc("TRN2", target_bir_lowering=False, num_devices=1)
    arrays, args = {}, {}
    for name in NAMES:
        v = _np.ascontiguousarray(inputs[name])
        arrays[f"in_{name}_dram"] = v
        args[name] = nc.dram_tensor(f"in_{name}_dram", v.shape, _mybir.dt.from_np(v.dtype), kind="ExternalInput").ap()
    out = nc.dram_tensor("out_0_dram", (N, D), F32, kind="ExternalOutput").ap()
    program(nc, args, out)
    r = _run(nc, [arrays], core_ids=[0])
    return r.results[0]["out_0_dram"]
```

```python
from contextlib import ExitStack

import concourse.bass as bass
from concourse import mybir

P = 128
F32 = mybir.dt.float32
F32R = mybir.dt.float32r
BF16 = mybir.dt.bfloat16
F16 = mybir.dt.float16
I32 = mybir.dt.int32
F8 = mybir.dt.float8e4
ALU = mybir.AluOpType
ACT = mybir.ActivationFunctionType
AX = mybir.AxisListType

N = 2048
D = 256
T = N // P
FT = D // P
CH = 512
C = N // CH
TC = CH // P
STEPS = 5
HEADS = 8
HD = D // HEADS
EPS = 1e-5
NEG_INIT = -3.4e38
RING = 4


def program(nc, a, out):
    ctx = ExitStack()
    with ctx:
        def sem(name):
            return ctx.enter_context(nc.semaphore(name))

        def sb(name, shape, dt, scope=ctx):
            return scope.enter_context(nc.sbuf_tensor(name, shape, dt))

        x1_dram = nc.dram_tensor("x1_rows_scratch", [N, D], F32, kind="Internal").ap()
        ps = ctx.enter_context(nc.psum_tensor("ps", [P, 8, 512], F32))

        identf = sb("identf", [P, P], F32)
        identh = sb("identh", [P, P], F16)
        onesf = sb("onesf", [P, P], F32)
        sel = sb("sel", [P, 2, 8], F16)
        eps_col = sb("eps_col", [P, 1], F32)
        stats = sb("stats", [P, TC, 6], F32)
        EARLY = 3 * TC // 2
        mv = sb("mv", [P, T, 2], F32)
        rstd = sb("rstd", [P, T], F32)

        graph = ExitStack()
        A8 = sb("A8", [P, T, N], F8, graph)
        At8 = sb("At8", [P, T, N], F8, graph)
        xT = sb("xT", [P, FT, N], F32, graph)
        gates = 3 * D

        first = ExitStack()
        x32 = sb("x32", [P, T, D], F32, first)
        first.close()
        raw = ExitStack()
        graw = sb("graw", [P, 3, FT, gates], F32, raw)
        ioW = sb("ioW", [P, 2 * FT, D], F32, raw)
        raw.close()
        fin = ExitStack()
        oraw = sb("oraw", [P, 2 * FT, D], F32, fin)
        oT = sb("oT", [P, 2 * FT, D], F32, fin)
        o2b = sb("o2b", [1, D], F32, fin)
        bias1 = sb("bias1", [P, D], F32, fin)
        o1col = sb("o1col", [P, FT], F32, fin)
        x1r = sb("x1r", [P, 2, TC, D], F32, fin)
        TT = sb("TT", [P, FT, CH], F32, fin)
        fin.close()
        rows16 = sb("rows16", [P, T, 2, D], F16, graph)
        SX = sb("SX", [P, 2, FT, CH], F32R, graph)
        RX = sb("RX", [P, 2, FT, CH], F32R, graph)

        l0 = ExitStack()
        stage = sb("stage", [P, 2, N], I32, l0)
        a16 = sb("a16", [P, TC, N], F16, l0)
        xb = sb("xb", [P, T, 2, D], F32R, l0)
        mk = sb("mk", [P, RING, CH], F32R, l0)
        hits = sb("hits", [P, N], F8, l0)
        rdeg = sb("rdeg", [P, T], F32, l0)
        W0 = sb("W0", [P, 2 * FT, D], F32, l0)
        bias0 = sb("bias0", [P, D], F32, l0)
        bcol0 = sb("bcol0", [P, 2 * FT], F32, l0)
        parts0 = ExitStack()
        w_raw = sb("w_raw", [P, 4 * FT, D], F32, parts0)
        w_tr = sb("w_tr", [P, 2 * FT, D], F32, parts0)
        bstat = sb("bstat", [P, 2 * FT, P], F32, parts0)
        bcomb = sb("bcomb", [1, D], F32, parts0)
        parts0.close()
        aggT = sb("aggT", [P, FT, CH], F32, l0)
        over = sb("over", [P, CH], F32, l0)
        xres = sb("xres", [P, TC, D], F32, l0)
        y0 = sb("y0", [P, TC, D], F32, l0)
        l0.close()

        l1 = ExitStack()
        drows = sb("drows", [8, N], F32R, l1)
        dw = sb("dw", [8, gates], F32R, l1)
        Wg = sb("Wg", [P, 2, 3 * FT, gates], F32R, l1)
        gb = sb("gb", [P, 3 * FT], F32, l1)
        gz = sb("gz", [P, 2 * FT, CH], F32, l1)
        bcol1 = sb("bcol1", [P, 2 * FT], F32, l1)
        bst1 = sb("bst1", [P, 2 * FT, 8], F32, l1)
        dmask = sb("dmask", [8, 4], F32, l1)
        dsum = gz[0:8, :, :].rearrange("p a b -> p (a b)")
        prep = ExitStack()
        RT = sb("RT", [P, 2 * FT, gates], F32, prep)
        prep.close()
        U = sb("U", [P, 2, 2 * FT, CH], F32R, l1)
        l1.close()
        graph.close()

        l2 = ExitStack()
        kst = sb("kst", [P, HEADS, N], F32R, l2)
        PT = sb("PT", [P, 2, 4, CH], F32, l2)
        before = ExitStack()
        place_of_fin = sb("place_of_fin", [P, 4, N], F32, before)
        kin = sb("kin", [P, 2, TC, D], F32, before)
        kstk = sb("kstk", [P, 2, HEADS, 4, HD], F32R, before)
        before.close()
        prob = sb("prob", [P, HEADS, N], F32, l2)
        xr = sb("xr", [P, T, D], F32, l2)
        v_sb = sb("v_sb", [P, T, D], F32, l2)
        adj2 = sb("adj2", [P, N], I32, l2)
        bias2 = sb("bias2", [P, 2, N], BF16, l2)
        qst = sb("qst", [P, 2, HEADS, P], F32R, l2)
        qstk = sb("qstk", [P, HEADS, 4, HD], F32R, l2)
        oT2 = sb("oT2", [P, P], F32, l2)
        mv1 = sb("mv1", [P, 2], F32, l2)
        row2 = sb("row2", [P, D], F32, l2)
        mx2 = sb("mx2", [P, 16, 2], F32, l2)
        neg2 = sb("neg2", [P, 16], F32, l2)
        rsum2 = sb("rsum2", [P, 16], F32, l2)
        rinv2 = sb("rinv2", [P, 4], F32, l2)
        l2.close()

        l3 = ExitStack()
        adj3 = sb("adj3", [P, 2, N], I32, l3)
        bias3 = sb("bias3", [P, 2, N], F32, l3)
        coef = sb("coef", [P, 2, N], F32, l3)
        coefT = sb("coefT", [P, 2, N], F32, l3)
        y3 = sb("y3", [P, T, D], F32, l3)
        f2 = sb("f2", [P, N], F32, l3)
        f1 = sb("f1", [P, T], F32, l3)
        W1 = sb("W1", [P, D], F32, l3)
        w23 = sb("w23", [P, 2], F32, l3)
        b23 = sb("b23", [1, 2], F32, l3)
        bc23 = sb("bc23", [P, 2], F32, l3)
        wb = sb("wb", [P, 2, P], F32, l3)
        ub = sb("ub", [P, 2, D], F32, l3)
        dot = sb("dot", [P, 2, 2, D], F32, l3)
        f2c = sb("f2c", [P, T], F32, l3)
        mv3 = sb("mv3", [P, 2], F32, l3)
        row3 = sb("row3", [P, 2, D], F32, l3)
        mx3 = sb("mx3", [P, 2], F32, l3)
        neg3 = sb("neg3", [P, 2], F32, l3)
        rsum3 = sb("rsum3", [P, 2], F32, l3)
        rinv3 = sb("rinv3", [P, 2], F32, l3)
        l3.close()

        s_const = sem("s_const")
        s_x = sem("s_x")
        s_w0 = sem("s_w0")
        s_adj = [sem(f"s_adj{b}") for b in range(2)]
        s_xres = sem("s_xres")
        s_xhi = sem("s_xhi")
        s_xb = sem("s_xb")
        s_count = sem("s_count")
        s_rdeg = sem("s_rdeg")
        s_rdegt = sem("s_rdegt")
        s_over = sem("s_over")
        s_bstat = sem("s_bstat")
        s_cast = sem("s_cast")
        s_cast8 = sem("s_cast8")
        s_tadj = sem("s_tadj")
        s_tadj_out = sem("s_tadj_out")
        s_w0t = sem("s_w0t")
        s_w0t_out = sem("s_w0t_out")
        s_w0c = sem("s_w0c")
        s_w0c_out = sem("s_w0c_out")
        s_xt = sem("s_xt")
        s_xt_out = sem("s_xt_out")
        s_mask = sem("s_mask")
        s_agg_m = sem("s_agg_m")
        s_agg_out = sem("s_agg_out")
        s_lin = sem("s_lin")
        s_lin_out = sem("s_lin_out")
        s_var0 = sem("s_var0")
        s_std0 = sem("s_std0")
        s_x1 = sem("s_x1")
        s_x1_saved = sem("s_x1_saved")
        s_x1t = sem("s_x1t")
        s_x1t_out = sem("s_x1t_out")
        s_w1 = sem("s_w1")
        s_b1 = sem("s_b1")
        s_wlo = sem("s_wlo")
        s_gt_lo = sem("s_gt_lo")
        s_Ulo = sem("s_Ulo")
        s_shi = sem("s_shi")
        s_slo = sem("s_slo")
        s_rhi = sem("s_rhi")
        s_deg = sem("s_deg")
        s_deg_out = sem("s_deg_out")
        s_sel = sem("s_sel")
        s_gt = sem("s_gt")
        s_gt_out = sem("s_gt_out")
        s_wg = sem("s_wg")
        s_wg_out = sem("s_wg_out")
        s_dwp = sem("s_dwp")
        s_dwp_out = sem("s_dwp_out")
        s_state = sem("s_state")
        s_turn = sem("s_turn")
        s_hi = sem("s_hi")
        s_rows = sem("s_rows")
        s_prod = sem("s_prod")
        s_U = sem("s_U")
        s_gate = sem("s_gate")
        s_r = sem("s_r")
        s_z = sem("s_z")
        s_rs = sem("s_rs")
        s_h = sem("s_h")
        s_upd = sem("s_upd")
        s_ow = sem("s_ow")
        s_ot = sem("s_ot")
        s_ot_out = sem("s_ot_out")
        s_x1r = [sem(f"s_x1r{b}") for b in range(2)]
        s_o1 = sem("s_o1")
        s_o1_out = sem("s_o1_out")
        s_o2 = sem("s_o2")
        s_x1b = sem("s_x1b")
        s_y1 = sem("s_y1")
        s_stat1 = sem("s_stat1")
        s_var1 = sem("s_var1")
        s_std1 = sem("s_std1")
        s_x2 = sem("s_x2")
        s_kin = [sem(f"s_kin{b}") for b in range(2)]
        s_v = sem("s_v")
        s_passed = {"dve": sem("s_passed_dve"), "pool": sem("s_passed_pool"), "pe": sem("s_passed_pe")}
        s_fin2 = sem("s_fin2")
        s_stat2 = sem("s_stat2")
        s_f3 = sem("s_f3")
        s_inv3 = sem("s_inv3")
        s_khi = sem("s_khi")
        s_klo = sem("s_klo")
        s_kt = sem("s_kt")
        s_kout = sem("s_kout")
        s_adj2 = sem("s_adj2")
        s_bias2 = sem("s_bias2")
        s_qhi = sem("s_qhi")
        s_qlo = sem("s_qlo")
        s_qT = sem("s_qT")
        s_qout = [sem(f"s_qout{b}") for b in range(2)]
        s_score = sem("s_score")
        s_masked = sem("s_masked")
        s_neg = sem("s_neg")
        s_exp = sem("s_exp")
        s_T = sem("s_T")
        s_PT = {"act": sem("s_PT_act"), "dve": sem("s_PT_dve")}
        s_pv = sem("s_pv")
        s_o = sem("s_o")
        s_oT = sem("s_oT")
        s_att = sem("s_att")
        s_var2 = sem("s_var2")
        s_std2 = sem("s_std2")
        s_x3 = sem("s_x3")
        s_w3 = sem("s_w3")
        s_u = sem("s_u")
        s_u_out = sem("s_u_out")
        s_f = sem("s_f")
        s_wb = sem("s_wb")
        s_dot = sem("s_dot")
        s_f_out = sem("s_f_out")
        s_adj3 = [sem(f"s_adj3{b}") for b in range(2)]
        s_bias3 = sem("s_bias3")
        s_logit = sem("s_logit")
        s_l3 = sem("s_l3")
        s_neg3 = sem("s_neg3")
        s_exp3 = sem("s_exp3")
        s_T3 = sem("s_T3")
        s_T3_out = sem("s_T3_out")
        s_val = sem("s_val")
        s_val_out = sem("s_val_out")
        s_var3 = sem("s_var3")
        s_std3 = sem("s_std3")
        s_y3 = sem("s_y3")
        s_out = sem("s_out")
        s_dve = sem("s_dve")

        x_rows = a["x"].rearrange("(t p) d -> p t d", p=P)
        adj_rows = a["adj"].rearrange("(t p) n -> t p n", p=P)
        x1_rows = x1_dram.rearrange("(t p) d -> p t d", p=P)
        CASTS, COUNTS, TURNS, OVER = (4,7,10,13), (6,9,12,15), (6,9,12,15), 11
        GATE_BANKS = (6, 0, 1, 4, 5)
        GROUPS = 2 * T

        TAKER = ["dve" if b in (1, 5, 11, 14, 15) else "act" for b in range(T)]
        TAKEN = {who: TAKER.count(who) for who in ("act", "dve")}

        def wait_block_taken(eng, g, b):
            who = TAKER[b]
            eng.wait_ge(s_PT[who], TAKEN[who] * g + TAKER[:b + 1].count(who))

        RING_BANKS = (4, 5, 7)
        USERS = []
        for hh in range(2):
            for j in range(4):
                USERS += [("p", hh, b) for b in range(4 * j, 4 * j + 4)]
                USERS += [("o", hh, 0)] if j == 1 else []
                USERS += [("q", hh, j - 2)] if hh == 1 and j >= 2 else []
        assert len(USERS) % len(RING_BANKS) == 0

        def bank_of(kind, hh, n):
            return RING_BANKS[USERS.index((kind, hh, n)) % len(RING_BANKS)]

        def wait_bank_free(eng, t, kind, hh, n):
            at = USERS.index((kind, hh, n))
            while True:
                at -= len(RING_BANKS)
                tile = t if at >= 0 else t - 1
                kind, hh, n = USERS[at % len(USERS)]
                if isinstance(tile, int) and tile < 0:
                    return
                first = isinstance(tile, int) and 2 * tile + hh
                if kind == "p" and (first is False or 1 <= first <= GROUPS):
                    return wait_block_taken(eng, 2 * tile + hh - 1, n)
                if kind == "o" and (first is False or first >= 2):
                    return eng.wait_ge(s_att, 2 * tile + hh - 1)
                if kind == "q" and not (isinstance(tile, int) and tile >= T - 1):
                    return eng.wait_ge(s_qout[n], tile + 2)
                assert isinstance(tile, int)

        def take_block(eng, copy, hh, g, b, has_before):
            eng.wait_ge(s_T, T * g + b + 1)
            q = b // 4
            if has_before or q >= 2:
                eng.wait_ge(s_pv, 4 * g + q - 1)
            copy(PT[:, q % 2, b % 4, :], ps[:, bank_of("p", hh, b), :]).then_inc(s_PT[TAKER[b]], 1)

        def k_twice(t):
            return kin[:, (t // TC) % 2, t % TC, :].rearrange("p (h d) -> p h d", h=HEADS).unsqueeze(2)\
                .broadcast_to([P, HEADS, 2, HD])

        def layer2(eng, slot, between):
            for gamma in range(4):
                for j in range(4):
                    slot(gamma // 2, gamma, gamma, j, gamma >= 1, gamma >= 2, True, True)
            with eng.Fori(1, T // 2 - 1) as i:
                for gamma in range(4):
                    for j in range(4):
                        slot(2 * i + gamma // 2, 4 * i + gamma, gamma, j, True, True, True, True)
            for gamma in range(4):
                for j in range(4):
                    slot(T - 2 + gamma // 2, GROUPS - 4 + gamma, gamma, j, True, True, True, gamma < 2)
            for j in range(4):
                between(j)
                slot(T, GROUPS, 0, j, True, True, False, False)
            for j in range(3):
                between(4 + j)
                slot(T, GROUPS + 1, 1, j, False, True, False, False)

        block = ctx.enter_context(nc.Block())

        @block.gpsimd
        def _(pool):
            pool.memset(identf[:, :], 0.0).then_inc(s_const, 1)
            pool.memset(identh[:, :], 0.0).then_inc(s_const, 1)
            pool.memset(onesf[:, :], 1.0).then_inc(s_const, 1)
            pool.memset(eps_col[:, :], EPS).then_inc(s_const, 1)
            pool.memset(sel[:, :, :], 0.0).then_inc(s_const, 1)
            pool.wait_ge(s_const, 5)
            for m in (identf, identh):
                pool.affine_select(out=m[:, :], in_=m[:, :], compare_op=ALU.not_equal, fill=1.0, base=0,
                                   pattern=[[-1, P]], channel_multiplier=1).then_inc(s_const, 1)
            for k in range(2):
                pool.memset(sel[:, k, 4 * k:4 * k + 4], 1.0).then_inc(s_const, 1)
            for c in range(C):
                if c == 0:
                    pool.wait_ge(s_w0c, 3)
                else:
                    pool.wait_ge(s_lin_out, TC * c)
                pool.dma_start(xres[:, :, :], x_rows[:, c * TC:(c + 1) * TC, :]).then_inc(s_xres, 16)
                pool.wait_ge(s_x1, TC * (c + 1))
                pool.dma_start(x1_rows[:, c * TC:(c + 1) * TC, :], y0[:, :, :]).then_inc(s_x1_saved, 16)
            pool.wait_ge(s_x1_saved, 16 * C)
            def x1_bias(c):
                pool.wait_ge(s_ot_out, 3)
                pool.wait_ge(s_x1r[c % 2], 16 * (c // 2 + 1))
                rows = x1r[:, c % 2, :, :]
                pool.tensor_tensor(rows, rows, bias1[:, :].unsqueeze(1).broadcast_to([P, TC, D]), ALU.add)\
                    .then_inc(s_x1b, 1)

            pool.wait_ge(s_prod, 16 * STEPS)
            for c in range(C):
                if c == 1:
                    pool.wait_ge(s_gate, 24 * STEPS)
                if c >= 2:
                    pool.wait_ge(s_y1, TC * (c - 1))
                pool.dma_start(x1r[:, c % 2, :, :], x1_rows[:, c * TC:(c + 1) * TC, :]).then_inc(s_x1r[c % 2], 16)
                if c >= 1:
                    x1_bias(c - 1)
            x1_bias(C - 1)

            def bias_2(t, b, used):
                pool.wait_ge(s_adj2, 16 * t + 16)
                if used:
                    pool.wait_ge(s_neg, 8 * t - 8)
                pool.sem_inc(s_passed["pool"], 1)
                pool.tensor_scalar(bias2[:, b, :], adj2[:, :], 0.0, -9e15, ALU.is_le, ALU.mult).then_inc(s_bias2, 1)

            bias_2(0, 0, False)
            bias_2(1, 1, False)
            with pool.Fori(1, T // 2) as i:
                for b in range(2):
                    bias_2(2 * i + b, b, True)

            def bias_3(t, k, b, used):
                pool.wait_ge(s_adj3[b], 16 * k + 16)
                if used:
                    pool.wait_ge(s_neg3, t - 1)
                pool.sem_inc(s_passed["pool"], 1)
                pool.tensor_scalar(bias3[:, b, :], adj3[:, b, :], 0.0, -1e9, ALU.is_le, ALU.mult).then_inc(s_bias3, 1)

            bias_3(0, 0, 0, False)
            bias_3(1, 0, 1, False)
            with pool.Fori(1, T // 2) as i:
                for b in range(2):
                    bias_3(2 * i + b, i, b, True)

        @block.sync
        def _(sp):
            sp.dma_start(x32[:, :, :], x_rows).then_inc(s_x, 16)
            sp.dma_start(w_raw[:, 0:2, :], a["L0_gnn_W_self"].rearrange("(k p) d -> p k d", p=P)).then_inc(s_w0, 16)
            sp.dma_start(w_raw[:, 2:4, :], a["L0_gnn_W_nb"].rearrange("(k p) d -> p k d", p=P)).then_inc(s_w0, 16)
            sp.dma_start(w_raw[:, 4:8, :], a["L0_gnn_W_comb"].rearrange("(k p) d -> p k d", p=P)).then_inc(s_w0, 16)
            sp.dma_start(bcol0[:, 0:2], a["L0_gnn_b_self"].rearrange("(k p) -> p k", p=P), allow_slow_non_contiguous=True).then_inc(s_w0, 16)
            sp.dma_start(bcol0[:, 2:4], a["L0_gnn_b_nb"].rearrange("(k p) -> p k", p=P), allow_slow_non_contiguous=True).then_inc(s_w0, 16)
            sp.dma_start(bcomb[:, :], a["L0_gnn_b_comb"].rearrange("(a d) -> a d", a=1)).then_inc(s_w0, 16)
            for t in range(T):
                if t >= 2:
                    sp.wait_ge(s_cast, t - 1)
                sp.dma_start(stage[:, t % 2, :], adj_rows[t]).then_inc(s_adj[t % 2], 16)

            sp.wait_ge(s_xb, C)
            sp.wait_ge(s_xt, 2 * C)
            for k, name in enumerate(("in", "out")):
                sp.dma_start(ioW[:, 2 * k:2 * k + 2, :],
                             a[f"L1_gnn_{name}_W"].rearrange("(k p) d -> p k d", p=P)).then_inc(s_w1, 16)
            for k, name in enumerate(("r", "z", "h")):
                sp.dma_start(graw[:, k, :, :], a[f"L1_gnn_{name}_W"].rearrange("(k p) d -> p k d", p=P))\
                    .then_inc(s_w1, 16)
            sp.wait_ge(s_x1_saved, 16 * C)
            sp.wait_ge(s_x1t_out, FT * C)
            for k, name in enumerate(("in", "out")):
                sp.dma_start(bcol1[:, 2 * k:2 * k + 2], a[f"L1_gnn_{name}_b"].rearrange("(k p) -> p k", p=P),
                             allow_slow_non_contiguous=True).then_inc(s_b1, 16)
            for k, name in enumerate(("r", "z", "h")):
                sp.dma_start(gb[:, 2 * k:2 * k + 2], a[f"L1_gnn_{name}_b"].rearrange("(k p) -> p k", p=P),
                             allow_slow_non_contiguous=True).then_inc(s_b1, 16)
            sp.wait_ge(s_prod, 16 * STEPS)
            for k in range(2):
                sp.dma_start(oraw[:, 2 * k:2 * k + 2, :],
                             a[f"L1_gnn_o{k + 1}_W"].rearrange("(k p) d -> p k d", p=P)).then_inc(s_ow, 16)
            sp.dma_start(o1col[:, :], a["L1_gnn_o1_b"].rearrange("(k p) -> p k", p=P),
                         allow_slow_non_contiguous=True).then_inc(s_ow, 16)
            sp.dma_start(o2b[:, :], a["L1_gnn_o2_b"].rearrange("(a d) -> a d", a=1)).then_inc(s_ow, 16)

            def load_adj2(t, used):
                if used:
                    sp.wait_ge(s_bias2, t)
                sp.dma_start(adj2[:, :], adj_rows[t]).then_inc(s_adj2, 16)

            sp.wait_ge(s_gate, 24 * STEPS)
            for c in range(C):
                if c >= 2:
                    sp.wait_ge(s_klo, TC * (c - 1))
                sp.dma_start(kin[:, c % 2, :, :], a["L2_gnn_x2"].rearrange("(t p) d -> p t d", p=P)[:, c * TC:(c + 1) * TC, :])\
                    .then_inc(s_kin[c % 2], 16)
                if c == 1:
                    sp.wait_ge(s_state, 4 + C * STEPS)
                    load_adj2(0, False)
            sp.dma_start(v_sb[:, :, :], a["L2_gnn_v"].rearrange("(t p) d -> p t d", p=P)).then_inc(s_v, 16)
            for t in range(1, T):
                load_adj2(t, True)

            sp.wait_ge(s_score, 2 * HEADS * T)
            for b in range(2):
                sp.dma_start(adj3[:, b, :], adj_rows[b]).then_inc(s_adj3[b], 16)
            sp.wait_ge(s_T, T * (GROUPS - 1))
            sp.dma_start(W1[:, :], a["L3_gnn_W1"]).then_inc(s_w3, 16)
            for k in range(2):
                sp.dma_start(w23[:, k:k + 1], a[f"L3_gnn_w{k + 2}"].rearrange("(p a) -> p a", a=1)).then_inc(s_w3, 16)
                sp.dma_start(b23[:, k:k + 1], a[f"L3_gnn_b{k + 2}"].rearrange("(p a) -> p a", a=1)).then_inc(s_w3, 16)
            for t in range(2, T):
                sp.wait_ge(s_bias3, t - 1)
                sp.wait_ge(s_logit, t - 1)
                sp.dma_start(adj3[:, t % 2, :], adj_rows[t]).then_inc(s_adj3[t % 2], 16)
            parts = [slice(c * TC, min((c + 1) * TC, T - 2)) for c in range(C)] + [slice(T - 2, T)]
            for tiles in parts:
                sp.wait_ge(s_y3, tiles.stop)
                sp.dma_start(out.rearrange("(t p) d -> p t d", p=P)[:, tiles, :], y3[:, tiles, :]).then_inc(s_out, 16)
            sp.wait_ge(s_out, 16 * len(parts))

        @block.scalar
        def _(act):
            def copy(dst, src, **kw):
                return act.activation(dst, src, ACT.Copy, **kw)

            act.wait_ge(s_x, 16)
            for c in range(C):
                copy(xb[:, c * TC:(c + 1) * TC, 0, :], x32[:, c * TC:(c + 1) * TC, :]).then_inc(s_xhi, 1)
            act.wait_ge(s_w0t, 1)
            copy(w_tr[:, 0:2, :], ps[:, 4, :]).then_inc(s_w0t_out, 1)
            act.wait_ge(s_w0t, 2)
            copy(w_tr[:, 2:4, :], ps[:, 5, :]).then_inc(s_w0t_out, 1)
            for k in range(2):
                act.wait_ge(s_w0c, k + 1)
                copy(W0[:, 2 * k:2 * k + 2, :], ps[:, k, :]).then_inc(s_w0c_out, 1)

            def xt_out(pieces):
                for n in pieces:
                    f, c = n // C, n % C
                    act.wait_ge(s_xt, n + 1)
                    copy(xT[:, f, c * CH:(c + 1) * CH], ps[:, 4 + n % 2, :]).then_inc(s_xt_out, 1)

            def tadj_out(t):
                for h in range(2):
                    act.wait_ge(s_tadj, 2 * t + h + 1)
                    copy(At8[:, 8 * h:8 * h + 8, t * P:(t + 1) * P],
                         ps[:, 6 + h, :].bitcast(F16).rearrange("p (b n) -> p b n", n=P),
                         saturate=False).then_inc(s_tadj_out, 1)

            def cast8(t):
                act.wait_ge(s_cast, t + 1)
                copy(A8[:, t, :], a16[:, t % TC, :], saturate=False).then_inc(s_cast8, 1)

            def x1t_out(c):
                for f in range(FT):
                    act.wait_ge(s_x1t, FT * c + f + 1)
                    copy(xT[:, f, c * CH:(c + 1) * CH], ps[:, 4 + f, :]).then_inc(s_x1t_out, 1)

            tadj_out(0)
            act.wait_ge(s_w0c, 3)
            copy(bias0[:, :], ps[:, 2, 0:D]).then_inc(s_w0c_out, 1)
            tadj_out(1)
            xt_out(range(C))
            tadj_out(2)
            xt_out(range(C, 2 * C))
            tadj_out(3)
            for t in range(TC):
                cast8(t)
            for c in range(C):
                if c + 1 < C:
                    for t in range(TC * (c + 1), TC * (c + 2)):
                        tadj_out(t)
                        cast8(t)
                act.wait_ge(s_var0, c + 1)
                act.activation(rstd[:, c * TC:(c + 1) * TC], mv[:, c * TC:(c + 1) * TC, 1], ACT.Sqrt,
                               bias=eps_col[:, 0:1]).then_inc(s_std0, 1)
                x1t_out(c)

            act.wait_ge(s_deg, 1)
            for c in range(C):
                copy(dsum[:, c * CH:(c + 1) * CH], ps[32 * c:32 * c + 8, 7, :]).then_inc(s_deg_out, 1)
            for n in range(9):
                g, kk = n // 3, n % 3
                act.wait_ge(s_gt, n + 1)
                dst = (RT[:, 2 * kk:2 * kk + 2, g * D:(g + 1) * D] if kk < 2 else Wg[:, 0, 4:6, g * D:(g + 1) * D])
                copy(dst, ps[:, GATE_BANKS[n % 5], :].rearrange("p (k n) -> p k n", k=2)).then_inc(s_gt_out, 1)
            for n in range(4):
                act.wait_ge(s_wg, n + 1)
                copy(Wg[:, 0, n, :], ps[:, 2 * (n % 2):2 * (n % 2) + 2, :].rearrange("p a b -> p (a b)")[:, 0:gates])\
                    .then_inc(s_wg_out, 1)

            def hi(i, pairs):
                for p in pairs:
                    act.wait_ge(s_turn, 8 * i + p + 1)
                    act.activation(rows16[:, 2 * p:2 * p + 2, 0, :],
                                   ps[:, p % 4, :].rearrange("p (t n) -> p t n", t=2), ACT.Copy,
                                   scale=2048.0).then_inc(s_hi, 1)

            def step(i, last):
                hi(i, range(EARLY, T // 2))
                for c in range(C):
                    act.wait_ge(s_state, 4 * i + 4 + c)
                    copy(SX[:, 0, :, :], xT[:, :, c * CH:(c + 1) * CH]).then_inc(s_shi, 1)
                    for g in range(2 * FT):
                        act.wait_ge(s_prod, 16 * i + 4 * c + g + 1)
                        act.activation(U[:, 0, g, :], ps[:, g, :], ACT.Copy, scale=1.0 / 2048).then_inc(s_U, 1)
                    for j in range(2 * FT):
                        act.wait_ge(s_gate, 24 * i + 6 * c + j + 1)
                        act.activation(gz[:, j, :], ps[:, 4 + j, :], ACT.Sigmoid, bias=gb[:, j:j + 1])\
                            .then_inc(s_r if j < 2 else s_z, 1)
                        if j == 1:
                            act.wait_ge(s_rs, 8 * i + 2 * c + 1)
                            copy(RX[:, 0, :, :], gz[:, 0:2, :]).then_inc(s_rhi, 1)
                    if c == C - 1 and not last:
                        hi(i + 1, range(EARLY))
                    act.wait_ge(s_gate, 24 * i + 6 * c + 6)
                    for f in range(FT):
                        act.activation(gz[:, f, :], ps[:, 4 + f, :], ACT.Tanh, bias=gb[:, 4 + f:5 + f]).then_inc(s_h, 1)

            hi(0, range(EARLY))
            with act.Fori(0, STEPS - 1) as i:
                step(i, False)
            step(STEPS - 1, True)

            for k in range(2):
                act.wait_ge(s_ot, k + 1)
                copy(oT[:, 2 * k:2 * k + 2, :], ps[:, k, :].rearrange("p (k n) -> p k n", k=2)).then_inc(s_ot_out, 1)
            act.wait_ge(s_ot, 3)
            copy(bias1[:, :], ps[:, 2, 0:D]).then_inc(s_ot_out, 1)

            def k_hi(t):
                c = t // TC
                act.wait_ge(s_kin[c % 2], 16 * (c // 2 + 1))
                if t >= 2:
                    act.wait_ge(s_kt, 2 * (t - 1))
                copy(kstk[:, t % 2, :, 0:4:2, :], k_twice(t)).then_inc(s_khi, 1)

            def x2_norm(tiles):
                act.wait_ge(s_var1, tiles.stop)
                act.activation(rstd[:, tiles], mv[:, tiles, 1], ACT.Sqrt, bias=eps_col[:, 0:1]).then_inc(s_std1, 1)

            k_hi(0)
            for t in range(T):
                c = t // TC
                if t + 1 < T:
                    k_hi(t + 1)
                if t % TC == 0:
                    if c >= 1:
                        act.wait_ge(s_o2, TC * c)
                    for g in range(FT):
                        act.wait_ge(s_o1, FT * c + g + 1)
                        act.activation(TT[:, g, :], ps[:, 4 + g, :], ACT.Tanh, bias=o1col[:, g:g + 1]).then_inc(s_o1_out, 1)
                if t == T - TC + 1:
                    x2_norm(slice(0, T - TC))
                act.wait_ge(s_kt, 2 * t + 2)
                copy(kst[:, :, t * P:(t + 1) * P],
                     ps[:, 2 * (t % 2):2 * (t % 2) + 2, :].rearrange("p a (h n) -> p (a h) n", n=P)).then_inc(s_kout, 1)

            SCALE = float(HD) ** -0.5

            def q_hi(t):
                for r in (0, 1):
                    act.activation(qstk[:, :, r, :], xr[:, t, :].rearrange("p (h d) -> p h d", h=HEADS), ACT.Copy,
                                   scale=SCALE).then_inc(s_qhi, 1)

            def q_out(t, b, bank):
                act.wait_ge(s_qT, 2 * t + 1)
                copy(qst[:, b, 0:4, :], ps[:, bank, :].rearrange("p (h n) -> p h n", h=4)).then_inc(s_qout[0], 1)

            act.wait_ge(s_x2, 1)
            q_hi(0)
            q_out(0, 0, 4)
            x2_norm(slice(T - TC, T))
            act.wait_ge(s_x2, T)

            def slot(t, g, gamma, j, has1, has2, front, more):
                hh, n = gamma % 2, 4 * g + j
                ring = 4 * gamma + j
                if has2 and j == 1:
                    act.wait_ge(s_pv, 4 * g - 4)
                    copy(oT2[:, :], ps[:, 6, 0:P]).then_inc(s_o, 1)
                if more and hh == 1 and j == 0:
                    q_hi(t + 1)
                if more and hh == 1 and j == 3:
                    q_out(t + 1, (gamma // 2 + 1) % 2, bank_of("q", 1, 0))
                if has1:
                    for b in range(4 * j, 4 * j + 4):
                        if TAKER[b] == "act":
                            take_block(act, copy, hh, g - 1, b, has2)
                if front:
                    act.wait_ge(s_neg, n + 1)
                    act.activation(prob[:, 4 * hh + j, :], prob[:, 4 * hh + j, :], ACT.Exp, bias=neg2[:, ring:ring + 1],
                                   accum_out=rsum2[:, ring:ring + 1]).then_inc(s_exp, 1)

            def x3_norm(k, tiles):
                act.wait_ge(s_var2, k)
                act.activation(rstd[:, tiles], mv[:, tiles, 1], ACT.Sqrt, bias=eps_col[:, 0:1]).then_inc(s_std2, 1)

            def f2_out(c):
                act.wait_ge(s_f, c + 1)
                act.activation(f2[:, c * CH:(c + 1) * CH], ps[:, 2 + c % 2, :], ACT.Identity, bias=bc23[:, 1:2])\
                    .then_inc(s_f_out, 1)

            def between(k):
                if k == 0:
                    x3_norm(1, slice(0, T - 1))
                if k == 3:
                    act.wait_ge(s_u, 1)
                    copy(ub[:, :, :], ps[:, 0, :].rearrange("p (k d) -> p k d", k=2)).then_inc(s_u_out, 1)
                    copy(bc23[:, :], ps[:, 1, 0:2]).then_inc(s_u_out, 1)
                    act.wait_ge(s_u_out, 2)
                if k >= 5:
                    f2_out(k - 5)

            layer2(act, slot, between)
            f2_out(C - 2)
            x3_norm(2, slice(T - 1, T))
            f2_out(C - 1)

            def tile3(t, b):
                act.wait_ge(s_neg3, t + 1)
                act.activation(coef[:, b, :], coef[:, b, :], ACT.Exp, bias=neg3[:, b:b + 1],
                               accum_out=rsum3[:, b:b + 1]).then_inc(s_exp3, 1)
                if isinstance(t, int) and t == T - 1:
                    out3_norm(1, slice(0, T - 2))
                for c in range(C):
                    act.wait_ge(s_T3, C * t + c + 1)
                    copy(coefT[:, b, c * CH:(c + 1) * CH], ps[:, 2 + c, :]).then_inc(s_T3_out, 1)

            def out3_norm(k, tiles):
                act.wait_ge(s_var3, k)
                act.activation(rstd[:, tiles], mv[:, tiles, 1], ACT.Sqrt, bias=eps_col[:, 0:1]).then_inc(s_std3, 1)

            with act.Fori(0, T // 2 - 1) as i:
                for b in range(2):
                    tile3(2 * i + b, b)
            for b in range(2):
                tile3(T - 2 + b, b)
            out3_norm(2, slice(T - 2, T))

        @block.tensor
        def _(pe):
            pe.wait_ge(s_const, 7)
            pe.wait_ge(s_w0, 16 * 6)
            for k in range(2):
                for i in range(2):
                    for j in range(2):
                        mm = pe.transpose(ps[:, 4 + k, j * D + i * P:j * D + (i + 1) * P],
                                          w_raw[:, 2 * k + i, j * P:(j + 1) * P], identf[:, :])
                mm.then_inc(s_w0t, 1)
            for k in range(2):
                pe.wait_ge(s_w0t_out, k + 1)
                for i in range(2):
                    for j in range(2):
                        mm = pe.matmul(ps[:, k, i * D:(i + 1) * D], w_tr[:, 2 * k + j, i * P:(i + 1) * P],
                                       w_raw[:, 4 + 2 * k + j, :], start=(j == 0), stop=(j == 1))
                mm.then_inc(s_w0c, 1)

            def bias_0():
                pe.wait_ge(s_bstat, 1)
                for j in range(4):
                    pe.matmul(ps[:, 2, 0:D], bstat[:, j, :], w_raw[:, 4 + j, :], start=(j == 0), stop=False)
                pe.matmul(ps[:, 2, 0:D], onesf[0:1, :], bcomb[:, :], start=False, stop=True).then_inc(s_w0c, 1)

            def transpose_x(pieces):
                pe.wait_ge(s_x, 16)
                for n in pieces:
                    f, c = n // C, n % C
                    if n < 2:
                        pe.wait_ge(s_w0t_out, n + 1)
                    else:
                        pe.wait_ge(s_xt_out, n - 1)
                    for q in range(TC):
                        mm = pe.transpose(ps[:, 4 + n % 2, q * P:(q + 1) * P],
                                          x32[:, c * TC + q, f * P:(f + 1) * P], identf[:, :])
                    mm.then_inc(s_xt, 1)

            def transpose_adj(t):
                pe.wait_ge(s_cast, t + 1)
                for h in range(2):
                    if t >= 1:
                        pe.wait_ge(s_tadj_out, 2 * t - 1 + h)
                    bank = ps[:, 6 + h, :].bitcast(F16)
                    for b in range(8):
                        m = 8 * h + b
                        mm = pe.transpose(bank[:, b * P:(b + 1) * P], a16[:, t % TC, m * P:(m + 1) * P], identh[:, :])
                    mm.then_inc(s_tadj, 1)

            def aggregate(c):
                if c == 0:
                    pe.wait_ge(s_w0c_out, 3)
                else:
                    pe.wait_ge(s_agg_out, c)
                for m in range(T):
                    pe.wait_ge(s_mask, c * T + m + 1)
                    mask = mk[:, m % RING, :]
                    if c == 0 and m % TC == 0:
                        pe.wait_ge(s_xb, m // TC + 1)
                    for f in range(FT):
                        for s in range(2):
                            mm = pe.matmul(ps[:, f, :], xb[:, m, s, f * P:(f + 1) * P], mask,
                                           start=(m == 0 and s == 0), stop=(m == T - 1 and s == 1))
                    mm.then_inc(s_agg_m, 1)
                    if m == T // 2:
                        pe.wait_ge(s_rdeg, c + 1)
                        if c >= 1:
                            pe.wait_ge(s_lin_out, TC * c - 1)
                        for q in range(TC):
                            n = c * TC + q
                            mm = pe.transpose(ps[:, 2, q * P:(q + 1) * P], rdeg[:, n:n + 1].broadcast_to([P, P]),
                                              identf[:, :])
                        mm.then_inc(s_rdegt, 1)
                    if m == 4 and c >= 1:
                        transpose_x1(c - 1)
                    if m in TURNS and c + 1 < C:
                        transpose_adj(TC * (c + 1) + TURNS.index(m))

            def linear(c):
                pe.wait_ge(s_agg_out, c + 1)
                if c == 0:
                    pe.wait_ge(s_xt_out, 2 * C)
                for q in range(TC):
                    n = c * TC + q
                    if n >= 2:
                        pe.wait_ge(s_lin_out, n - 1)
                    o = ps[:, 2 + q % 2, 0:D]
                    for f in range(FT):
                        pe.matmul(o, xT[:, f, n * P:(n + 1) * P], W0[:, f, :], start=(f == 0), stop=False)
                    for f in range(FT):
                        mm = pe.matmul(o, aggT[:, f, q * P:(q + 1) * P], W0[:, FT + f, :], start=False,
                                       stop=(f == FT - 1))
                    mm.then_inc(s_lin, 1)

            def transpose_x1(c):
                pe.wait_ge(s_x1, TC * (c + 1))
                for f in range(FT):
                    if c >= 1:
                        pe.wait_ge(s_x1t_out, FT * (c - 1) + f + 1)
                    for q in range(TC):
                        mm = pe.transpose(ps[:, 4 + f, q * P:(q + 1) * P], y0[:, q, f * P:(f + 1) * P], identf[:, :])
                    mm.then_inc(s_x1t, 1)

            transpose_adj(0)
            bias_0()
            transpose_adj(1)
            transpose_x(range(C))
            transpose_adj(2)
            transpose_x(range(C, 2 * C))
            transpose_adj(3)
            for c in range(C):
                aggregate(c)
                linear(c)

            pe.wait_ge(s_const, 9)
            pe.wait_ge(s_tadj_out, 2 * T)
            pe.wait_ge(s_cast8, T)
            for k, adj8 in enumerate((At8, A8)):
                for m in range(T):
                    for c in range(C):
                        mm = pe.matmul(ps[32 * c:32 * c + 8, 7, :], sel[:, k, :], adj8[:, m, c * CH:(c + 1) * CH],
                                       start=(k == 0 and m == 0), stop=(k == 1 and m == T - 1), tile_position=(0, 32 * c))
            mm.then_inc(s_deg, 1)
            transpose_x1(C - 1)
            for n in range(9):
                g, kk, before = n // 3, n % 3, n - len(GATE_BANKS)
                if n == 0:
                    pe.wait_ge(s_w1, 16 * 5)
                if GATE_BANKS[n % 5] == 4:
                    pe.wait_ge(s_x1t_out, FT * C)
                if before >= 0:
                    pe.wait_ge(s_gt_out, before + 1)
                    if before % 3 == 2:
                        pe.wait_ge(s_gt_lo, before // 3 + 1)
                for k in range(2):
                    for j in range(2):
                        mm = pe.transpose(ps[:, GATE_BANKS[n % 5], k * D + j * P:k * D + (j + 1) * P],
                                          graw[:, g, j, (2 * kk + k) * P:(2 * kk + k + 1) * P], identf[:, :])
                mm.then_inc(s_gt, 1)
            pe.wait_ge(s_gt_out, 9)
            pe.wait_ge(s_gt_lo, 3)
            pe.wait_ge(s_deg_out, C)
            for n in range(4):
                io, i = n // 2, n % 2
                if n >= 2:
                    pe.wait_ge(s_wlo, n - 1)
                for lo, hi, bank in ((0, 512, 0), (512, gates, 1)):
                    for j in range(2):
                        mm = pe.matmul(ps[:, 2 * (n % 2) + bank, 0:hi - lo], ioW[:, 2 * io + j, i * P:(i + 1) * P],
                                       RT[:, 2 * io + j, lo:hi], start=(j == 0), stop=(j == 1))
                mm.then_inc(s_wg, 1)
            pe.wait_ge(s_sel, 1)
            for lo, hi, bank in ((0, 512, 6), (512, gates, 7)):
                for j in range(4):
                    mm = pe.matmul(ps[0:8, bank, 0:hi - lo], bst1[:, j, :], RT[:, j, lo:hi], start=(j == 0), stop=(j == 3))
            mm.then_inc(s_dwp, 1)
            pe.wait_ge(s_wlo, 4)

            def turn(i, p):
                pe.wait_ge(s_state, 4 * i + p // 2 + 1)
                if p in (4, 5):
                    pe.wait_ge(s_rows, 8 * i + p - 3)
                for t in range(2):
                    for f in range(FT):
                        n = 2 * p + t
                        mm = pe.transpose(ps[:, p % 4, t * D + f * P:t * D + (f + 1) * P],
                                          xT[:, f, n * P:(n + 1) * P], identf[:, :])
                mm.then_inc(s_turn, 1)

            def aggregate1(c, g, tiles):
                f, moving = g % 2, (At8 if g < 2 else A8)
                for m in tiles:
                    for s in range(2):
                        mm = pe.matmul(ps[:, g, :], rows16[:, m, s, f * P:(f + 1) * P],
                                       moving[:, m, c * CH:(c + 1) * CH], start=(m == 0 and s == 0),
                                       stop=(m == T - 1 and s == 1))
                if m == T - 1:
                    mm.then_inc(s_prod, 1)

            def step(i, last):
                for c in range(C):
                    if c == 0:
                        early, late = 2 * EARLY, range(2 * EARLY, T)
                        pe.wait_ge(s_rows, 8 * i + EARLY)
                        pe.sem_inc(s_passed["pe"], 1)
                        aggregate1(0, 0, range(early))
                        aggregate1(0, 1, range(early - TC))
                        for p in range(EARLY, T // 2):
                            turn(i, p)
                        aggregate1(0, 1, range(early - TC, early))
                        pe.wait_ge(s_rows, 8 * i + 8)
                        pe.sem_inc(s_passed["pe"], 1)
                        for g in range(2):
                            aggregate1(0, g, late)
                        for g in (2, 3):
                            aggregate1(0, g, range(T))
                    else:
                        for g in range(2 * FT):
                            pe.wait_ge(s_Ulo, 16 * i + 4 * (c - 1) + g + 1)
                            pe.sem_inc(s_passed["pe"], 1)
                            aggregate1(c, g, range(T))
                    cols = slice(c * CH, (c + 1) * CH)

                    def gate(j):
                        o, w = ps[:, 4 + j % 4, :], slice(j * P, (j + 1) * P)
                        pe.matmul(o, dw[:, w], drows[:, cols], start=True, stop=False)

                        def three(k, src, f, last=False):
                            for wp, xp in ((0, 0), (0, 1), (1, 0)):
                                mm = pe.matmul(o, Wg[:, wp, k, w], src[:, xp, f, :], start=False,
                                               stop=(last and wp == 1))
                            return mm

                        if j == 0:
                            pe.wait_ge(s_slo, 4 * i + c + 1)
                        if j < 4:
                            for f in range(FT):
                                three(4 + f, SX, f)
                        for g in range(2 * FT):
                            if j == 0:
                                pe.wait_ge(s_Ulo, 16 * i + 4 * c + g + 1)
                            mm = three(g, U, g, j < 4 and g == 3)
                        if j >= 4:
                            pe.wait_ge(s_rs, 8 * i + 2 * c + 2)
                            for f in range(FT):
                                mm = three(4 + f, RX, f, f == 1)
                        mm.then_inc(s_gate, 1)

                    if c >= 1:
                        pe.wait_ge(s_h, 8 * i + 2 * c)
                        pe.wait_ge(s_z, 8 * i + 8 + 2 * c)
                    if c == 0:
                        pe.wait_ge(s_dwp_out, 1)
                    for j in range(4):
                        gate(j)
                        if c == C - 1 and not last and j in (1, 2):
                            if j == 1:
                                pe.wait_ge(s_Ulo, 16 * i + 16)
                            for p in (2 * j - 2, 2 * j - 1):
                                turn(i + 1, p)
                    pe.wait_ge(s_r, 8 * i + 2 * c + 2)
                    for j in range(4, 6):
                        gate(j)
                        if c == C - 1 and not last and j == 4:
                            for p in range(4, EARLY):
                                turn(i + 1, p)

            for p in range(EARLY):
                turn(0, p)
            with pe.Fori(0, STEPS - 1) as i:
                step(i, False)
            step(STEPS - 1, True)

            pe.wait_ge(s_ow, 16 * 4)
            pe.wait_ge(s_Ulo, 16 * STEPS)
            for k in range(2):
                for j in range(2):
                    for i in range(2):
                        mm = pe.transpose(ps[:, k, j * D + i * P:j * D + (i + 1) * P],
                                          oraw[:, 2 * k + i, j * P:(j + 1) * P], identf[:, :])
                mm.then_inc(s_ot, 1)
            pe.matmul(ps[:, 2, 0:D], onesf[0:1, :], o2b[:, :], start=True, stop=True).then_inc(s_ot, 1)
            pe.wait_ge(s_ot_out, 3)
            pe.wait_ge(s_h, 8 * STEPS)
            pe.wait_ge(s_z, 8 + 8 * STEPS)

            def turn_k(t):
                pe.wait_ge(s_klo, t + 1)
                if t >= 2:
                    pe.wait_ge(s_kout, t - 1)
                for hh in range(2):
                    for h in range(4):
                        mm = pe.transpose(ps[:, 2 * (t % 2) + hh, h * P:(h + 1) * P],
                                          kstk[:, t % 2, 4 * hh + h, :, :].bitcast(F32).rearrange("p a b -> p (a b)"),
                                          identf[:, :])
                    mm.then_inc(s_kt, 1)

            for c in range(C):
                pe.wait_ge(s_state, 4 + C * (STEPS - 1) + c + 1)
                for g in range(FT):
                    if c >= 1:
                        pe.wait_ge(s_o1_out, FT * (c - 1) + g + 1)
                    for k in range(FT):
                        mm = pe.matmul(ps[:, 4 + g, :], oT[:, k, g * P:(g + 1) * P], xT[:, k, c * CH:(c + 1) * CH],
                                       start=(k == 0), stop=(k == 1))
                    mm.then_inc(s_o1, 1)
                for q in range(TC):
                    n = c * TC + q
                    turn_k(n)
                    if q == 0:
                        pe.wait_ge(s_o1_out, FT * (c + 1))
                    if n >= 2:
                        pe.wait_ge(s_y1, n - 1)
                    for k in range(FT):
                        mm = pe.matmul(ps[:, 6 + q % 2, 0:D], TT[:, k, q * P:(q + 1) * P], oT[:, 2 + k, :],
                                       start=(k == 0), stop=(k == 1))
                    mm.then_inc(s_o2, 1)

            def turn_q(t, hh, bank):
                pe.wait_ge(s_qlo, 2 * t + 2)
                for h in range(4):
                    mm = pe.transpose(ps[:, bank, h * P:(h + 1) * P],
                                      qstk[:, 4 * hh + h, :, :].bitcast(F32).rearrange("p a b -> p (a b)"),
                                      identf[:, :])
                mm.then_inc(s_qT, 1)

            turn_q(0, 0, 4)
            turn_q(0, 1, 5)
            pe.wait_ge(s_kout, T)
            pe.wait_ge(s_v, 16)

            def products(g, q):
                hh = q[1]
                for who in ("act", "dve"):
                    wait_block_taken(pe, g, max(b for b in range(4 * q[0] + 4) if TAKER[b] == who))
                for b in range(4 * q[0], 4 * q[0] + 4):
                    for h in range(4):
                        col = (4 * hh + h) * HD
                        mm = pe.matmul(ps[h * HD:(h + 1) * HD, 6, 0:P], v_sb[:, b, col:col + HD],
                                       PT[:, q[0] % 2, b % 4, h * P:(h + 1) * P], start=(b == 0), stop=(b == T - 1),
                                       tile_position=(0, h * HD))
                mm.then_inc(s_pv, 1)

            def scores(t, g, gamma, j, u, first):
                h = 4 * (gamma % 2) + j
                if j == 0 and u == 0:
                    pe.wait_ge(s_qout[gamma % 2], t + 1)
                if not first:
                    pe.wait_ge(s_masked, 2 * (4 * g + j) + u - 1)
                for w in range(2):
                    mm = pe.matmul(ps[:, 2 * u + w, :], qst[:, gamma // 2, h, :],
                                   kst[:, h, (2 * u + w) * CH:(2 * u + w + 1) * CH], start=True, stop=True)
                mm.then_inc(s_score, 1)

            def slot(t, g, gamma, j, has1, has2, front, more):
                hh = gamma % 2
                if j < 3:
                    ahead = (t, g, gamma, j + 1)
                else:
                    ahead = (t + hh, g + 1, (gamma + 1) % 4, 0)
                is_ahead = front and (more or gamma < 3 or j < 3)
                if has1 and j == 0:
                    pe.wait_ge(s_exp, 4 * g)
                for b in range(4 * j, 4 * j + 4):
                    if b % 4 == 2 and is_ahead:
                        scores(*ahead, 0, False)
                    if has1:
                        wait_bank_free(pe, t, "p", hh, b)
                        for h in range(4):
                            mm = pe.transpose(ps[:, bank_of("p", hh, b), h * P:(h + 1) * P],
                                              prob[:, 4 * (1 - hh) + h, b * P:(b + 1) * P], identf[:, :])
                        mm.then_inc(s_T, 1)
                if has2 and j == 1:
                    pe.wait_ge(s_o, g - 1)
                    wait_bank_free(pe, t, "o", hh, 0)
                    pe.transpose(ps[:, bank_of("o", hh, 0), 0:P], oT2[:, :], identf[:, :]).then_inc(s_oT, 1)
                if is_ahead:
                    scores(*ahead, 1, False)
                if j == 0:
                    if has2:
                        products(g - 2, (3, hh))
                elif has1:
                    products(g - 1, (j - 1, 1 - hh))
                if more and hh == 1 and j >= 2:
                    wait_bank_free(pe, t, "q", 1, j - 2)
                    turn_q(t + 1, j - 2, bank_of("q", 1, j - 2))

            for u in range(2):
                scores(0, 0, 0, 0, u, True)
            def f2_turn(c):
                pe.wait_ge(s_dot, 2 * min(TC * (c + 1), T))
                if c >= 2:
                    pe.wait_ge(s_f_out, c - 1)
                for q in range(TC):
                    n = c * TC + q
                    mm = pe.transpose(ps[:, 2 + c % 2, q * P:(q + 1) * P], f2c[:, n:n + 1].broadcast_to([P, P]),
                                      identf[:, :])
                mm.then_inc(s_f, 1)

            def between(k):
                if k == 3:
                    pe.wait_ge(s_wb, 1)
                    pe.wait_ge(s_masked, 2 * HEADS * T)
                    for w in range(2):
                        pe.matmul(ps[:, 0, w * D:(w + 1) * D], wb[:, w, :], W1[:, :], start=True, stop=True)
                    pe.matmul(ps[:, 1, 0:2], onesf[0:1, :], b23[:, :], start=True, stop=True).then_inc(s_u, 1)
                if k >= 5:
                    f2_turn(k - 5)

            layer2(pe, slot, between)
            f2_turn(C - 2)
            f2_turn(C - 1)
            pe.wait_ge(s_f_out, C)

            def tile3(t, b, first, used):
                pe.wait_ge(s_exp3, t + 1)
                for c in range(C + 1):
                    if c < C:
                        if not first:
                            pe.wait_ge(s_T3_out, C * t + c - 3)
                        for q in range(TC):
                            m = c * TC + q
                            mm = pe.transpose(ps[:, 2 + c, q * P:(q + 1) * P], coef[:, b, m * P:(m + 1) * P],
                                              identf[:, :])
                        mm.then_inc(s_T3, 1)
                    if used and c == 1:
                        pe.wait_ge(s_val_out, t - 1)
                    if c >= 1:
                        pe.wait_ge(s_T3_out, C * t + c)
                        for m in range((c - 1) * TC, c * TC):
                            mm = pe.matmul(ps[:, 6 + b, 0:D], coefT[:, b, m * P:(m + 1) * P], xr[:, m, :],
                                           start=(m == 0), stop=(m == T - 1))
                mm.then_inc(s_val, 1)

            tile3(0, 0, True, False)
            tile3(1, 1, False, False)
            with pe.Fori(1, T // 2) as i:
                for b in range(2):
                    tile3(2 * i + b, b, False, True)

        @block.vector
        def _(dve):
            steps = [0]

            def link(ins):
                steps[0] += 1
                ins.then_inc(s_dve, 1)
                dve.wait_ge(s_dve, steps[0])

            def x_lo(c):
                part = slice(c * TC, (c + 1) * TC)
                dve.wait_ge(s_xhi, c + 1)
                dve.tensor_tensor(xb[:, part, 1, :], x32[:, part, :], xb[:, part, 0, :].bitcast(F32),
                                  ALU.subtract).then_inc(s_xb, 1)

            def bias_columns():
                dve.wait_ge(s_w0, 16 * 6)
                for j in range(4):
                    last = dve.tensor_scalar(bstat[:, j, :], onesf[:, :], bcol0[:, j:j + 1], None, ALU.mult)
                last.then_inc(s_bstat, 1)

            dve.wait_ge(s_const, 7)

            def cast(t):
                dve.wait_ge(s_adj[t % 2], 16 * (t // 2 + 1))
                if t >= TC:
                    dve.wait_ge(s_tadj, 2 * (t - TC + 1))
                    dve.wait_ge(s_cast8, t - TC + 1)
                dve.tensor_copy(a16[:, t % TC, :], stage[:, t % 2, :]).then_inc(s_cast, 1)

            def count(t):
                dve.wait_ge(s_cast, t + 1)
                if t >= 1:
                    dve.wait_ge(s_count, t)
                dve.tensor_scalar(hits[:, :], a16[:, t % TC, :], 0.0, None, ALU.is_gt, ALU.add,
                                  accum_out=rdeg[:, t:t + 1], saturate=False).then_inc(s_count, 1)
                if t % TC == TC - 1:
                    d = rdeg[:, t - TC + 1:t + 1]
                    dve.wait_ge(s_count, t + 1)
                    link(dve.tensor_scalar(d, d, 1.0, None, ALU.max))
                    dve.reciprocal(d, d).then_inc(s_rdeg, 1)

            def mask(c, m):
                n = c * T + m
                if m == 0:
                    dve.wait_ge(s_tadj_out, 2 * TC * (c + 1))
                if n >= RING:
                    dve.wait_ge(s_agg_m, n - RING + 1)
                dve.tensor_scalar(mk[:, m % RING, :], At8[:, m, c * CH:(c + 1) * CH], 0.0, None, ALU.is_gt).then_inc(s_mask, 1)

            def over_out(c):
                dve.wait_ge(s_rdegt, c + 1)
                dve.tensor_copy(over[:, :], ps[:, 2, :]).then_inc(s_over, 1)

            def mean_of_neighbours(c):
                dve.wait_ge(s_over, c + 1)
                dve.wait_ge(s_agg_m, T * (c + 1))
                if c >= 1:
                    dve.wait_ge(s_lin, TC * c)
                for f in range(FT):
                    last = dve.tensor_tensor(aggT[:, f, :], ps[:, f, :], over[:, :], ALU.mult)
                last.then_inc(s_agg_out, 1)

            def residual(c):
                dve.wait_ge(s_xres, 16 * (c + 1))
                if c == 0:
                    dve.wait_ge(s_w0c_out, 3)
                else:
                    dve.wait_ge(s_x1_saved, 16 * c)
                    dve.wait_ge(s_x1t, FT * c)
                for q in range(TC):
                    n = c * TC + q
                    dve.wait_ge(s_lin, n + 1)
                    link(dve.tensor_tensor(y0[:, q, :], ps[:, 2 + q % 2, 0:D], bias0[:, :], ALU.add))
                    steps[0] += 1
                    dve.scalar_tensor_tensor(y0[:, q, :], y0[:, q, :], 0.0, xres[:, q, :], ALU.max,
                                             ALU.add).then_inc(s_lin_out, 1)
                    steps[0] -= 1
                    dve.wait_ge(s_lin_out, n + 1)
                    link(dve.bn_stats(stats[:, q, :], y0[:, q, :]))
                    ins = dve.bn_aggr(mv[:, n, :], stats[:, q, :])
                    if q == TC - 1:
                        ins.then_inc(s_var0, 1)
                    else:
                        link(ins)

            def normalise(c):
                dve.wait_ge(s_std0, c + 1)
                r = rstd[:, c * TC:(c + 1) * TC]
                link(dve.reciprocal(r, r))
                for q in range(TC):
                    n = c * TC + q
                    dve.tensor_scalar(y0[:, q, :], y0[:, q, :], mv[:, n, 0:1], rstd[:, n:n + 1], ALU.subtract,
                                      ALU.mult).then_inc(s_x1, 1)

            x_lo(0)
            x_lo(1)
            cast(0)
            bias_columns()
            cast(1)
            x_lo(2)
            cast(2)
            x_lo(3)
            count(0)
            cast(3)
            count(1)
            count(2)
            for m in range(RING):
                mask(0, m)
            for c in range(C):
                for m in range(RING, T):
                    mask(c, m)
                    if m in CASTS and c + 1 < C:
                        cast(TC * (c + 1) + CASTS.index(m))
                    if m == RING and c == 0:
                        count(3)
                    if m in COUNTS and c + 1 < C:
                        count(TC * (c + 1) + COUNTS.index(m))
                    if m == OVER:
                        over_out(c)
                mean_of_neighbours(c)
                if c + 1 < C:
                    for m in range(RING):
                        mask(c + 1, m)
                residual(c)
                normalise(c)

            dve.wait_ge(s_x1t_out, FT * C)
            dve.wait_ge(s_x1_saved, 16 * C)
            eye = identf[0:8, 0:8]
            halves = eye.rearrange("p (a b) -> p a b", b=4)
            evens = eye.rearrange("p (a b) -> p b a", b=2)
            dve.tensor_reduce(dmask[:, 0:1], halves[:, :, 0:2], AX.XY, ALU.add)
            dve.tensor_reduce(dmask[:, 1:2], halves[:, :, 2:4], AX.XY, ALU.add)
            dve.tensor_reduce(dmask[:, 2:3], evens[:, 0, :], AX.X, ALU.add)
            link(dve.tensor_reduce(dmask[:, 3:4], evens[:, 1, :], AX.X, ALU.add))

            def split_rows(dst, src, masks):
                link(dve.tensor_copy(dst, src))
                link(dve.tensor_tensor(src, src, dst.bitcast(F32), ALU.subtract))
                link(dve.tensor_scalar(src, src, dmask[:, masks + 1:masks + 2], None, ALU.mult))
                return dve.scalar_tensor_tensor(dst, dst.bitcast(F32), dmask[:, masks:masks + 1], src, ALU.mult, ALU.add)

            for n in range(9):
                g, kk = n // 3, n % 3
                if kk == 2:
                    dve.wait_ge(s_gt_out, n + 1)
                    w = slice(g * D, (g + 1) * D)
                    link(dve.tensor_tensor(Wg[:, 1, 4:6, w], ps[:, GATE_BANKS[n % 5], :].rearrange("p (k n) -> p k n", k=2),
                                           Wg[:, 0, 4:6, w].bitcast(F32), ALU.subtract))
                    dve.sem_inc(s_gt_lo, 1)
            link(dve.memset(bst1[:, :, :], 0.0))
            dve.wait_ge(s_b1, 16 * 5)
            for j in range(4):
                k = j // 2
                last = dve.tensor_scalar(bst1[:, j, 4 * k:4 * k + 4], onesf[:, 0:4], bcol1[:, j:j + 1], None, ALU.mult)
            last.then_inc(s_sel, 1)
            for n in range(4):
                dve.wait_ge(s_wg_out, n + 1)
                dve.tensor_tensor(Wg[:, 1, n, :],
                                  ps[:, 2 * (n % 2):2 * (n % 2) + 2, :].rearrange("p a b -> p (a b)")[:, 0:gates],
                                  Wg[:, 0, n, :].bitcast(F32), ALU.subtract).then_inc(s_wlo, 1)
            dve.sem_inc(s_z, 8)
            dve.sem_inc(s_state, 4)

            def lo(i, pairs):
                for p in pairs:
                    dve.wait_ge(s_hi, 8 * i + p + 1)
                    dve.scalar_tensor_tensor(rows16[:, 2 * p:2 * p + 2, 1, :],
                                             ps[:, p % 4, :].rearrange("p (t n) -> p t n", t=2), 2048.0,
                                             rows16[:, 2 * p:2 * p + 2, 0, :], ALU.mult, ALU.subtract).then_inc(s_rows, 1)

            def step(i, last):
                lo(i, range(EARLY, T // 2))
                for c in range(C):
                    state = xT[:, :, c * CH:(c + 1) * CH]
                    r, z = gz[:, 0:2, :], gz[:, 2:4, :]
                    dve.wait_ge(s_shi, 4 * i + c + 1)
                    dve.tensor_tensor(SX[:, 1, :, :], state, SX[:, 0, :, :].bitcast(F32), ALU.subtract).then_inc(s_slo, 1)
                    for g in range(2 * FT):
                        dve.wait_ge(s_U, 16 * i + 4 * c + g + 1)
                        dve.scalar_tensor_tensor(U[:, 1, g, :], ps[:, g, :], 1.0 / 2048, U[:, 0, g, :].bitcast(F32),
                                                 ALU.mult, ALU.subtract).then_inc(s_Ulo, 1)
                    dve.wait_ge(s_r, 8 * i + 2 * c + 2)
                    dve.tensor_tensor(r, r, state, ALU.mult).then_inc(s_rs, 1)
                    dve.wait_ge(s_rhi, 4 * i + c + 1)
                    dve.tensor_tensor(RX[:, 1, :, :], r, RX[:, 0, :, :].bitcast(F32), ALU.subtract).then_inc(s_rs, 1)
                    if c == C - 1 and not last:
                        lo(i + 1, range(EARLY))
                    dve.wait_ge(s_h, 8 * i + 2 * c + 2)
                    dve.tensor_tensor(r, r, state, ALU.subtract).then_inc(s_upd, 1)
                    dve.wait_ge(s_upd, 8 * i + 2 * c + 1)
                    dve.wait_ge(s_z, 8 * i + 8 + 2 * c + 2)
                    dve.tensor_tensor(r, r, z, ALU.mult).then_inc(s_upd, 1)
                    dve.wait_ge(s_upd, 8 * i + 2 * c + 2)
                    dve.tensor_tensor(state, state, r, ALU.add).then_inc(s_state, 1)

            lo(0, range(EARLY))
            dve.wait_ge(s_deg_out, C)
            link(split_rows(drows[:, :], dsum, 0))
            dve.wait_ge(s_dwp, 1)
            link(dve.tensor_copy(dsum[:, 0:gates], ps[0:8, 6:8, :].rearrange("p a b -> p (a b)")[:, 0:gates]))
            split_rows(dw[:, :], dsum[:, 0:gates], 2).then_inc(s_dwp_out, 1)
            with dve.Fori(0, STEPS - 1) as i:
                step(i, False)
            step(STEPS - 1, True)

            def k_lo(t):
                dve.wait_ge(s_khi, t + 1)
                dve.tensor_tensor(kstk[:, t % 2, :, 1:4:2, :], k_twice(t), kstk[:, t % 2, :, 0:4:2, :].bitcast(F32),
                                  ALU.subtract).then_inc(s_klo, 1)

            def x2_out(tiles):
                for n in tiles:
                    dve.tensor_scalar(xr[:, n, :], xr[:, n, :], mv[:, n, 0:1], rstd[:, n:n + 1], ALU.subtract,
                                      ALU.mult).then_inc(s_x2, 1)

            def x2_rstd(k, tiles):
                dve.wait_ge(s_std1, k)
                link(dve.reciprocal(rstd[:, tiles], rstd[:, tiles]))

            def x2_mean(n):
                dve.wait_ge(s_stat1, n + 1)
                dve.bn_aggr(mv[:, n, :], stats[:, n % TC, :]).then_inc(s_var1, 1)

            k_lo(0)
            for n in range(T):
                c, q = n // TC, n % TC
                if n + 1 < T:
                    k_lo(n + 1)
                if q == 0:
                    dve.wait_ge(s_x1b, c + 1)
                dve.wait_ge(s_o2, n + 1)
                dve.tensor_tensor(xr[:, n, :], ps[:, 6 + q % 2, 0:D], x1r[:, c % 2, q, :], ALU.add).then_inc(s_y1, 1)
                dve.wait_ge(s_y1, n + 1)
                dve.bn_stats(stats[:, q, :], xr[:, n, :]).then_inc(s_stat1, 1)
                if n >= 1:
                    x2_mean(n - 1)
                if n == T - TC + 1:
                    x2_rstd(1, slice(0, T - TC))
                if n > T - TC:
                    x2_out(range(TC * (n - T + TC - 1), TC * (n - T + TC)))
            x2_mean(T - 1)

            SCALE = float(HD) ** -0.5

            def q_lo(t):
                for r in (0, 1):
                    dve.wait_ge(s_qhi, 2 * t + r + 1)
                    dve.scalar_tensor_tensor(qstk[:, :, 2 + r, :], xr[:, t, :].rearrange("p (h d) -> p h d", h=HEADS),
                                             SCALE, qstk[:, :, r, :].bitcast(F32), ALU.mult, ALU.subtract)\
                        .then_inc(s_qlo, 1)

            def q_out(t, b, bank):
                dve.wait_ge(s_qT, 2 * t + 2)
                dve.tensor_copy(qst[:, b, 4:8, :], ps[:, bank, :].rearrange("p (h n) -> p h n", h=4)).then_inc(s_qout[1], 1)

            q_lo(0)
            q_out(0, 0, 5)
            x2_rstd(2, slice(T - TC, T))
            x2_out(range(T - TC, T))

            def slot(t, g, gamma, j, has1, has2, front, more):
                hh, n = gamma % 2, 4 * g + j
                ring = 4 * gamma + j
                if front:
                    if hh == 0 and j == 0:
                        dve.wait_ge(s_bias2, t + 1)
                    if has2:
                        dve.wait_ge(s_T, T * (g - 1))
                    for u in range(2):
                        half = slice(u * 1024, (u + 1) * 1024)
                        dve.wait_ge(s_score, 2 * n + u + 1)
                        dve.sem_inc(s_passed["dve"], 1)
                        dve.tensor_tensor_reduce(prob[:, 4 * hh + j, half],
                                                 ps[:, 2 * u:2 * u + 2, :].rearrange("p a b -> p (a b)"),
                                                 bias2[:, gamma // 2, half], 1.0, NEG_INIT, ALU.add, ALU.max,
                                                 mx2[:, ring, u:u + 1]).then_inc(s_masked, 1)
                    dve.wait_ge(s_masked, 2 * n + 2)
                    dve.tensor_scalar(neg2[:, ring:ring + 1], mx2[:, ring, 0:1], mx2[:, ring, 1:2], -1.0, ALU.max,
                                      ALU.mult).then_inc(s_neg, 1)
                if has2 and front and hh == 0 and j == 0:
                    q_out(t, gamma // 2, bank_of("q", 1, 1))
                if has2 and j == 2:
                    old = (gamma + 2) % 4
                    rows = xr[:, t - 1, hh * P:(hh + 1) * P]
                    base = 2 * (g - 2)
                    dve.wait_ge(s_exp, 4 * g - 4)
                    dve.reciprocal(rinv2[:, :], rsum2[:, 4 * old:4 * old + 4]).then_inc(s_fin2, 1)
                    dve.wait_ge(s_oT, g - 1)
                    dve.wait_ge(s_fin2, base + 1)
                    dve.tensor_tensor(row2[:, hh * P:(hh + 1) * P].rearrange("p (h d) -> p h d", h=4),
                                      ps[:, bank_of("o", hh, 0), 0:P].rearrange("p (h d) -> p h d", h=4),
                                      rinv2[:, :].unsqueeze(2).broadcast_to([P, 4, HD]), ALU.mult).then_inc(s_att, 1)
                    dve.wait_ge(s_att, g - 1)
                    dve.tensor_tensor(row2[:, hh * P:(hh + 1) * P], rows, row2[:, hh * P:(hh + 1) * P], ALU.add).then_inc(s_fin2, 1)
                    if hh == 1:
                        dve.wait_ge(s_fin2, base + 2)
                        dve.sem_inc(s_passed["dve"], 1)
                        dve.bn_stats(stats[:, 0, :], row2[:, :]).then_inc(s_stat2, 1)
                        dve.tensor_copy(xr[:, t - 1, :], row2[:, :]).then_inc(s_stat2, 1)
                        dve.wait_ge(s_stat2, 4 * t - 2)
                        dve.sem_inc(s_passed["dve"], 1)
                        dve.bn_aggr(mv1[:, :], stats[:, 0, :]).then_inc(s_stat2, 1)
                        dve.wait_ge(s_stat2, 4 * t - 1)
                        dve.tensor_copy(mv[:, t - 1, :], mv1[:, :]).then_inc(s_stat2, 1)
                if more and hh == 1 and j == 1:
                    q_lo(t + 1)
                if has1:
                    for b in range(4 * j, 4 * j + 4):
                        if TAKER[b] == "dve":
                            take_block(dve, dve.tensor_copy, hh, g - 1, b, has2)


            def x3_out(tiles):
                for n in tiles:
                    dve.tensor_scalar(xr[:, n, :], xr[:, n, :], mv[:, n, 0:1], rstd[:, n:n + 1], ALU.subtract,
                                      ALU.mult).then_inc(s_x3, 1)

            def between(k):
                if k == 0:
                    dve.wait_ge(s_stat2, 4 * (T - 1))
                    dve.sem_inc(s_var2, 1)
                if k == 1:
                    dve.wait_ge(s_std2, 1)
                    link(dve.reciprocal(rstd[:, 0:T - 1], rstd[:, 0:T - 1]))
                if 1 <= k <= C:
                    x3_out(range(TC * (k - 1), min(TC * k, T - 1)))
                if k == 2:
                    dve.wait_ge(s_w3, 16 * 5)
                    for w in range(2):
                        last = dve.tensor_scalar(wb[:, w, :], onesf[:, :], w23[:, w:w + 1], None, ALU.mult)
                    last.then_inc(s_wb, 1)
                if k >= 4:
                    if k == 4:
                        dve.wait_ge(s_u_out, 2)
                        dve.wait_ge(s_x3, T - 1)
                    dots(range(5 * (k - 4), 5 * (k - 3)))

            def dots(tiles):
                for n in tiles:
                    if n >= 2:
                        dve.wait_ge(s_dot, 2 * (n - 1))
                    for w, f in ((0, f1), (1, f2c)):
                        dve.tensor_tensor_reduce(dot[:, n % 2, w, :], xr[:, n, :], ub[:, w, :], 1.0, 0.0, ALU.mult, ALU.add,
                                                 f[:, n:n + 1]).then_inc(s_dot, 1)

            layer2(dve, slot, between)
            dve.wait_ge(s_stat2, 4 * T)
            dve.sem_inc(s_var2, 1)
            dve.wait_ge(s_std2, 2)
            link(dve.reciprocal(rstd[:, T - 1:T], rstd[:, T - 1:T]))
            x3_out([T - 1])
            dve.wait_ge(s_x3, T)
            dots([T - 1])
            dve.wait_ge(s_dot, 2 * T)
            link(dve.tensor_scalar(f1[:, :], f1[:, :], bc23[:, 0:1], None, ALU.add))
            dve.wait_ge(s_f_out, C)

            def inverse3(t, b):
                dve.wait_ge(s_exp3, t + 1)
                dve.reciprocal(rinv3[:, b:b + 1], rsum3[:, b:b + 1]).then_inc(s_inv3, 1)

            def logits3(t, b, k, used):
                w = coef[:, b, :]
                dve.wait_ge(s_adj3[b], 16 * k + 16)
                if used:
                    dve.wait_ge(s_T3, C * (t - 1))
                dve.scalar_tensor_tensor(w, f2[:, :], f1[:, t:t + 1] if isinstance(t, int) else f1[:, bass.ds(t, 1)],
                                         adj3[:, b, :], ALU.add, ALU.mult).then_inc(s_logit, 1)
                dve.wait_ge(s_logit, t + 1)
                dve.scalar_tensor_tensor(w, w, 0.01, w, ALU.mult, ALU.max).then_inc(s_l3, 1)
                if not isinstance(t, int) or t >= 1:
                    inverse3(t - 1, 1 - b)
                dve.wait_ge(s_l3, 2 * t + 1)
                dve.wait_ge(s_bias3, t + 1)
                dve.sem_inc(s_passed["dve"], 1)
                dve.tensor_tensor_reduce(w, w, bias3[:, b, :], 1.0, NEG_INIT, ALU.add, ALU.max, mx3[:, b:b + 1])\
                    .then_inc(s_l3, 1)
                dve.wait_ge(s_l3, 2 * t + 2)
                dve.tensor_scalar(neg3[:, b:b + 1], mx3[:, b:b + 1], -1.0, None, ALU.mult).then_inc(s_neg3, 1)

            def finish3(t, b):
                row = row3[:, b, :]
                base = 5 * t
                dve.wait_ge(s_val, t + 1)
                dve.wait_ge(s_inv3, t + 1)
                dve.tensor_scalar(row, ps[:, 6 + b, 0:D], rinv3[:, b:b + 1], 0.0, ALU.mult, ALU.max)\
                    .then_inc(s_val_out, 1)
                dve.wait_ge(s_val_out, t + 1)
                dve.tensor_tensor(row, row, xr[:, t, :], ALU.add).then_inc(s_f3, 1)
                dve.wait_ge(s_f3, base + 1)
                dve.sem_inc(s_passed["dve"], 1)
                dve.bn_stats(stats[:, 0, :], row).then_inc(s_f3, 1)
                dve.tensor_copy(y3[:, t, :], row).then_inc(s_f3, 1)
                dve.wait_ge(s_f3, base + 3)
                dve.sem_inc(s_passed["dve"], 1)
                dve.bn_aggr(mv3[:, :], stats[:, 0, :]).then_inc(s_f3, 1)
                dve.wait_ge(s_f3, base + 4)
                dve.tensor_copy(mv[:, t, :], mv3[:, :]).then_inc(s_f3, 1)

            logits3(0, 0, 0, False)
            logits3(1, 1, 0, False)
            with dve.Fori(1, T // 2) as i:
                for b in range(2):
                    logits3(2 * i + b, b, i, True)
                    finish3(2 * i + b - 2, b)
            inverse3(T - 1, 1)

            def out3(k, tiles):
                dve.wait_ge(s_std3, k)
                link(dve.reciprocal(rstd[:, tiles], rstd[:, tiles]))
                for n in range(tiles.start, tiles.stop):
                    dve.tensor_scalar(y3[:, n, :], y3[:, n, :], mv[:, n, 0:1], rstd[:, n:n + 1], ALU.subtract,
                                      ALU.mult).then_inc(s_y3, 1)

            dve.wait_ge(s_f3, 5 * (T - 2))
            dve.sem_inc(s_var3, 1)
            finish3(T - 2, 0)
            out3(1, slice(0, T - 2))
            finish3(T - 1, 1)
            dve.wait_ge(s_f3, 5 * T)
            dve.sem_inc(s_var3, 1)
            out3(2, slice(T - 2, T))


NAMES = ["x", "adj", "L0_gnn_W_self", "L0_gnn_b_self", "L0_gnn_W_nb", "L0_gnn_b_nb", "L0_gnn_W_comb", "L0_gnn_b_comb",
         "L1_gnn_in_W", "L1_gnn_in_b", "L1_gnn_out_W", "L1_gnn_out_b", "L1_gnn_r_W", "L1_gnn_r_b", "L1_gnn_z_W",
         "L1_gnn_z_b", "L1_gnn_h_W", "L1_gnn_h_b", "L1_gnn_o1_W", "L1_gnn_o1_b", "L1_gnn_o2_W", "L1_gnn_o2_b",
         "L2_gnn_x2", "L2_gnn_v", "L3_gnn_W1", "L3_gnn_w2", "L3_gnn_b2", "L3_gnn_w3", "L3_gnn_b3"]


def kernel(**inputs):
    import numpy as _np
    import concourse.bacc as _bacc
    from concourse import mybir as _mybir
    from concourse.bass_utils import run_bass_kernel_spmd as _run

    nc = _bacc.Bacc("TRN2", target_bir_lowering=False, num_devices=1)
    arrays, args = {}, {}
    for name in NAMES:
        v = _np.ascontiguousarray(inputs[name])
        arrays[f"in_{name}_dram"] = v
        args[name] = nc.dram_tensor(f"in_{name}_dram", v.shape, _mybir.dt.from_np(v.dtype), kind="ExternalInput").ap()
    out = nc.dram_tensor("out_0_dram", (N, D), F32, kind="ExternalOutput").ap()
    program(nc, args, out)
    r = _run(nc, [arrays], core_ids=[0])
    return r.results[0]["out_0_dram"]
```
